# Optimizing a Trainium2 kernel written in Bass

```python
import numpy as np
import jax
import jax.numpy as jnp

def _softmax(x, axis=-1):
    return jax.nn.softmax(x, axis=axis)

def _gelu(x):
    return jax.nn.gelu(x, approximate=True)

def _silu(x):
    return jax.nn.silu(x)

def _sigmoid(x):
    return jax.nn.sigmoid(x)

def _layernorm(x, axis=-1, eps=1e-05):
    m = jnp.mean(x, axis=axis, keepdims=True)
    v = jnp.var(x, axis=axis, keepdims=True)
    return (x - m) / jnp.sqrt(v + eps)

def _scatter_add(tgt, idx, src, axis=0):
    return tgt.at[idx].add(src)

def _segment_sum(src, seg, n):
    return jax.ops.segment_sum(src, seg, n)
kernel_name = 'mk_seq_preln_d2_jaxref_r8_59c7b7'

def setup_inputs(seed: int=0):
    np.random.seed(seed)
    _w = jnp.asarray

    def _L0_attn_setup():
        import jax, jax.numpy as jnp
        import numpy as np
        CHUNK = 64
        NORM_EPS = 1e-05
        DENOM_EPS = 1.0
        B, S, HID, H = (4, 512, 128, 8)
        D = HID // H

        def rmsnorm(x, w, eps=NORM_EPS):
            var = jnp.mean(x * x, axis=-1, keepdims=True)
            return x * jax.lax.rsqrt(var + eps) * w

        def chunked_linear_attn(q, k, v):
            b, s, h, d = q.shape
            n = s // CHUNK

            def to_chunks(x):
                return x.reshape(b, n, CHUNK, h, d).transpose(1, 0, 3, 2, 4)
            qc, kc, vc = (to_chunks(q), to_chunks(k), to_chunks(v))
            mask = jnp.tril(jnp.ones((CHUNK, CHUNK), dtype=q.dtype))

            def step(state, inp):
                qq, kk, vv = inp
                inter = jnp.einsum('bhcd,bhde->bhce', qq, state)
                scores = jnp.einsum('bhcd,bhed->bhce', qq, kk) * mask
                intra = jnp.einsum('bhce,bhed->bhcd', scores, vv)
                state = state + jnp.einsum('bhcd,bhce->bhde', kk, vv)
                return (state, inter + intra)
            init = jnp.zeros((b, h, d, d), dtype=q.dtype)
            _, o = jax.lax.scan(step, init, (qc, kc, vc))
            return o.transpose(1, 0, 3, 2, 4).reshape(b, s, h, d)
        key = jax.random.key(seed)
        k0, k1, k2, k3, k4 = jax.random.split(key, 5)
        hidden_states = jax.random.normal(k0, (B, S, HID), dtype=jnp.float32)
        Wq = jax.random.normal(k1, (HID, HID), dtype=jnp.float32) * 0.02
        Wk = jax.random.normal(k2, (HID, HID), dtype=jnp.float32) * 0.02
        Wv = jax.random.normal(k3, (HID, HID), dtype=jnp.float32) * 0.02
        Wo = jax.random.normal(k4, (HID, HID), dtype=jnp.float32) * 0.02
        norm_w = jnp.ones((D,), dtype=jnp.float32)
        return {'hidden_states': hidden_states, 'Wq': Wq, 'Wk': Wk, 'Wv': Wv, 'Wo': Wo, 'norm_w': norm_w}
    _L0_attn_in = _L0_attn_setup()

    def _L0_ffn_setup():
        import jax, jax.numpy as jnp
        import numpy as np
        E = 16
        K = 4
        NG = 4
        TG = 2
        SCALE = 2.5
        NORM_TOPK = True
        H = 128
        I = 64
        SH_I = I * 2
        B, S = (2, 256)
        key = jax.random.key(seed)
        ks = jax.random.split(key, 9)

        def w(k, shape, fan_in):
            return jax.random.normal(k, shape, jnp.float32) * (1.0 / np.sqrt(fan_in))
        return {'hidden_states': jax.random.normal(ks[0], (B, S, H), jnp.float32), 'gate_w': w(ks[1], (E, H), H), 'gate_bias': jnp.zeros((E,), jnp.float32), 'Wg': w(ks[2], (E, I, H), H), 'Wu': w(ks[3], (E, I, H), H), 'Wd': w(ks[4], (E, H, I), I), 'Ws_g': w(ks[5], (SH_I, H), H), 'Ws_u': w(ks[6], (SH_I, H), H), 'Ws_d': w(ks[7], (H, SH_I), SH_I)}
    _L0_ffn_in = _L0_ffn_setup()

    def _L1_attn_setup():
        import jax, jax.numpy as jnp
        import numpy as np
        B, T, D = (2, 512, 128)
        H, HD = (16, 64)
        KV = H * HD

        def _l2norm(t, eps=1e-06):
            return t * jax.lax.rsqrt(jnp.sum(t * t, axis=-1, keepdims=True) + eps)
        key = jax.random.key(seed)
        ks = jax.random.split(key, 6)
        sc = lambda k, shape, s: jax.random.normal(k, shape, jnp.float32) * s
        return {'x': sc(ks[0], (B, T, D), 1.0), 'W_in': sc(ks[1], (D, 4 * KV), D ** (-0.5)), 'W_ba': sc(ks[2], (D, 2 * H), D ** (-0.5)), 'conv_w': sc(ks[3], (3 * KV, 1, 4), 0.5), 'dt_bias': jnp.ones((H,), jnp.float32), 'A_log': jnp.log(jax.random.uniform(ks[4], (H,), jnp.float32, 0.001, 16.0)), 'norm_w': jnp.ones((HD,), jnp.float32), 'W_o': sc(ks[5], (KV, D), KV ** (-0.5))}
    _L1_attn_in = _L1_attn_setup()

    def _L1_ffn_setup():
        import jax, jax.numpy as jnp
        import numpy as np
        D = 128
        H = 4
        HD = D // H
        E = 8
        FF = 512
        CAP_FACTOR = 1.0

        def _ln(x, g, b, eps=1e-05):
            mu = jnp.mean(x, -1, keepdims=True)
            v = jnp.mean((x - mu) ** 2, -1, keepdims=True)
            return (x - mu) * jax.lax.rsqrt(v + eps) * g + b

        def _mha(x, w, b, ow, ob):
            L, N, _ = x.shape
            qkv = x @ w.T + b
            q, k, v = jnp.split(qkv, 3, axis=-1)
            rh = lambda t: t.reshape(L, N, H, HD).transpose(1, 2, 0, 3)
            q, k, v = (rh(q), rh(k), rh(v))
            scores = jnp.einsum('nhld,nhmd->nhlm', q, k) / np.float32(np.sqrt(HD))
            attn = jax.nn.softmax(scores, axis=-1)
            o = jnp.einsum('nhlm,nhmd->nhld', attn, v).transpose(2, 0, 1, 3).reshape(L, N, D)
            return o @ ow.T + ob

        def _moe(x, wg, w1, b1, w2, b2):
            L, N, _ = x.shape
            S = L * N
            cap = int(CAP_FACTOR * S) // E
            xf = x.reshape(S, D)
            gates = jax.nn.softmax(xf @ wg, axis=-1)
            idx = jnp.argmax(gates, axis=-1)
            mask1 = jax.nn.one_hot(idx, E, dtype=x.dtype)
            loc = jnp.sum((jnp.cumsum(mask1, 0) - 1.0) * mask1, -1).astype(jnp.int32)
            keep = loc < cap
            gate_val = jnp.take_along_axis(gates, idx[:, None], -1)[:, 0]
            slot = jnp.where(keep, idx.astype(jnp.int32) * cap + loc, E * cap)
            disp = jnp.zeros((E * cap, D), x.dtype).at[slot].set(xf, mode='drop')
            disp = disp.reshape(E, cap, D)
            h = jnp.einsum('ecd,edf->ecf', disp, w1) + b1[:, None, :]
            y = (jnp.einsum('ecf,efd->ecd', h, w2) + b2[:, None, :]).reshape(E * cap, D)
            out = jnp.where(keep[:, None], gate_val[:, None] * y[jnp.minimum(slot, E * cap - 1)], 0.0)
            return out.reshape(L, N, D)
        key = jax.random.key(seed)
        ks = jax.random.split(key, 8)
        L, N = (128, 16)
        s = 0.02
        return {'x': jax.random.normal(ks[0], (L, N, D), jnp.float32), 'in_proj_w': jax.random.normal(ks[1], (3 * D, D), jnp.float32) * s, 'in_proj_b': jnp.zeros((3 * D,), jnp.float32), 'out_proj_w': jax.random.normal(ks[2], (D, D), jnp.float32) * s, 'out_proj_b': jnp.zeros((D,), jnp.float32), 'ln1_g': jnp.ones((D,), jnp.float32), 'ln1_b': jnp.zeros((D,), jnp.float32), 'ln2_g': jnp.ones((D,), jnp.float32), 'ln2_b': jnp.zeros((D,), jnp.float32), 'wg': jax.random.normal(ks[3], (D, E), jnp.float32) * s, 'w1': jax.random.normal(ks[4], (E, D, FF), jnp.float32) * s, 'b1': jnp.zeros((E, FF), jnp.float32), 'w2': jax.random.normal(ks[5], (E, FF, D), jnp.float32) * s, 'b2': jnp.zeros((E, D), jnp.float32)}
    _L1_ffn_in = _L1_ffn_setup()
    _d = {'L0_attn_hidden_states': _L0_attn_in['hidden_states'], 'L0_attn_Wq': _L0_attn_in['Wq'], 'L0_attn_Wk': _L0_attn_in['Wk'], 'L0_attn_Wv': _L0_attn_in['Wv'], 'L0_attn_Wo': _L0_attn_in['Wo'], 'L0_attn_norm_w': _L0_attn_in['norm_w'], 'L0_ffn_gate_w': _L0_ffn_in['gate_w'], 'L0_ffn_gate_bias': _L0_ffn_in['gate_bias'], 'L0_ffn_Wg': _L0_ffn_in['Wg'], 'L0_ffn_Wu': _L0_ffn_in['Wu'], 'L0_ffn_Wd': _L0_ffn_in['Wd'], 'L0_ffn_Ws_g': _L0_ffn_in['Ws_g'], 'L0_ffn_Ws_u': _L0_ffn_in['Ws_u'], 'L0_ffn_Ws_d': _L0_ffn_in['Ws_d'], 'L1_attn_W_in': _L1_attn_in['W_in'], 'L1_attn_W_ba': _L1_attn_in['W_ba'], 'L1_attn_conv_w': _L1_attn_in['conv_w'], 'L1_attn_dt_bias': _L1_attn_in['dt_bias'], 'L1_attn_A_log': _L1_attn_in['A_log'], 'L1_attn_norm_w': _L1_attn_in['norm_w'], 'L1_attn_W_o': _L1_attn_in['W_o'], 'L1_ffn_in_proj_w': _L1_ffn_in['in_proj_w'], 'L1_ffn_in_proj_b': _L1_ffn_in['in_proj_b'], 'L1_ffn_out_proj_w': _L1_ffn_in['out_proj_w'], 'L1_ffn_out_proj_b': _L1_ffn_in['out_proj_b'], 'L1_ffn_ln1_g': _L1_ffn_in['ln1_g'], 'L1_ffn_ln1_b': _L1_ffn_in['ln1_b'], 'L1_ffn_ln2_g': _L1_ffn_in['ln2_g'], 'L1_ffn_ln2_b': _L1_ffn_in['ln2_b'], 'L1_ffn_wg': _L1_ffn_in['wg'], 'L1_ffn_w1': _L1_ffn_in['w1'], 'L1_ffn_b1': _L1_ffn_in['b1'], 'L1_ffn_w2': _L1_ffn_in['w2'], 'L1_ffn_b2': _L1_ffn_in['b2']}
    _x0 = _d['L0_attn_hidden_states']
    _d['L0_attn_hidden_states'] = jax.random.normal(jax.random.fold_in(jax.random.key(seed), 1), (16, 512, 128), dtype=_x0.dtype)
    del _x0
    return _d

def reference(L0_attn_hidden_states, L0_attn_Wq, L0_attn_Wk, L0_attn_Wv, L0_attn_Wo, L0_attn_norm_w, L0_ffn_gate_w, L0_ffn_gate_bias, L0_ffn_Wg, L0_ffn_Wu, L0_ffn_Wd, L0_ffn_Ws_g, L0_ffn_Ws_u, L0_ffn_Ws_d, L1_attn_W_in, L1_attn_W_ba, L1_attn_conv_w, L1_attn_dt_bias, L1_attn_A_log, L1_attn_norm_w, L1_attn_W_o, L1_ffn_in_proj_w, L1_ffn_in_proj_b, L1_ffn_out_proj_w, L1_ffn_out_proj_b, L1_ffn_ln1_g, L1_ffn_ln1_b, L1_ffn_ln2_g, L1_ffn_ln2_b, L1_ffn_wg, L1_ffn_w1, L1_ffn_b1, L1_ffn_w2, L1_ffn_b2):

    def _L0_attn_ref(hidden_states, Wq, Wk, Wv, Wo, norm_w):
        import jax, jax.numpy as jnp
        import numpy as np
        CHUNK = 64
        NORM_EPS = 1e-05
        DENOM_EPS = 1.0
        B, S, HID, H = (4, 512, 128, 8)
        D = HID // H

        def rmsnorm(x, w, eps=NORM_EPS):
            var = jnp.mean(x * x, axis=-1, keepdims=True)
            return x * jax.lax.rsqrt(var + eps) * w

        def chunked_linear_attn(q, k, v):
            b, s, h, d = q.shape
            n = s // CHUNK

            def to_chunks(x):
                return x.reshape(b, n, CHUNK, h, d).transpose(1, 0, 3, 2, 4)
            qc, kc, vc = (to_chunks(q), to_chunks(k), to_chunks(v))
            mask = jnp.tril(jnp.ones((CHUNK, CHUNK), dtype=q.dtype))

            def step(state, inp):
                qq, kk, vv = inp
                inter = jnp.einsum('bhcd,bhde->bhce', qq, state)
                scores = jnp.einsum('bhcd,bhed->bhce', qq, kk) * mask
                intra = jnp.einsum('bhce,bhed->bhcd', scores, vv)
                state = state + jnp.einsum('bhcd,bhce->bhde', kk, vv)
                return (state, inter + intra)
            init = jnp.zeros((b, h, d, d), dtype=q.dtype)
            _, o = jax.lax.scan(step, init, (qc, kc, vc))
            return o.transpose(1, 0, 3, 2, 4).reshape(b, s, h, d)
        b, s, _ = hidden_states.shape
        q = jnp.einsum('bsd,ed->bse', hidden_states, Wq).reshape(b, s, H, D)
        k = jnp.einsum('bsd,ed->bse', hidden_states, Wk).reshape(b, s, H, D)
        v = jnp.einsum('bsd,ed->bse', hidden_states, Wv).reshape(b, s, H, D)
        o = chunked_linear_attn(q, k, v)
        z = jnp.cumsum(k, axis=1)
        denom = jnp.maximum(jnp.abs(jnp.sum(q * z, axis=-1)), DENOM_EPS)[..., None]
        o = o / denom
        o = rmsnorm(o, norm_w)
        o = o.reshape(b, s, H * D)
        return jnp.einsum('bse,de->bsd', o, Wo)

    def _L0_ffn_ref(hidden_states, gate_w, gate_bias, Wg, Wu, Wd, Ws_g, Ws_u, Ws_d):
        import jax, jax.numpy as jnp
        import numpy as np
        E = 16
        K = 4
        NG = 4
        TG = 2
        SCALE = 2.5
        NORM_TOPK = True
        H = 128
        I = 64
        SH_I = I * 2
        B, S = (2, 256)
        x = hidden_states
        b, s, h = x.shape
        n = b * s
        xf = x.reshape(n, h)
        logits = xf @ gate_w.T
        scores = jax.nn.sigmoid(logits)
        sfc = scores + gate_bias
        epg = E // NG
        grp = sfc.reshape(n, NG, epg)
        g_scores = jax.lax.top_k(grp, 2)[0].sum(-1)
        _, gidx = jax.lax.top_k(g_scores, TG)
        gmask = jax.nn.one_hot(gidx, NG, dtype=sfc.dtype).sum(1)
        emask = jnp.repeat(gmask, epg, axis=1)
        masked = jnp.where(emask > 0, sfc, -jnp.inf)
        _, topk_idx = jax.lax.top_k(masked, K)
        topk_w = jnp.take_along_axis(scores, topk_idx, axis=1)
        if K > 1 and NORM_TOPK:
            topk_w = topk_w / (topk_w.sum(-1, keepdims=True) + 1e-20)
        topk_w = topk_w * SCALE
        cw = (jax.nn.one_hot(topk_idx, E, dtype=topk_w.dtype) * topk_w[..., None]).sum(1)
        hg = jnp.einsum('nh,eih->nei', xf, Wg)
        hu = jnp.einsum('nh,eih->nei', xf, Wu)
        act = jax.nn.silu(hg) * hu
        y = jnp.einsum('nei,ne,ehi->nh', act, cw, Wd)
        shared = jax.nn.silu(xf @ Ws_g.T) * (xf @ Ws_u.T) @ Ws_d.T
        y = y + shared
        return (x + y.reshape(b, s, h)).astype(hidden_states.dtype)

    def _L1_attn_ref(x, W_in, W_ba, conv_w, dt_bias, A_log, norm_w, W_o):
        import jax, jax.numpy as jnp
        import numpy as np
        B, T, D = (2, 512, 128)
        H, HD = (16, 64)
        KV = H * HD

        def _l2norm(t, eps=1e-06):
            return t * jax.lax.rsqrt(jnp.sum(t * t, axis=-1, keepdims=True) + eps)
        Bb, Tt, _ = x.shape
        qkvz = x @ W_in
        q, k, v, z = jnp.split(qkvz, 4, axis=-1)
        b, a = jnp.split(x @ W_ba, 2, axis=-1)
        qkv = jnp.concatenate([q, k, v], axis=-1).transpose(0, 2, 1)
        qkv = jax.lax.conv_general_dilated(qkv, conv_w, window_strides=(1,), padding=[(3, 0)], feature_group_count=3 * KV, dimension_numbers=('NCH', 'OIH', 'NCH'))
        qkv = jax.nn.silu(qkv).transpose(0, 2, 1)
        q, k, v = jnp.split(qkv, 3, axis=-1)
        rs = lambda t: t.reshape(Bb, Tt, H, HD)
        q, k, v, z = (rs(q), rs(k), rs(v), rs(z))
        beta = jax.nn.sigmoid(b)
        A = jnp.exp(jnp.maximum(A_log, -2.3))
        g = -A * jax.nn.softplus(a + dt_bias)
        q = _l2norm(q) * HD ** (-0.5)
        k = _l2norm(k)
        tm = lambda t: jnp.swapaxes(t, 0, 1)

        def step(S, inp):
            qt, kt, vt, gt, bt = inp
            S = S * jnp.exp(gt)[..., None, None]
            pred = jnp.einsum('bhk,bhkv->bhv', kt, S)
            S = S + jnp.einsum('bhk,bhv->bhkv', kt, (vt - pred) * bt[..., None])
            o = jnp.einsum('bhk,bhkv->bhv', qt, S)
            return (S, o)
        S0 = jnp.zeros((Bb, H, HD, HD), jnp.float32)
        _, y = jax.lax.scan(step, S0, (tm(q), tm(k), tm(v), tm(g), tm(beta)))
        y = jnp.swapaxes(y, 0, 1)
        y = y * jax.lax.rsqrt(jnp.mean(y * y, axis=-1, keepdims=True) + 1e-06)
        y = norm_w * y * jax.nn.silu(z)
        return y.reshape(Bb, Tt, KV) @ W_o

    def _L1_ffn_ref(x, in_proj_w, in_proj_b, out_proj_w, out_proj_b, ln1_g, ln1_b, ln2_g, ln2_b, wg, w1, b1, w2, b2):
        import jax, jax.numpy as jnp
        import numpy as np
        D = 128
        H = 4
        HD = D // H
        E = 8
        FF = 512
        CAP_FACTOR = 1.0

        def _ln(x, g, b, eps=1e-05):
            mu = jnp.mean(x, -1, keepdims=True)
            v = jnp.mean((x - mu) ** 2, -1, keepdims=True)
            return (x - mu) * jax.lax.rsqrt(v + eps) * g + b

        def _mha(x, w, b, ow, ob):
            L, N, _ = x.shape
            qkv = x @ w.T + b
            q, k, v = jnp.split(qkv, 3, axis=-1)
            rh = lambda t: t.reshape(L, N, H, HD).transpose(1, 2, 0, 3)
            q, k, v = (rh(q), rh(k), rh(v))
            scores = jnp.einsum('nhld,nhmd->nhlm', q, k) / np.float32(np.sqrt(HD))
            attn = jax.nn.softmax(scores, axis=-1)
            o = jnp.einsum('nhlm,nhmd->nhld', attn, v).transpose(2, 0, 1, 3).reshape(L, N, D)
            return o @ ow.T + ob

        def _moe(x, wg, w1, b1, w2, b2):
            L, N, _ = x.shape
            S = L * N
            cap = int(CAP_FACTOR * S) // E
            xf = x.reshape(S, D)
            gates = jax.nn.softmax(xf @ wg, axis=-1)
            idx = jnp.argmax(gates, axis=-1)
            mask1 = jax.nn.one_hot(idx, E, dtype=x.dtype)
            loc = jnp.sum((jnp.cumsum(mask1, 0) - 1.0) * mask1, -1).astype(jnp.int32)
            keep = loc < cap
            gate_val = jnp.take_along_axis(gates, idx[:, None], -1)[:, 0]
            slot = jnp.where(keep, idx.astype(jnp.int32) * cap + loc, E * cap)
            disp = jnp.zeros((E * cap, D), x.dtype).at[slot].set(xf, mode='drop')
            disp = disp.reshape(E, cap, D)
            h = jnp.einsum('ecd,edf->ecf', disp, w1) + b1[:, None, :]
            y = (jnp.einsum('ecf,efd->ecd', h, w2) + b2[:, None, :]).reshape(E * cap, D)
            out = jnp.where(keep[:, None], gate_val[:, None] * y[jnp.minimum(slot, E * cap - 1)], 0.0)
            return out.reshape(L, N, D)
        y1 = _ln(x + _mha(x, in_proj_w, in_proj_b, out_proj_w, out_proj_b), ln1_g, ln1_b)
        y2 = _ln(y1 + _moe(y1, wg, w1, b1, w2, b2), ln2_g, ln2_b)
        return y2
    x = L0_attn_hidden_states
    x = x + _L0_attn_ref(_layernorm(x, axis=-1), L0_attn_Wq, L0_attn_Wk, L0_attn_Wv, L0_attn_Wo, L0_attn_norm_w)
    x = x + _L0_ffn_ref(_layernorm(x, axis=-1), L0_ffn_gate_w, L0_ffn_gate_bias, L0_ffn_Wg, L0_ffn_Wu, L0_ffn_Wd, L0_ffn_Ws_g, L0_ffn_Ws_u, L0_ffn_Ws_d)
    x = x + _L1_attn_ref(_layernorm(x, axis=-1), L1_attn_W_in, L1_attn_W_ba, L1_attn_conv_w, L1_attn_dt_bias, L1_attn_A_log, L1_attn_norm_w, L1_attn_W_o)
    x = x + _L1_ffn_ref(_layernorm(x, axis=-1), L1_ffn_in_proj_w, L1_ffn_in_proj_b, L1_ffn_out_proj_w, L1_ffn_out_proj_b, L1_ffn_ln1_g, L1_ffn_ln1_b, L1_ffn_ln2_g, L1_ffn_ln2_b, L1_ffn_wg, L1_ffn_w1, L1_ffn_b1, L1_ffn_w2, L1_ffn_b2)
    return x

_drawn_inputs = setup_inputs


def setup_inputs(seed=0):
    import zlib

    import numpy as np

    out = dict(_drawn_inputs(seed))
    spreads = {'L0_attn_norm_w': (1.0, 0.2),
     'L0_ffn_gate_bias': (0.0, 0.1),
     'L1_attn_dt_bias': (1.0, 0.6),
     'L1_attn_norm_w': (1.0, 0.2),
     'L1_ffn_in_proj_b': (0.0, 0.8),
     'L1_ffn_out_proj_b': (0.0, 0.1),
     'L1_ffn_ln1_g': (1.0, 0.2),
     'L1_ffn_ln1_b': (0.0, 0.1),
     'L1_ffn_ln2_g': (1.0, 0.2),
     'L1_ffn_ln2_b': (0.0, 0.1),
     'L1_ffn_b1': (0.0, 0.8),
     'L1_ffn_b2': (0.0, 0.8)}
    factors = {'L1_ffn_in_proj_w': 8.0,
     'L1_ffn_out_proj_w': 6.542,
     'L1_ffn_wg': 7.907,
     'L1_ffn_w1': 8.0,
     'L1_ffn_w2': 8.0}
    for name, (base, spread) in spreads.items():
        noise = np.random.default_rng([zlib.crc32(name.encode()), seed]).standard_normal(out[name].shape)
        drawn = base * np.exp(spread * noise) if base else spread * noise
        out[name] = jnp.asarray(drawn.astype(out[name].dtype))
    for name, factor in factors.items():
        out[name] = (out[name] * factor).astype(out[name].dtype)
    return out
```

```python
from contextlib import ExitStack

import concourse.bass as bass
from concourse import mybir

F32 = mybir.dt.float32
ALU = mybir.AluOpType
ACT = mybir.ActivationFunctionType
AX_X = mybir.AxisListType.X

P = 128
D = 128
NSEQ, SEQ = 16, 512
NT = NSEQ * SEQ // P
LN_EPS = 1e-5


def semaphores(nc, ctx, phase):
    made = {}

    def sem(name):
        if name not in made:
            made[name] = nc.alloc_semaphore(name=f"{phase}_{name}")
        return made[name]

    def clear():
        nc.clear_and_free_semaphores(list(made.values()))
        nc.all_engine_barrier()
    ctx.callback(clear)
    return sem


def chain(engine, sem, start):
    done = [0]

    def link(ins):
        done[0] += 1
        ins.then_inc(sem, 1)
        engine.wait_ge(sem, start + done[0])
    return link, done


def load_seq(x, s):
    return x[bass.ds(s * SEQ, SEQ), :].rearrange("(c p) d -> p c d", p=P)


def make_identity(pool, ident, sem):
    pool.memset(ident[:, :], 0.0).then_inc(sem, 1)
    pool.wait_ge(sem, 1)
    pool.affine_select(out=ident[:, :], in_=ident[:, :], compare_op=ALU.not_equal, fill=1.0, base=0,
                       pattern=[[-1, P]], channel_multiplier=1).then_inc(sem, 1)


def linear_attention_phase(nc, x_in, x_out, wq_t, wk_t, wv_t, wo_t, norm_w):
    H, HD, HP = 8, 16, 32
    G = 4
    NC = SEQ // P
    V1 = HD + 1
    DVE_LINKS = 13
    with ExitStack() as ctx:
        def sb(name, shape):
            return ctx.enter_context(nc.sbuf_tensor("a_" + name, shape, F32))
        sem = semaphores(nc, ctx, "a")
        ident = sb("ident", [P, P])
        causal = sb("causal", [P, P])
        own_head = sb("own_head", [P, G, V1])
        mhalf = sb("mhalf", [P, 32])
        wq = sb("wq", [P, 2 * P])
        wkv = sb("wkv", [P, 3 * P])
        wo = sb("wo", [P, P])
        nw = sb("nw", [P, HD])
        xt = sb("xt", [P, NC, D])
        h = sb("h", [P, NC, D])
        hT = sb("hT", [P, SEQ])
        qT = sb("qT", [P, 2, SEQ])
        kT = sb("kT", [P, 2, SEQ])
        kt = sb("kt", [P, NC, 2 * P])
        v1 = sb("v1", [P, NC, H, V1])
        pr = sb("pr", [P, 2, G, 2, P])
        state = sb("state", [P, 2, G, V1])
        upd = sb("upd", [P, 2, G, V1])
        o = sb("o", [P, NC * H, V1])
        on = sb("on", [P, NC * H, HD])
        sq = sb("sq", [P, NC * H, HD])
        oT = sb("oT", [P, SEQ])
        xo = sb("xo", [P, NC, D])
        st = sb("st", [P, NC, 6])
        mv = sb("mv", [P, NC, 2])
        ve = sb("ve", [P, NC])
        rstd = sb("rstd", [P, NC])
        den = sb("den", [P, NC * H])
        rden = sb("rden", [P, NC * H])
        var = sb("var", [P, NC * H])
        rms = sb("rms", [P, NC * H])
        ps = [ctx.enter_context(nc.psum_tensor(f"a_ps{n}", [P, 512], F32)) for n in range(8)]
        block = ctx.enter_context(nc.Block())

        @block.sync
        def _(sp):
            sp.wait_ge(sem("padded"), 2)
            sp.dma_start(wq[:, :].rearrange("p (h e) -> p h e", e=HP)[:, :, 0:HD],
                         wq_t.rearrange("d (h e) -> d h e", e=HD)).then_inc(sem("weights"), 16)
            sp.dma_start(wkv[:, 0:2 * P].rearrange("p (h e) -> p h e", e=HP)[:, :, 0:HD],
                         wk_t.rearrange("d (h e) -> d h e", e=HD)).then_inc(sem("weights"), 16)
            sp.dma_start(wkv[:, 2 * P:3 * P], wv_t).then_inc(sem("weights"), 16)
            sp.dma_start(wo[:, :], wo_t).then_inc(sem("weights"), 16)
            sp.dma_start(nw[:, :], norm_w.partition_broadcast(P)).then_inc(sem("weights"), 16)
            with sp.Fori(0, NSEQ) as s:
                sp.wait_ge(sem("x_used"), s)
                sp.dma_start(xt[:, :, :], load_seq(x_in, s)).then_inc(sem("x_loaded"), 16)
                sp.wait_ge(sem("x_used"), s + 1)
                sp.dma_start(load_seq(x_out, s), xo[:, :, :]).then_inc(sem("stored"), 16)
            sp.wait_ge(sem("stored"), 16 * NSEQ)

        @block.gpsimd
        def _(pool):
            make_identity(pool, ident, sem("ident"))
            pool.memset(wq[:, :], 0.0).then_inc(sem("padded"), 1)
            pool.memset(wkv[:, :], 0.0).then_inc(sem("padded"), 1)
            pool.memset(mhalf[:, :], -0.5).then_inc(sem("ones"), 1)
            pool.memset(v1[:, :, :, :], 1.0).then_inc(sem("ones"), 1)
            pool.memset(causal[:, :], 1.0).then_inc(sem("ones"), 1)
            pool.memset(own_head[:, :, :], 1.0).then_inc(sem("ones"), 1)
            pool.wait_ge(sem("ones"), 4)
            pool.affine_select(out=causal[:, :], in_=causal[:, :], compare_op=ALU.is_ge, fill=0.0, base=0,
                               pattern=[[1, P]], channel_multiplier=-1).then_inc(sem("ones"), 1)
            pool.affine_select(out=own_head[:, :, :], in_=own_head[:, :, :], compare_op=ALU.is_ge, fill=0.0,
                               base=0, pattern=[[-HP, G], [0, V1]], channel_multiplier=1).then_inc(sem("ones"), 1)
            pool.wait_ge(sem("ones"), 6)
            pool.affine_select(out=own_head[:, :, :], in_=own_head[:, :, :], compare_op=ALU.is_ge, fill=0.0,
                               base=HP - 1, pattern=[[HP, G], [0, V1]], channel_multiplier=-1).then_inc(sem("ones"), 1)
            with pool.Fori(0, NSEQ) as s:
                pool.wait_ge(sem("var_ready"), s + 1)
                pool.tensor_tensor(rstd[:, :], ve[:, :], mhalf[:, 0:NC], ALU.pow).then_inc(sem("rstd_ready"), 1)
                pool.wait_ge(sem("hvar_ready"), s + 1)
                pool.tensor_tensor(rms[:, :], var[:, :], mhalf[:, :], ALU.pow).then_inc(sem("rms_ready"), 1)

        @block.scalar
        def _(act):
            with act.Fori(0, NSEQ) as s:
                act.wait_ge(sem("h_turned"), s + 1)
                act.activation(hT[:, :], ps[0][:, :], ACT.Copy).then_inc(sem("hT_ready"), 1)
                act.wait_ge(sem("qk_ready"), s + 1)
                for g in range(2):
                    act.activation(qT[:, g, :], ps[1 + g][:, :], ACT.Copy)
                    last = act.activation(kT[:, g, :], ps[3 + g][:, :], ACT.Copy)
                last.then_inc(sem("qkT_ready"), 1)
                act.wait_ge(sem("o_turned"), s + 1)
                act.activation(oT[:, :], ps[0][:, :], ACT.Copy).then_inc(sem("oT_ready"), 1)

        @block.tensor
        def _(pe):
            pe.wait_ge(sem("ident"), 2)
            pe.wait_ge(sem("weights"), 16 * 5)
            with pe.Fori(0, NSEQ) as s:
                pe.wait_ge(sem("h_ready"), s + 1)
                for c in range(NC):
                    last = pe.transpose(ps[0][:, c * P:(c + 1) * P], h[:, c, :], ident[:, :])
                last.then_inc(sem("h_turned"), 1)
                pe.wait_ge(sem("hT_ready"), s + 1)
                for g in range(2):
                    pe.matmul(ps[1 + g][:, :], wq[:, g * P:(g + 1) * P], hT[:, :], start=True, stop=True)
                    last = pe.matmul(ps[3 + g][:, :], wkv[:, g * P:(g + 1) * P], hT[:, :], start=True, stop=True)
                last.then_inc(sem("qk_ready"), 1)
                for c in range(NC):
                    if c == 3:
                        pe.wait_ge(sem("kv_used"), NC * s + 1)
                    pe.matmul(ps[5 + c % 3][:, 0:3 * P], hT[:, c * P:(c + 1) * P], wkv[:, :],
                              start=True, stop=True).then_inc(sem("kv_ready"), 1)
                pe.wait_ge(sem("qkT_ready"), s + 1)
                for c in range(NC):
                    here = slice(c * P, (c + 1) * P)
                    half = (c % 2) * 2 * P
                    for j in range(G):
                        for g in range(2):
                            last = pe.matmul(ps[1 + j][:, half + g * P:half + (g + 1) * P],
                                             kT[HP * j:HP * j + HD, g, here], qT[HP * j:HP * j + HD, g, here],
                                             start=True, stop=True)
                    last.then_inc(sem("scores"), 1)
                    pe.wait_ge(sem("state_ready"), (NC + 1) * s + c + 1)
                    for g in range(2):
                        pe.matmul(ps[5][:, g * G * V1:(g + 1) * G * V1], qT[:, g, here],
                                  state[:, g, :, :].rearrange("p h e -> p (h e)"),
                                  start=(g == 0), stop=False, skip_group_check=True)
                    pe.wait_ge(sem("probs"), NC * s + c + 1)
                    for hd in range(H):
                        last = pe.matmul(ps[5][:, hd * V1:(hd + 1) * V1], pr[:, c % 2, hd % G, hd // G, :],
                                         v1[:, c, hd, :], start=False, stop=True, skip_group_check=True)
                    last.then_inc(sem("o_ready"), 1)
                    for g in range(2):
                        last = pe.matmul(ps[7][:, g * G * V1:(g + 1) * G * V1], kt[:, c, g * P:(g + 1) * P],
                                         v1[:, c, g * G:(g + 1) * G, :].rearrange("p h e -> p (h e)"),
                                         start=True, stop=True)
                    last.then_inc(sem("update"), 1)
                pe.wait_ge(sem("on_ready"), s + 1)
                for c in range(NC):
                    last = pe.transpose(ps[0][:, c * P:(c + 1) * P],
                                        on[:, c * H:(c + 1) * H, :].rearrange("p h e -> p (h e)"), ident[:, :])
                last.then_inc(sem("o_turned"), 1)
                pe.wait_ge(sem("oT_ready"), s + 1)
                for c in range(NC):
                    last = pe.matmul(ps[6][:, c * P:(c + 1) * P], oT[:, c * P:(c + 1) * P], wo[:, :],
                                     start=True, stop=True)
                last.then_inc(sem("y_ready"), 1)

        @block.vector
        def _(dve):
            dve.wait_ge(sem("ones"), 7)
            dve.wait_ge(sem("weights"), 16 * 5)
            with dve.Fori(0, NSEQ) as s:
                link, links = chain(dve, sem("dve"), s * DVE_LINKS)
                dve.wait_ge(sem("x_loaded"), 16 * s + 16)
                for c in range(NC):
                    last = dve.bn_stats(st[:, c, :], xt[:, c, :])
                link(last)
                dve.sem_inc(sem("passed"))
                for c in range(NC):
                    last = dve.bn_aggr(mv[:, c, :], st[:, c, :])
                link(last)
                dve.tensor_scalar(ve[:, :], mv[:, :, 1], LN_EPS, None, ALU.add).then_inc(sem("var_ready"), 1)
                dve.wait_ge(sem("rstd_ready"), s + 1)
                for c in range(NC):
                    last = dve.tensor_scalar(h[:, c, :], xt[:, c, :], mv[:, c, 0:1], rstd[:, c:c + 1],
                                             ALU.subtract, ALU.mult)
                last.then_inc(sem("h_ready"), 1)
                for c in range(NC):
                    dve.wait_ge(sem("kv_ready"), NC * s + c + 1)
                    dve.tensor_copy(kt[:, c, :], ps[5 + c % 3][:, 0:2 * P])
                    last = dve.tensor_copy(v1[:, c, :, 0:HD],
                                           ps[5 + c % 3][:, 2 * P:3 * P].rearrange("p (h e) -> p h e", e=HD))
                    last.then_inc(sem("kv_used"), 1)
                dve.wait_ge(sem("kv_used"), NC * s + NC)
                dve.memset(state[:, :, :, :], 0.0).then_inc(sem("state_ready"), 1)
                for c in range(NC):
                    half = (c % 2) * 2 * P
                    dve.wait_ge(sem("scores"), NC * s + c + 1)
                    for j in range(G):
                        last = dve.tensor_tensor(
                            pr[:, c % 2, j, :, :], ps[1 + j][:, half:half + 2 * P].rearrange("p (g t) -> p g t", g=2),
                            causal[:, :].unsqueeze(1).to_broadcast([P, 2, P]), ALU.mult)
                    last.then_inc(sem("probs"), 1)
                    dve.wait_ge(sem("o_ready"), NC * s + c + 1)
                    dve.tensor_copy(o[:, c * H:(c + 1) * H, :],
                                    ps[5][:, 0:H * V1].rearrange("p (h e) -> p h e", e=V1))
                    dve.wait_ge(sem("update"), NC * s + c + 1)
                    link(dve.tensor_tensor(upd[:, :, :, :].rearrange("p g h e -> p g (h e)"),
                                           ps[7][:, 0:H * V1].rearrange("p (g e) -> p g e", g=2),
                                           own_head[:, :, :].rearrange("p h e -> p (h e)").unsqueeze(1)
                                           .to_broadcast([P, 2, G * V1]), ALU.mult))
                    dve.tensor_tensor(state[:, :, :, :], state[:, :, :, :], upd[:, :, :, :], ALU.add)\
                       .then_inc(sem("state_ready"), 1)
                    dve.wait_ge(sem("state_ready"), (NC + 1) * s + c + 2)
                link(dve.scalar_tensor_tensor(out=den[:, :], in0=o[:, :, HD], scalar=-1.0, in1=o[:, :, HD],
                                              op0=ALU.mult, op1=ALU.max))
                link(dve.tensor_scalar(den[:, :], den[:, :], 1.0, None, ALU.max))
                link(dve.reciprocal(rden[:, :], den[:, :]))
                link(dve.tensor_tensor(on[:, :, :], o[:, :, 0:HD],
                                       rden[:, :].unsqueeze(2).to_broadcast([P, NC * H, HD]), ALU.mult))
                link(dve.tensor_tensor(sq[:, :, :], on[:, :, :], on[:, :, :], ALU.mult))
                link(dve.tensor_reduce(var[:, :], sq[:, :, :], AX_X, ALU.add))
                dve.tensor_scalar(var[:, :], var[:, :], 1.0 / HD, 1e-5, ALU.mult, ALU.add)\
                   .then_inc(sem("hvar_ready"), 1)
                dve.wait_ge(sem("rms_ready"), s + 1)
                link(dve.tensor_tensor(on[:, :, :], on[:, :, :],
                                       rms[:, :].unsqueeze(2).to_broadcast([P, NC * H, HD]), ALU.mult))
                dve.tensor_tensor(on[:, :, :], on[:, :, :],
                                  nw[:, :].unsqueeze(1).to_broadcast([P, NC * H, HD]), ALU.mult)\
                   .then_inc(sem("on_ready"), 1)
                dve.wait_ge(sem("y_ready"), s + 1)
                dve.wait_ge(sem("stored"), 16 * s)
                dve.tensor_tensor(xo[:, :, :], xt[:, :, :], ps[6][:, :].rearrange("p (c d) -> p c d", c=NC), ALU.add)\
                   .then_inc(sem("x_used"), 1)
                assert links[0] == DVE_LINKS, links


def expert_phase(nc, x_in, x_out, gate_t, gate_bias, wg_t, wu_t, wd_t, wsg_t, wsu_t, wsd_t):
    E, NG, K, TG, SCALE = 16, 4, 4, 2, 2.5
    EG = E // NG
    NC = SEQ // P
    NB = E * 64 // P
    DVE_LINKS = 35
    BIG = 1e30
    with ExitStack() as ctx:
        def sb(name, shape):
            return ctx.enter_context(nc.sbuf_tensor("b_" + name, shape, F32))
        sem = semaphores(nc, ctx, "b")
        ident = sb("ident", [P, P])
        spread = sb("spread", [E, E, 64])
        before_g = sb("before_g", [P, NG, NG])
        before_e = sb("before_e", [P, E, E])
        mhalf = sb("mhalf", [P, 32])
        gw = sb("gw", [P, E])
        bias = sb("bias", [P, E])
        wg = sb("wg", [P, NB + 1, P])
        wu = sb("wu", [P, NB + 1, P])
        wd = sb("wd", [P, NB + 1, D])
        xt = sb("xt", [P, NC, D])
        h = sb("h", [P, NC, D])
        hT = sb("hT", [P, SEQ])
        th = sb("th", [P, 2, SEQ])
        gated = sb("gated", [P, 2, SEQ])
        both = sb("both", [P, 2, SEQ])
        act_sb = sb("act", [P, NB + 1, SEQ])
        xo = sb("xo", [P, NC, D])
        st = sb("st", [P, NC, 6])
        mv = sb("mv", [P, NC, 2])
        ve = sb("ve", [P, NC])
        rstd = sb("rstd", [P, NC])
        ex = sb("ex", [P, NC, E])
        ex1 = sb("ex1", [P, NC, E])
        score = sb("score", [P, NC, E])
        sf = sb("sf", [P, NC * NG, EG])
        hi = sb("hi", [P, NC * NG, 2])
        lo = sb("lo", [P, NC * NG, 2])
        top1 = sb("top1", [P, NC * NG])
        mid = sb("mid", [P, NC * NG])
        lows = sb("lows", [P, NC * NG])
        gs = sb("gs", [P, NC, NG])
        ggt = sb("ggt", [P, NC, NG * NG])
        geq = sb("geq", [P, NC, NG * NG])
        grank = sb("grank", [P, NC * NG])
        gin = sb("gin", [P, NC * NG])
        gout = sb("gout", [P, NC * NG])
        sfm = sb("sfm", [P, NC, E])
        egt = sb("egt", [P, NC, E * E])
        eeq = sb("eeq", [P, NC, E * E])
        erank = sb("erank", [P, NC * E])
        w = sb("w", [P, NC, E])
        wsum = sb("wsum", [P, NC])
        wrec = sb("wrec", [P, NC])
        cw = sb("cw", [P, NC, E])
        cwT = sb("cwT", [E, SEQ])
        ps = [ctx.enter_context(nc.psum_tensor(f"b_ps{n}", [P, 512], F32)) for n in range(8)]
        block = ctx.enter_context(nc.Block())
        WEIGHTS = 16 * 8

        @block.sync
        def _(sp):
            for to, of in ((gw[:, :], gate_t), (bias[:, :], gate_bias.partition_broadcast(P)),
                           (wg[:, 0:NB, :], wg_t.rearrange("d (b m) -> d b m", m=P)),
                           (wu[:, 0:NB, :], wu_t.rearrange("d (b m) -> d b m", m=P)),
                           (wd[:, 0:NB, :], wd_t.rearrange("(b m) d -> m b d", m=P)),
                           (wg[:, NB, :], wsg_t), (wu[:, NB, :], wsu_t), (wd[:, NB, :], wsd_t)):
                sp.dma_start(to, of).then_inc(sem("weights"), 16)
            with sp.Fori(0, NSEQ) as s:
                sp.wait_ge(sem("x_used"), s)
                sp.dma_start(xt[:, :, :], load_seq(x_in, s)).then_inc(sem("x_loaded"), 16)
                sp.wait_ge(sem("x_used"), s + 1)
                sp.dma_start(load_seq(x_out, s), xo[:, :, :]).then_inc(sem("stored"), 16)
            sp.wait_ge(sem("stored"), 16 * NSEQ)

        @block.gpsimd
        def _(pool):
            make_identity(pool, ident, sem("ident"))
            pool.memset(mhalf[:, :], -0.5).then_inc(sem("ones"), 1)
            pool.memset(spread[:, :, :], 1.0).then_inc(sem("ones"), 1)
            pool.memset(before_g[:, :, :], 1.0).then_inc(sem("ones"), 1)
            pool.memset(before_e[:, :, :], 1.0).then_inc(sem("ones"), 1)
            pool.wait_ge(sem("ones"), 4)
            pool.affine_select(out=spread[:, :, :], in_=spread[:, :, :], compare_op=ALU.is_equal, fill=0.0, base=0,
                               pattern=[[-1, E], [0, 64]], channel_multiplier=1).then_inc(sem("ones"), 1)
            pool.affine_select(out=before_g[:, :, :], in_=before_g[:, :, :], compare_op=ALU.is_gt, fill=0.0, base=0,
                               pattern=[[1, NG], [-1, NG]], channel_multiplier=0).then_inc(sem("ones"), 1)
            pool.affine_select(out=before_e[:, :, :], in_=before_e[:, :, :], compare_op=ALU.is_gt, fill=0.0, base=0,
                               pattern=[[1, E], [-1, E]], channel_multiplier=0).then_inc(sem("ones"), 1)
            with pool.Fori(0, NSEQ) as s:
                pool.wait_ge(sem("var_ready"), s + 1)
                pool.tensor_tensor(rstd[:, :], ve[:, :], mhalf[:, 0:NC], ALU.pow).then_inc(sem("rstd_ready"), 1)

        @block.scalar
        def _(act):
            with act.Fori(0, NSEQ) as s:
                act.wait_ge(sem("h_turned"), s + 1)
                act.activation(hT[:, :], ps[0][:, :], ACT.Copy).then_inc(sem("hT_ready"), 1)
                act.wait_ge(sem("logits"), s + 1)
                act.activation(ex[:, :, :], ps[1][:, 0:NC * E].rearrange("p (c e) -> p c e", e=E), ACT.Exp, scale=-1.0)\
                   .then_inc(sem("ex_ready"), 1)
                for b in range(NB + 1):
                    act.wait_ge(sem("gate_up"), (NB + 1) * s + b + 1)
                    if b >= 2:
                        act.wait_ge(sem("gate_used"), (NB + 1) * s + b - 1)
                    act.activation(th[:, b % 2, :], ps[2 + b % 2][:, :], ACT.Tanh, scale=0.5)\
                       .then_inc(sem("tanh"), 1)
                    if b == 1:
                        act.wait_ge(sem("cw_turned"), s + 1)
                        act.activation(cwT[:, :], ps[1][0:E, :], ACT.Copy).then_inc(sem("cwT_ready"), 1)

        @block.tensor
        def _(pe):
            pe.wait_ge(sem("ident"), 2)
            pe.wait_ge(sem("ones"), 7)
            pe.wait_ge(sem("weights"), WEIGHTS)
            with pe.Fori(0, NSEQ) as s:
                pe.wait_ge(sem("h_ready"), s + 1)
                for c in range(NC):
                    last = pe.transpose(ps[0][:, c * P:(c + 1) * P], h[:, c, :], ident[:, :])
                last.then_inc(sem("h_turned"), 1)
                pe.wait_ge(sem("hT_ready"), s + 1)
                for c in range(NC):
                    last = pe.matmul(ps[1][:, c * E:(c + 1) * E], hT[:, c * P:(c + 1) * P], gw[:, :],
                                     start=True, stop=True)
                last.then_inc(sem("logits"), 1)

                def up(b):
                    if b >= 2:
                        pe.wait_ge(sem("gate_used"), (NB + 1) * s + b - 1)
                    pe.matmul(ps[2 + b % 2][:, :], wg[:, b, :], hT[:, :], start=True, stop=True)
                    pe.matmul(ps[4 + b % 2][:, :], wu[:, b, :], hT[:, :], start=True, stop=True)\
                      .then_inc(sem("gate_up"), 1)

                up(0)
                up(1)
                pe.wait_ge(sem("cw_ready"), s + 1)
                for c in range(NC):
                    last = pe.transpose(ps[1][0:E, c * P:(c + 1) * P], cw[:, c, :], ident[:, :])
                last.then_inc(sem("cw_turned"), 1)
                pe.wait_ge(sem("cwT_ready"), s + 1)
                for b in range(NB):
                    if b >= 2:
                        up(b)
                        pe.wait_ge(sem("acted"), NB * s + b - 1)
                    pe.matmul(ps[6 + b % 2][:, :], spread[:, 2 * b:2 * b + 2, :].rearrange("e a i -> e (a i)"),
                              cwT[:, :], start=True, stop=True).then_inc(sem("cw_spread"), 1)
                up(NB)
                pe.wait_ge(sem("all_acted"), s + 1)
                for c in range(NC):
                    for b in range(NB + 1):
                        last = pe.matmul(ps[0][:, c * P:(c + 1) * P], act_sb[:, b, c * P:(c + 1) * P], wd[:, b, :],
                                         start=(b == 0), stop=(b == NB))
                last.then_inc(sem("y_ready"), 1)

        @block.vector
        def _(dve):
            dve.wait_ge(sem("ones"), 7)
            dve.wait_ge(sem("weights"), WEIGHTS)
            with dve.Fori(0, NSEQ) as s:
                link, links = chain(dve, sem("dve"), s * DVE_LINKS)
                dve.wait_ge(sem("x_loaded"), 16 * s + 16)
                for c in range(NC):
                    last = dve.bn_stats(st[:, c, :], xt[:, c, :])
                link(last)
                dve.sem_inc(sem("passed"))
                for c in range(NC):
                    last = dve.bn_aggr(mv[:, c, :], st[:, c, :])
                link(last)
                dve.tensor_scalar(ve[:, :], mv[:, :, 1], LN_EPS, None, ALU.add).then_inc(sem("var_ready"), 1)
                dve.wait_ge(sem("rstd_ready"), s + 1)
                for c in range(NC):
                    last = dve.tensor_scalar(h[:, c, :], xt[:, c, :], mv[:, c, 0:1], rstd[:, c:c + 1],
                                             ALU.subtract, ALU.mult)
                last.then_inc(sem("h_ready"), 1)
                dve.wait_ge(sem("ex_ready"), s + 1)
                link(dve.tensor_scalar(ex1[:, :, :], ex[:, :, :], 1.0, None, ALU.add))
                link(dve.reciprocal(score[:, :, :], ex1[:, :, :]))
                sf_e = sf[:, :, :].rearrange("p (c g) a -> p c (g a)", c=NC)
                link(dve.tensor_tensor(sf_e, score[:, :, :], bias[:, :].unsqueeze(1).to_broadcast([P, NC, E]), ALU.add))
                dve.tensor_tensor(hi[:, :, :], sf[:, :, 0:EG:2], sf[:, :, 1:EG:2], ALU.max)
                link(dve.tensor_tensor(lo[:, :, :], sf[:, :, 0:EG:2], sf[:, :, 1:EG:2], ALU.min))
                dve.tensor_tensor(top1[:, :], hi[:, :, 0], hi[:, :, 1], ALU.max)
                dve.tensor_tensor(mid[:, :], hi[:, :, 0], hi[:, :, 1], ALU.min)
                link(dve.tensor_tensor(lows[:, :], lo[:, :, 0], lo[:, :, 1], ALU.max))
                link(dve.tensor_tensor(mid[:, :], mid[:, :], lows[:, :], ALU.max))
                link(dve.tensor_tensor(gs[:, :, :].rearrange("p c g -> p (c g)"), top1[:, :], mid[:, :], ALU.add))

                def rank(gt, eq, values, before, n, out):
                    view = lambda t, c: t[:, c, :].rearrange("p (i j) -> p i j", i=n)
                    for c in range(NC):
                        other = values[:, c, :].unsqueeze(1).to_broadcast([P, n, n])
                        own = values[:, c, :].unsqueeze(2).to_broadcast([P, n, n])
                        dve.tensor_tensor(view(gt, c), other, own, ALU.is_gt)
                        last = dve.tensor_tensor(view(eq, c), other, own, ALU.is_equal)
                    link(last)
                    link(dve.tensor_tensor(eq[:, :, :], eq[:, :, :], before[:, :, :].rearrange("p i j -> p (i j)")
                                           .unsqueeze(1).to_broadcast([P, NC, n * n]), ALU.mult))
                    link(dve.tensor_tensor(gt[:, :, :], gt[:, :, :], eq[:, :, :], ALU.add))
                    link(dve.tensor_reduce(out, gt[:, :, :].rearrange("p c (i j) -> p (c i) j", i=n), AX_X, ALU.add))

                rank(ggt, geq, gs, before_g, NG, grank[:, :])
                link(dve.tensor_scalar(gin[:, :], grank[:, :], float(TG), None, ALU.is_lt))
                dve.tensor_scalar(gout[:, :], gin[:, :], BIG, -BIG, ALU.mult, ALU.add)
                sfm_g = sfm[:, :, :].rearrange("p c (g a) -> p (c g) a", a=EG)
                link(dve.tensor_tensor(sfm_g, sf[:, :, :], gin[:, :].unsqueeze(2).to_broadcast([P, NC * NG, EG]), ALU.mult))
                link(dve.tensor_tensor(sfm_g, sfm_g, gout[:, :].unsqueeze(2).to_broadcast([P, NC * NG, EG]), ALU.add))
                rank(egt, eeq, sfm, before_e, E, erank[:, :])
                link(dve.tensor_scalar(erank[:, :], erank[:, :], float(K), None, ALU.is_lt))
                link(dve.tensor_tensor(w[:, :, :], score[:, :, :], erank[:, :].rearrange("p (c e) -> p c e", e=E), ALU.mult))
                link(dve.tensor_reduce(wsum[:, :], w[:, :, :], AX_X, ALU.add))
                link(dve.tensor_scalar(wsum[:, :], wsum[:, :], 1e-20, None, ALU.add))
                link(dve.reciprocal(wrec[:, :], wsum[:, :]))
                link(dve.tensor_scalar(wrec[:, :], wrec[:, :], SCALE / 2, None, ALU.mult))
                dve.tensor_tensor(cw[:, :, :], w[:, :, :], wrec[:, :].unsqueeze(2).to_broadcast([P, NC, E]), ALU.mult)\
                   .then_inc(sem("cw_ready"), 1)
                for b in range(NB + 1):
                    dve.wait_ge(sem("tanh"), (NB + 1) * s + b + 1)
                    link(dve.scalar_tensor_tensor(out=gated[:, b % 2, :], in0=th[:, b % 2, :], scalar=1.0,
                                                  in1=ps[2 + b % 2][:, :], op0=ALU.add, op1=ALU.mult))
                    if b < NB:
                        dve.tensor_tensor(both[:, b % 2, :], gated[:, b % 2, :], ps[4 + b % 2][:, :], ALU.mult)\
                           .then_inc(sem("gate_used"), 1)
                        dve.wait_ge(sem("gate_used"), (NB + 1) * s + b + 1)
                        dve.wait_ge(sem("cw_spread"), NB * s + b + 1)
                        dve.tensor_tensor(act_sb[:, b, :], both[:, b % 2, :], ps[6 + b % 2][:, :], ALU.mult)\
                           .then_inc(sem("acted"), 1)
                    else:
                        dve.scalar_tensor_tensor(out=act_sb[:, b, :], in0=gated[:, b % 2, :], scalar=0.5,
                                                 in1=ps[4 + b % 2][:, :], op0=ALU.mult, op1=ALU.mult)\
                           .then_inc(sem("all_acted"), 1)
                dve.wait_ge(sem("stored"), 16 * s)
                dve.tensor_tensor(xo[:, :, :], xt[:, :, :], h[:, :, :], ALU.add).then_inc(sem("gate_used"), 1)
                dve.wait_ge(sem("gate_used"), (NB + 1) * s + NB + 1)
                dve.wait_ge(sem("y_ready"), s + 1)
                dve.tensor_tensor(xo[:, :, :], xo[:, :, :], ps[0][:, :].rearrange("p (c d) -> p c d", c=NC), ALU.add)\
                   .then_inc(sem("x_used"), 1)
                assert links[0] == DVE_LINKS, links


CH = 64
NCH = SEQ // CH
NPAIR = NSEQ // 2
NSTEP = NPAIR * NCH
DH, DHD, DJ = 16, 64, 8
TAPS = 4
GATES = 5 * DH


def pair_rows(x, p, b, q, n):
    return x[bass.ds(p * (2 * SEQ) + (b * SEQ + q * n * CH), n * CH), :].rearrange("(c t) d -> t c d", t=CH)


def gate_phase(nc, x_in, h_t, gates, w_ba, dt_bias, a_log):
    NC = 4
    DVE_LINKS = 7
    with ExitStack() as ctx:
        def sb(name, shape):
            return ctx.enter_context(nc.sbuf_tensor("g_" + name, shape, F32))
        sem = semaphores(nc, ctx, "g")
        ident = sb("ident", [P, P])
        upto = sb("upto", [P, 2, CH])
        after = sb("after", [P, 2, CH])
        of_seq = sb("of_seq", [P, 2, CH])
        mhalf = sb("mhalf", [P, NC])
        pad = sb("pad", [P, NSEQ, TAPS - 1])
        wba = sb("wba", [P, 2 * DH])
        dt = sb("dt", [P, DH])
        alog = sb("alog", [P, DH])
        neg_a = sb("neg_a", [P, DH])
        xt = sb("xt", [P, NC, D])
        h = sb("h", [P, NC, D])
        hT = sb("hT", [P, NC, 2, CH])
        st = sb("st", [P, NC, 6])
        mv = sb("mv", [P, NC, 2])
        ve = sb("ve", [P, NC])
        rstd = sb("rstd", [P, NC])
        eb = sb("eb", [P, NC, DH])
        ad = sb("ad", [P, NC, DH])
        aa = sb("aa", [P, NC, DH])
        ea = sb("ea", [P, NC, DH])
        la = sb("la", [P, NC, DH])
        gg = sb("gg", [P, NC, DH])
        out = sb("out", [P, NC, 5, DH])
        ps = [ctx.enter_context(nc.psum_tensor(f"g_ps{n}", [P, 512], F32)) for n in range(4)]
        block = ctx.enter_context(nc.Block())

        @block.sync
        def _(sp):
            sp.dma_start(wba[:, :], w_ba).then_inc(sem("weights"), 16)
            sp.dma_start(dt[:, :], dt_bias.partition_broadcast(P)).then_inc(sem("weights"), 16)
            sp.dma_start(alog[:, :], a_log.partition_broadcast(P)).then_inc(sem("weights"), 16)
            sp.wait_ge(sem("pad_ready"), 1)
            sp.dma_start(h_t[:, :, 0:TAPS - 1], pad[:, :, :]).then_inc(sem("padded"), 16)
            with sp.Fori(0, NPAIR) as p:
                for q in range(2):
                    u = 2 * p + q
                    sp.wait_ge(sem("h_ready"), u)
                    for b in range(2):
                        sp.dma_start(xt[64 * b:64 * b + 64, :, :], pair_rows(x_in, p, b, q, NC))\
                          .then_inc(sem("x_loaded"), 16)
                    sp.wait_ge(sem("hT_ready"), u + 1)
                    for b in range(2):
                        sp.dma_start(h_t[:, bass.ds(2 * p + b, 1), TAPS - 1 + q * NC * CH:TAPS - 1 + (q + 1) * NC * CH],
                                     hT[:, :, b, :].unsqueeze(1)).then_inc(sem("stored"), 16)
                    sp.wait_ge(sem("gates_ready"), u + 1)
                    sp.dma_start(gates[bass.ds(p * NCH + q * NC, NC), :, :].rearrange("c p f -> p c f"),
                                 out[:, :, :, :].rearrange("p c a h -> p c (a h)")).then_inc(sem("stored"), 16)
            sp.wait_ge(sem("stored"), 16 * 3 * 2 * NPAIR)
            sp.wait_ge(sem("padded"), 16)

        @block.gpsimd
        def _(pool):
            make_identity(pool, ident, sem("ident"))
            link, _ = chain(pool, sem("setup"), 0)
            link(pool.memset(pad[:, :, :], 0.0))
            pool.sem_inc(sem("pad_ready"))
            link(pool.memset(mhalf[:, :], -0.5))
            for t in (upto, after, of_seq):
                link(pool.memset(t[:, :, :], 0.0))
                for b in range(2):
                    link(pool.memset(t[64 * b:64 * b + 64, b, :], 1.0))
            for b in range(2):
                own = slice(64 * b, 64 * b + 64)
                link(pool.affine_select(out=upto[own, b, :], in_=upto[own, b, :], compare_op=ALU.is_ge, fill=0.0,
                                        base=0, pattern=[[1, CH]], channel_multiplier=-1))
                link(pool.affine_select(out=after[own, b, :], in_=after[own, b, :], compare_op=ALU.is_gt, fill=0.0,
                                        base=0, pattern=[[-1, CH]], channel_multiplier=1))
            pool.sem_inc(sem("masks"))
            with pool.Fori(0, 2 * NPAIR) as u:
                pool.wait_ge(sem("var_ready"), u + 1)
                pool.tensor_tensor(rstd[:, :], ve[:, :], mhalf[:, :], ALU.pow).then_inc(sem("rstd_ready"), 1)

        @block.scalar
        def _(act):
            act.wait_ge(sem("alog_ready"), 1)
            act.activation(neg_a[:, :], alog[:, :], ACT.Exp).then_inc(sem("a_ready"), 1)
            with act.Fori(0, 2 * NPAIR) as u:
                act.wait_ge(sem("h_turned"), u + 1)
                act.wait_ge(sem("stored"), 48 * u)
                act.activation(hT[:, :, :, :].rearrange("p c b t -> p (c b t)"), ps[0][:, :], ACT.Copy)\
                   .then_inc(sem("hT_ready"), 1)
                act.wait_ge(sem("ba_ready"), u + 1)
                act.activation(eb[:, :, :], ps[1][:, 0:NC * 2 * DH].rearrange("p (c e) -> p c e", c=NC)[:, :, 0:DH],
                               ACT.Exp, scale=-1.0).then_inc(sem("eb_ready"), 1)
                act.wait_ge(sem("aa_ready"), u + 1)
                act.activation(ea[:, :, :], aa[:, :, :], ACT.Exp, scale=-1.0).then_inc(sem("act"), 1)
                act.wait_ge(sem("act"), 2 * u + 1)
                act.activation(la[:, :, :], ea[:, :, :], ACT.Ln, bias=1.0).then_inc(sem("act"), 1)
                act.wait_ge(sem("sums_ready"), u + 1)
                act.activation(out[:, :, 2, :], ps[2][:, 0:NC * DH].rearrange("p (c h) -> p c h", c=NC), ACT.Exp)
                act.activation(out[:, :, 3, :], ps[2][:, NC * DH:2 * NC * DH].rearrange("p (c h) -> p c h", c=NC),
                               ACT.Exp)
                for b in range(2):
                    last = act.activation(out[:, :, 4, b * DJ:(b + 1) * DJ],
                                          ps[3][:, b * NC * DJ:(b + 1) * NC * DJ].rearrange("p (c j) -> p c j", c=NC),
                                          ACT.Exp)
                last.then_inc(sem("gates_ready"), 1)

        @block.tensor
        def _(pe):
            pe.wait_ge(sem("ident"), 2)
            pe.wait_ge(sem("masks"), 1)
            pe.wait_ge(sem("weights"), 48)
            with pe.Fori(0, 2 * NPAIR) as u:
                pe.wait_ge(sem("h_ready"), u + 1)
                for c in range(NC):
                    last = pe.transpose(ps[0][:, c * P:(c + 1) * P], h[:, c, :], ident[:, :])
                last.then_inc(sem("h_turned"), 1)
                pe.wait_ge(sem("hT_ready"), u + 1)
                for c in range(NC):
                    last = pe.matmul(ps[1][:, c * 2 * DH:(c + 1) * 2 * DH], hT[:, c, :, :].rearrange("p b t -> p (b t)"),
                                     wba[:, :], start=True, stop=True)
                last.then_inc(sem("ba_ready"), 1)
                pe.wait_ge(sem("g_ready"), u + 1)
                flat = gg[:, :, :].rearrange("p c h -> p (c h)")
                pe.matmul(ps[2][:, 0:NC * DH], upto[:, :, :].rearrange("p b t -> p (b t)"), flat, start=True, stop=True)
                pe.matmul(ps[2][:, NC * DH:2 * NC * DH], after[:, :, :].rearrange("p b t -> p (b t)"), flat,
                          start=True, stop=True)
                for g in range(2):
                    for b in range(2):
                        last = pe.matmul(ps[3][64 * g:64 * g + 64, b * NC * DJ:(b + 1) * NC * DJ],
                                         of_seq[:, :, :].rearrange("p b t -> p t b")[:, :, b],
                                         gg[:, :, :].rearrange("p c (j g) -> p c j g", g=2)[:, :, :, g],
                                         start=True, stop=True)
                last.then_inc(sem("sums_ready"), 1)

        @block.vector
        def _(dve):
            dve.wait_ge(sem("weights"), 48)
            dve.tensor_scalar(alog[:, :], alog[:, :], -2.3, None, ALU.max).then_inc(sem("alog_ready"), 1)
            dve.wait_ge(sem("a_ready"), 1)
            dve.tensor_scalar(neg_a[:, :], neg_a[:, :], -1.0, None, ALU.mult).then_inc(sem("a_ready"), 1)
            dve.wait_ge(sem("a_ready"), 2)
            with dve.Fori(0, 2 * NPAIR) as u:
                link, links = chain(dve, sem("dve"), u * DVE_LINKS)
                dve.wait_ge(sem("x_loaded"), 32 * u + 32)
                for c in range(NC):
                    last = dve.bn_stats(st[:, c, :], xt[:, c, :])
                link(last)
                dve.sem_inc(sem("passed"))
                for c in range(NC):
                    last = dve.bn_aggr(mv[:, c, :], st[:, c, :])
                link(last)
                dve.tensor_scalar(ve[:, :], mv[:, :, 1], LN_EPS, None, ALU.add).then_inc(sem("var_ready"), 1)
                dve.wait_ge(sem("rstd_ready"), u + 1)
                for c in range(NC):
                    last = dve.tensor_scalar(h[:, c, :], xt[:, c, :], mv[:, c, 0:1], rstd[:, c:c + 1],
                                             ALU.subtract, ALU.mult)
                last.then_inc(sem("h_ready"), 1)
                dve.wait_ge(sem("ba_ready"), u + 1)
                dve.wait_ge(sem("eb_ready"), u + 1)
                link(dve.tensor_tensor(ad[:, :, :],
                                       ps[1][:, 0:NC * 2 * DH].rearrange("p (c e) -> p c e", c=NC)[:, :, DH:2 * DH],
                                       dt[:, :].unsqueeze(1).to_broadcast([P, NC, DH]), ALU.add))
                dve.scalar_tensor_tensor(out=aa[:, :, :], in0=ad[:, :, :], scalar=-1.0, in1=ad[:, :, :],
                                         op0=ALU.mult, op1=ALU.max).then_inc(sem("aa_ready"), 1)
                link(dve.tensor_scalar(eb[:, :, :], eb[:, :, :], 1.0, None, ALU.add))
                dve.wait_ge(sem("stored"), 48 * u)
                link(dve.reciprocal(out[:, :, 0, :], eb[:, :, :]))
                dve.wait_ge(sem("act"), 2 * u + 2)
                link(dve.scalar_tensor_tensor(out=gg[:, :, :], in0=ad[:, :, :], scalar=0.0, in1=la[:, :, :],
                                              op0=ALU.max, op1=ALU.add))
                link(dve.tensor_tensor(gg[:, :, :], gg[:, :, :], neg_a[:, :].unsqueeze(1).to_broadcast([P, NC, DH]),
                                       ALU.mult))
                dve.tensor_copy(out[:, :, 1, :], gg[:, :, :]).then_inc(sem("g_ready"), 1)
                assert links[0] == DVE_LINKS, links


def delta_phase(nc, x_in, x_out, h_t, gates, w_in, conv_t, norm_w, w_o):
    KV = DH * DHD
    LEVELS = (1, 2, 4, 8, 16, 32)
    NL = len(LEVELS)
    DVE_LINKS = 12
    L2_EPS, RMS_EPS = 1e-6, 1e-6
    GROUPS = range(2)
    with ExitStack() as ctx:
        def sb(name, shape):
            return ctx.enter_context(nc.sbuf_tensor("d_" + name, shape, F32))
        sem = semaphores(nc, ctx, "d")
        ident = sb("ident", [P, P])
        eye = sb("eye", [P, CH])
        later = sb("later", [P, 2, CH])
        upto = sb("upto", [P, CH])
        pair0 = sb("pair0", [P, CH])
        masks = sb("masks", [P, NL, CH // 2])
        powers = sb("powers", [P, 2, DH])
        mhalf = sb("mhalf", [P, DH])
        taps = sb("taps", [P, TAPS, 3 * KV])
        wz = sb("wz", [P, KV])
        wo = sb("wo", [P, DJ, D])
        nw = sb("nw", [P, DHD])
        hx = sb("hx", [P, 2, CH + TAPS - 1])
        hs = sb("hs", [P, TAPS, P])
        gin = sb("gin", [P, GATES])
        gt = sb("gt", [P, 5, DH])
        xt = sb("xt", [P, D])
        xo = sb("xo", [P, D])
        th = sb("th", [P, 2, 512])
        kqT = sb("kqT", [P, DJ, 2, P])
        ktok = sb("ktok", [P, KV])
        v = sb("v", [P, KV])
        z = sb("z", [P, KV])
        sq = sb("sq", [P, KV])
        n4 = sb("n4", [P, 2, DH])
        nr = sb("nr", [P, 2, DH])
        cc = sb("cc", [P, DH])
        wr = sb("wr", [P, DH])
        gU = sb("gU", [P, 2, DJ, CH])
        dd = sb("dd", [P, 2, DJ, CH])
        ddm = sb("ddm", [P, 2, DJ, CH])
        at = sb("at", [P, 2, DJ, CH])
        qk = sb("qk", [P, 2, DJ, CH])
        ti = sb("ti", [P, 2, DJ, CH])
        tt = sb("tt", [P, 2, DJ, CH])
        wl = sb("wl", [P, NL, 2 * DJ * CH])
        state = sb("state", [P, 2, DJ, DHD])
        r = sb("r", [P, KV])
        y = sb("y", [P, KV])
        oi = sb("oi", [P, KV])
        o = sb("o", [P, KV])
        ms = sb("ms", [P, DH])
        f = sb("f", [P, DH])
        f2 = sb("f2", [P, DH])
        pj = ctx.enter_context(nc.psum_tensor("d_pj", [P, 2, 512], F32))
        pg = [[ctx.enter_context(nc.psum_tensor(f"d_pg{g}{n}", [P, 512], F32)) for n in range(3)] for g in GROUPS]
        yw, sq2, yT = sq, r, kqT

        def of_group(t, g, n=DHD):
            return t[:, :].rearrange("p (j g d) -> p j g d", g=2, d=n)[:, :, g, :]

        def small(t, g):
            return t.rearrange("p (j g) -> p j g", g=2)[:, :, g].unsqueeze(2).to_broadcast([P, DJ, DHD])

        def w_level(l, g):
            return wl[:, l, g * DJ * CH:(g + 1) * DJ * CH]

        def halves(t, n, second=False):
            return t.rearrange("p (k m) -> p k m", m=2 * n)[:, :, n:2 * n] if second else \
                t.rearrange("p (k m) -> p k m", m=2 * n)[:, :, 0:n]

        def flat(t, g):
            return t[:, g, :, :].rearrange("p j c -> p (j c)")

        block = ctx.enter_context(nc.Block())
        WEIGHTS = 16 * (TAPS + 3)

        @block.sync
        def _(sp):
            for j in range(TAPS):
                sp.dma_start(taps[:, j, :], w_in[:, 0:3 * KV]).then_inc(sem("weights"), 16)
            sp.dma_start(wz[:, :], w_in[:, 3 * KV:4 * KV]).then_inc(sem("weights"), 16)
            sp.dma_start(wo[:, :, :], w_o.rearrange("(j m) d -> m j d", m=P)).then_inc(sem("weights"), 16)
            sp.dma_start(nw[:, :], norm_w.partition_broadcast(P)).then_inc(sem("weights"), 16)
            cwb = wl[:, :, :].rearrange("p l c -> p (l c)")
            for j in range(TAPS):
                sp.wait_ge(sem("tap_scaled"), j)
                sp.dma_start(cwb[:, 0:3 * KV], conv_t[j, :].partition_broadcast(P)).then_inc(sem("filter"), 16)
            with sp.Fori(0, NPAIR) as p:
                with sp.Fori(0, NCH) as c:
                    i = p * NCH + c
                    sp.wait_ge(sem("gates_taken"), i)
                    sp.dma_start(gin[:, :], gates[bass.ds(i, 1), :, :].rearrange("o p f -> p (o f)"))\
                      .then_inc(sem("gates_loaded"), 16)
                    sp.wait_ge(sem("shifted"), i)
                    for b in range(2):
                        sp.dma_start(hx[:, b, :], h_t[:, bass.ds(2 * p + b, 1), bass.ds(c * CH, CH + TAPS - 1)]
                                     .rearrange("d o t -> d (o t)")).then_inc(sem("h_loaded"), 16)
                    sp.wait_ge(sem("x_used"), i)
                    for b in range(2):
                        sp.dma_start(xt[64 * b:64 * b + 64, :], x_in[bass.ds(p * (2 * SEQ) + c * CH + b * SEQ, CH), :])\
                          .then_inc(sem("x_loaded"), 16)
                    sp.wait_ge(sem("x_used"), i + 1)
                    for b in range(2):
                        sp.dma_start(x_out[bass.ds(p * (2 * SEQ) + c * CH + b * SEQ, CH), :], xo[64 * b:64 * b + 64, :])\
                          .then_inc(sem("stored"), 16)
            sp.wait_ge(sem("stored"), 32 * NSTEP)

        @block.gpsimd
        def _(pool):
            make_identity(pool, ident, sem("ident"))
            link, _ = chain(pool, sem("setup"), 0)
            link(pool.memset(mhalf[:, :], -0.5))
            link(pool.memset(powers[:, 0, :], 0.5))
            link(pool.memset(powers[:, 1, :], -0.5))
            for t in (eye, pair0):
                link(pool.memset(t[:, :], 0.0))
            link(pool.memset(later[:, :, :], 0.0))
            link(pool.memset(upto[:, :], 1.0))
            link(pool.memset(masks[:, :, :], 1.0))
            for b in range(2):
                own = slice(64 * b, 64 * b + 64)
                link(pool.memset(later[own, b, :], 1.0))
                link(pool.affine_select(out=later[own, b, :], in_=later[own, b, :], compare_op=ALU.is_gt, fill=0.0,
                                        base=0, pattern=[[-1, CH]], channel_multiplier=1))
                link(pool.affine_select(out=upto[own, :], in_=upto[own, :], compare_op=ALU.is_ge, fill=0.0,
                                        base=0, pattern=[[1, CH]], channel_multiplier=-1))
                link(pool.affine_select(out=eye[own, :], in_=eye[own, :], compare_op=ALU.not_equal, fill=1.0,
                                        base=0, pattern=[[-1, CH]], channel_multiplier=1))
                odd = pair0[own, :].rearrange("p (k m) -> p k m", m=2)[:, :, 1]
                link(pool.affine_select(out=odd, in_=odd, compare_op=ALU.not_equal, fill=1.0,
                                        base=0, pattern=[[-2, CH // 2]], channel_multiplier=1))
                for l, n in enumerate(LEVELS):
                    m = masks[own, l, :].rearrange("p (k i) -> p k i", i=n)
                    link(pool.affine_select(out=m, in_=m, compare_op=ALU.is_ge, fill=0.0, base=-n,
                                            pattern=[[-2 * n, CH // 2 // n], [0, n]], channel_multiplier=1))
                    link(pool.affine_select(out=m, in_=m, compare_op=ALU.is_ge, fill=0.0, base=2 * n - 1,
                                            pattern=[[2 * n, CH // 2 // n], [0, n]], channel_multiplier=-1))
            pool.sem_inc(sem("masks"))
            pool.wait_ge(sem("nw_halved"), 1)
            with pool.Fori(0, NPAIR) as p:
                with pool.Fori(0, NCH) as c:
                    i = p * NCH + c
                    pool.wait_ge(sem("gates_taken"), i + 1)
                    for g in GROUPS:
                        last = pool.tensor_tensor(
                            gU[:, g, :, :], gt[:, 1, :].rearrange("p (j g) -> p j g", g=2)[:, :, g].unsqueeze(2)
                            .to_broadcast([P, DJ, CH]), upto[:, :].unsqueeze(1).to_broadcast([P, DJ, CH]), ALU.mult)
                    last.then_inc(sem("gU_ready"), 1)
                    pool.wait_ge(sem("n4_ready"), i + 1)
                    pool.tensor_tensor(nr[:, :, :], n4[:, :, :], powers[:, :, :], ALU.pow).then_inc(sem("nr_ready"), 1)
                    for g in GROUPS:
                        pool.wait_ge(sem("dd_ready"), 2 * i + g + 1)
                        pool.tensor_tensor(ddm[:, g, :, :], dd[:, g, :, :],
                                           upto[:, :].unsqueeze(1).to_broadcast([P, DJ, CH]), ALU.mult)\
                            .then_inc(sem("ddm_ready"), 1)
                    for g in GROUPS:
                        pool.wait_ge(sem("at_ready"), 2 * i + g + 1)
                        pool.tensor_tensor(tt[:, g, :, :], at[:, g, :, :],
                                           pair0[:, :].unsqueeze(1).to_broadcast([P, DJ, CH]), ALU.mult)\
                            .then_inc(sem("tt_part"), 1)
                        pool.wait_ge(sem("tt_part"), 2 * i + g + 1)
                        pool.tensor_tensor(tt[:, g, :, :], eye[:, :].unsqueeze(1).to_broadcast([P, DJ, CH]),
                                           tt[:, g, :, :], ALU.subtract).then_inc(sem("tt0_ready"), 1)
                    pool.wait_ge(sem("proj_used"), 8 * i + 8)
                    pool.tensor_tensor(z[:, :].rearrange("p (h d) -> p h d", d=DHD),
                                       z[:, :].rearrange("p (h d) -> p h d", d=DHD),
                                       nw[:, :].unsqueeze(1).to_broadcast([P, DH, DHD]), ALU.mult)\
                        .then_inc(sem("z_ready"), 1)
                    for g in GROUPS:
                        pool.wait_ge(sem("y_ready"), 2 * i + g + 1)
                        pool.tensor_tensor(of_group(yw, g), of_group(y, g), small(wr[:, :], g), ALU.mult)\
                            .then_inc(sem("yw_ready"), 1)
                    pool.wait_ge(sem("ms_ready"), i + 1)
                    pool.tensor_tensor(f[:, :], ms[:, :], mhalf[:, :], ALU.pow).then_inc(sem("f_ready"), 1)

        @block.scalar
        def _(act):
            with act.Fori(0, NPAIR) as p:
                with act.Fori(0, NCH) as c:
                    i = p * NCH + c
                    act.wait_ge(sem("h_loaded"), 32 * i + 32)
                    for t in range(TAPS):
                        last = act.activation(hs[:, t, :].rearrange("p (b t) -> p b t", b=2), hx[:, :, t:t + CH],
                                              ACT.Copy)
                    last.then_inc(sem("shifted"), 1)
                    for n in range(8):
                        act.wait_ge(sem("projected"), 8 * i + n + 1)
                        if n >= 2:
                            act.wait_ge(sem("proj_used"), 8 * i + n - 1)
                        act.activation(th[:, n % 2, :], pj[:, n % 2, :], ACT.Tanh, scale=0.5)\
                           .then_inc(sem("tanh"), 1)
                    for n in range(2):
                        act.wait_ge(sem("kq_turned"), 2 * i + n + 1)
                        turned = pj[:, :, :].rearrange("p a c -> p (a c)")
                        if n == 0:
                            act.activation(ktok[:, :], turned, ACT.Copy)
                            act.activation(sq[:, :], turned, ACT.Square).then_inc(sem("squared"), 1)
                        else:
                            act.wait_ge(sem("k_summed"), i + 1)
                            act.activation(sq[:, :], turned, ACT.Square).then_inc(sem("squared"), 1)
                    act.wait_ge(sem("exponents"), i + 1)
                    for g in GROUPS:
                        act.activation(flat(dd, g), pj[:, g, :], ACT.Exp).then_inc(sem("decays"), 1)
                    for g in GROUPS:
                        act.wait_ge(sem("solved"), 2 * i + g + 1)
                        act.activation(of_group(y, g), pg[g][1][:, :].rearrange("p (j d) -> p j d", j=DJ), ACT.Copy)\
                           .then_inc(sem("y_ready"), 1)
                    act.wait_ge(sem("o_ready"), i + 1)
                    act.activation(sq2[:, :], o[:, :], ACT.Square).then_inc(sem("o_squared"), 1)
                    for n in range(2):
                        act.wait_ge(sem("o_turned"), 2 * i + n + 1)
                        act.activation(yT[:, 4 * n:4 * n + 4, 0, :],
                                       pg[n][0][:, :].rearrange("p (j t) -> p j t", j=4), ACT.Copy)\
                           .then_inc(sem("yT_ready"), 1)

        @block.tensor
        def _(pe):
            def hold(s, value):
                pe.wait_ge(s, value)
                pe.sem_inc(sem("passed"))

            def each(g, product):
                for j in range(DJ):
                    for b in range(2):
                        last = product(j, b, slice(64 * b, 64 * b + 64))
                return last

            pe.wait_ge(sem("ident"), 2)
            pe.wait_ge(sem("masks"), 1)
            pe.wait_ge(sem("zeroed"), 1)
            with pe.Fori(0, NPAIR) as p:
                with pe.Fori(0, NCH) as c:
                    i = p * NCH + c
                    pe.wait_ge(sem("shifted"), i + 1)
                    for n in range(8):
                        if n >= 2:
                            pe.wait_ge(sem("proj_used"), 8 * i + n - 1)
                        if n < 4:
                            for jj in range(4):
                                for t in range(TAPS):
                                    ch = n * 512 + jj * P
                                    last = pe.matmul(pj[:, n % 2, jj * P:(jj + 1) * P], taps[:, t, ch:ch + P],
                                                     hs[:, t, :], start=(t == 0), stop=(t == TAPS - 1))
                        elif n < 6:
                            for t in range(TAPS):
                                ch = n * 512
                                last = pe.matmul(pj[:, n % 2, :], hs[:, t, :], taps[:, t, ch:ch + 512],
                                                 start=(t == 0), stop=(t == TAPS - 1))
                        else:
                            last = pe.matmul(pj[:, n % 2, :], hs[:, TAPS - 1, :],
                                             wz[:, (n - 6) * 512:(n - 5) * 512], start=True, stop=True)
                        last.then_inc(sem("projected"), 1)
                    pe.wait_ge(sem("proj_used"), 8 * i + 8)
                    for n in range(2):
                        if n:
                            pe.wait_ge(sem("squared"), 2 * i + 1)
                        for j in range(DJ):
                            last = pe.transpose(pj[:, j // 4, (j % 4) * P:(j % 4 + 1) * P], kqT[:, j, n, :], ident[:, :])
                        last.then_inc(sem("kq_turned"), 1)
                    pe.wait_ge(sem("gU_ready"), i + 1)
                    pe.wait_ge(sem("squared"), 2 * i + 2)
                    for g in GROUPS:
                        last = pe.matmul(pj[:, g, :], later[:, :, :].rearrange("p b s -> p (b s)"), flat(gU, g),
                                         start=True, stop=True)
                    last.then_inc(sem("exponents"), 1)
                    for g in GROUPS:
                        rows = slice(64 * g, 64 * g + 64)
                        last = each(g, lambda j, b, own: pe.matmul(
                            pg[g][j // 4][own, (j % 4) * P:(j % 4 + 1) * P], kqT[rows, j, 0, own], kqT[rows, j, :, own],
                            start=True, stop=True))
                        last.then_inc(sem("kkq"), 1)
                    hold(sem("state_ready"), 9 * p + c + 1)
                    for g in GROUPS:
                        rows = slice(64 * g, 64 * g + 64)
                        last = each(g, lambda j, b, own: pe.matmul(
                            pg[g][2][own, j * DHD:(j + 1) * DHD], kqT[rows, j, 0, own], state[rows, b, j, :],
                            start=True, stop=True))
                        last.then_inc(sem("ks"), 1)
                    hold(sem("decays"), 2 * i + 2)
                    for g in GROUPS:
                        rows = slice(64 * g, 64 * g + 64)
                        last = each(g, lambda j, b, own: pe.matmul(
                            pj[own, g, j * DHD:(j + 1) * DHD], kqT[rows, j, 1, own], state[rows, b, j, :],
                            start=True, stop=True))
                        last.then_inc(sem("qs"), 1)
                    for l, n in enumerate(LEVELS):
                        for g in GROUPS:
                            if l == 0:
                                hold(sem("qk_read"), 2 * i + g + 1)
                            else:
                                hold(sem("t_ready"), (NL - 1) * 2 * i + 2 * (l - 1) + g + 1)
                            last = each(g, lambda j, b, own: pe.matmul(
                                pg[g][0][own, j * 32:(j + 1) * 32], at[own, g, j, :],
                                halves(eye[own, :] if l == 0 else ti[own, g, j, :], n), start=True, stop=True))
                            last.then_inc(sem("w_sum"), 1)
                        if l == 0:
                            continue
                        for g in GROUPS:
                            w = w_level(l, g).rearrange("p (j c) -> p j c", j=DJ)
                            if l == 1:
                                hold(sem("tt0_ready"), 2 * i + g + 1)
                            else:
                                hold(sem("tt_ready"), (NL - 1) * 2 * i + 2 * (l - 2) + g + 1)
                            hold(sem("w_ready"), NL * 2 * i + 2 * l + g + 1)
                            if l < NL - 1:
                                last = each(g, lambda j, b, own: pe.matmul(
                                    pg[g][1][own, j * 32:(j + 1) * 32], tt[own, g, j, :], halves(w[own, j, :], n),
                                    start=True, stop=True))
                                last.then_inc(sem("tw"), 1)
                            if l == 1:
                                hold(sem("r_ready"), 2 * i + g + 1)
                            last = each(g, lambda j, b, own: pe.matmul(
                                pg[g][2][own, j * 32:(j + 1) * 32], w[own, j, :],
                                halves(tt[own, g, j, :], n, second=True), start=True, stop=True))
                            last.then_inc(sem("ttw"), 1)
                    for g in GROUPS:
                        hold(sem("tt_ready"), (NL - 1) * 2 * i + 2 * (NL - 2) + g + 1)
                        last = each(g, lambda j, b, own: pe.matmul(
                            pg[g][1][own, j * DHD:(j + 1) * DHD], tt[own, g, j, :],
                            r[own, (2 * j + g) * DHD:(2 * j + g + 1) * DHD], start=True, stop=True))
                        last.then_inc(sem("solved"), 1)
                    for g in GROUPS:
                        hold(sem("y_ready"), 2 * i + g + 1)
                        last = each(g, lambda j, b, own: pe.matmul(
                            pg[g][2][own, j * DHD:(j + 1) * DHD], qk[own, g, j, :],
                            y[own, (2 * j + g) * DHD:(2 * j + g + 1) * DHD], start=True, stop=True))
                        last.then_inc(sem("o_sum"), 1)
                    for g in GROUPS:
                        hold(sem("yw_ready"), 2 * i + g + 1)
                        if g == 0:
                            hold(sem("oi_ready"), 2 * i + 2)
                        rows = slice(64 * g, 64 * g + 64)
                        last = each(g, lambda j, b, own: pe.matmul(
                            pj[rows, b, j * DHD:(j + 1) * DHD], ktok[own, (2 * j + g) * DHD:(2 * j + g + 1) * DHD],
                            yw[own, (2 * j + g) * DHD:(2 * j + g + 1) * DHD], start=True, stop=True))
                    last.then_inc(sem("update"), 1)
                    pe.wait_ge(sem("on_ready"), i + 1)
                    for n in range(2):
                        for jj in range(4):
                            j = 4 * n + jj
                            last = pe.transpose(pg[n][0][:, jj * P:(jj + 1) * P], o[:, j * P:(j + 1) * P], ident[:, :])
                        last.then_inc(sem("o_turned"), 1)
                    pe.wait_ge(sem("yT_ready"), 2 * i + 2)
                    for j in range(DJ):
                        last = pe.matmul(pg[0][1][:, 0:D], yT[:, j, 0, :], wo[:, j, :], start=(j == 0), stop=(j == DJ - 1))
                    last.then_inc(sem("out_ready"), 1)
                    pe.wait_ge(sem("state_ready"), 9 * p + c + 2)
                    pe.wait_ge(sem("x_used"), i + 1)

        @block.vector
        def _(dve):
            cwb = wl[:, :, :].rearrange("p l c -> p (l c)")
            dve.wait_ge(sem("weights"), WEIGHTS)
            for j in range(TAPS):
                dve.wait_ge(sem("filter"), 16 * j + 16)
                dve.tensor_tensor(taps[:, j, :], taps[:, j, :], cwb[:, 0:3 * KV], ALU.mult).then_inc(sem("tap_scaled"), 1)
            dve.tensor_scalar(nw[:, :], nw[:, :], 0.5, None, ALU.mult).then_inc(sem("nw_halved"), 1)
            dve.wait_ge(sem("tap_scaled"), TAPS)
            dve.memset(cwb, 0.0).then_inc(sem("zeroed"), 1)
            dve.wait_ge(sem("zeroed"), 1)
            dve.wait_ge(sem("masks"), 1)
            with dve.Fori(0, NPAIR) as p:
                dve.memset(state[:, :, :, :], 0.0).then_inc(sem("state_ready"), 1)
                with dve.Fori(0, NCH) as c:
                    i = p * NCH + c
                    link, links = chain(dve, sem("dve"), i * DVE_LINKS)
                    dve.wait_ge(sem("gates_loaded"), 16 * i + 16)
                    dve.tensor_copy(gt[:, :, :].rearrange("p a h -> p (a h)"), gin[:, :]).then_inc(sem("gates_taken"), 1)
                    for n in range(8):
                        dve.wait_ge(sem("tanh"), 8 * i + n + 1)
                        if n < 4:
                            part = 1 - n // 2
                            to = kqT[:, 4 * (n % 2):4 * (n % 2) + 4, part, :]
                            own = lambda t: t.rearrange("p (j t) -> p j t", j=4)
                        else:
                            to = (v if n < 6 else z)[:, (n % 2) * 512:(n % 2 + 1) * 512]
                            own = lambda t: t
                        dve.scalar_tensor_tensor(out=to, in0=own(th[:, n % 2, :]), scalar=1.0, in1=own(pj[:, n % 2, :]),
                                                 op0=ALU.add, op1=ALU.mult).then_inc(sem("proj_used"), 1)
                    for part in range(2):
                        dve.wait_ge(sem("squared"), 2 * i + part + 1)
                        ins = dve.tensor_reduce(n4[:, part, :], sq[:, :].rearrange("p (h d) -> p h d", d=DHD), AX_X, ALU.add)
                        if part == 0:
                            ins.then_inc(sem("k_summed"), 1)
                        else:
                            link(ins)
                    dve.tensor_scalar(n4[:, :, :], n4[:, :, :], 0.25, L2_EPS, ALU.mult, ALU.add)\
                       .then_inc(sem("n4_ready"), 1)
                    dve.wait_ge(sem("n4_ready"), i + 1)
                    link(dve.reciprocal(cc[:, :], n4[:, 0, :]))
                    link(dve.scalar_tensor_tensor(out=cc[:, :], in0=cc[:, :], scalar=0.25, in1=gt[:, 0, :],
                                                  op0=ALU.mult, op1=ALU.mult))
                    dve.tensor_tensor(wr[:, :], cc[:, :], gt[:, 3, :], ALU.mult)
                    for g in GROUPS:
                        dve.wait_ge(sem("decays"), 2 * i + g + 1)
                        dve.tensor_tensor(dd[:, g, :, :], dd[:, g, :, :], small(cc[:, :], g), ALU.mult)\
                           .then_inc(sem("dd_ready"), 1)
                    for g in GROUPS:
                        dve.wait_ge(sem("kkq"), 2 * i + g + 1)
                        dve.wait_ge(sem("dd_ready"), 2 * i + g + 1)
                        for m in range(2):
                            last = dve.tensor_tensor(at[:, g, 4 * m:4 * m + 4, :], dd[:, g, 4 * m:4 * m + 4, :],
                                                     pg[g][m][:, :].rearrange("p (j a t) -> p j a t", j=4, a=2)[:, :, 0, :],
                                                     ALU.mult)
                        last.then_inc(sem("at_ready"), 1)
                        dve.wait_ge(sem("ddm_ready"), 2 * i + g + 1)
                        for m in range(2):
                            last = dve.tensor_tensor(qk[:, g, 4 * m:4 * m + 4, :], ddm[:, g, 4 * m:4 * m + 4, :],
                                                     pg[g][m][:, :].rearrange("p (j a t) -> p j a t", j=4, a=2)[:, :, 1, :],
                                                     ALU.mult)
                        last.then_inc(sem("qk_read"), 1)
                    dve.wait_ge(sem("nr_ready"), i + 1)
                    heads = lambda t: t[:, :].rearrange("p (h d) -> p h d", d=DHD)
                    link(dve.tensor_tensor(heads(v), heads(v),
                                           nr[:, 0, :].unsqueeze(2).to_broadcast([P, DH, DHD]), ALU.mult))
                    for g in GROUPS:
                        dve.wait_ge(sem("ks"), 2 * i + g + 1)
                        link(dve.tensor_tensor(of_group(r, g), pg[g][2][:, :].rearrange("p (j d) -> p j d", j=DJ),
                                               small(gt[:, 2, :], g), ALU.mult))
                        dve.tensor_tensor(of_group(r, g), of_group(v, g), of_group(r, g), ALU.subtract)\
                           .then_inc(sem("r_ready"), 1)
                    for g in GROUPS:
                        dve.wait_ge(sem("qs"), 2 * i + g + 1)
                        dve.tensor_tensor(of_group(oi, g), pj[:, g, :].rearrange("p (j d) -> p j d", j=DJ),
                                          small(gt[:, 2, :], g), ALU.mult).then_inc(sem("oi_ready"), 1)
                    dve.wait_ge(sem("oi_ready"), 2 * i + 2)
                    link(dve.tensor_tensor(state[:, :, :, :].rearrange("p b j d -> p (b j) d"),
                                           state[:, :, :, :].rearrange("p b j d -> p (b j) d"),
                                           gt[:, 4, :].unsqueeze(2).to_broadcast([P, 2 * DJ, DHD]), ALU.mult))
                    for l, n in enumerate(LEVELS):
                        for g in GROUPS:
                            dve.wait_ge(sem("w_sum"), NL * 2 * i + 2 * l + g + 1)
                            dve.tensor_tensor(
                                w_level(l, g).rearrange("p (j k m) -> p j (k m)", j=DJ, m=2 * n)
                                .rearrange("p j (k m) -> p j k m", m=2 * n)[:, :, :, 0:n],
                                pg[g][0][:, 0:256].rearrange("p (j k i) -> p j k i", j=DJ, i=n),
                                masks[:, l, :].rearrange("p (k i) -> p k i", i=n).unsqueeze(1)
                                .to_broadcast([P, DJ, CH // 2 // n, n]), ALU.mult).then_inc(sem("w_ready"), 1)
                        for g in GROUPS:
                            if l == 0:
                                dve.wait_ge(sem("w_ready"), NL * 2 * i + g + 1)
                                dve.tensor_tensor(ti[:, g, :, :], eye[:, :].unsqueeze(1).to_broadcast([P, DJ, CH]),
                                                  w_level(l, g).rearrange("p (j c) -> p j c", j=DJ), ALU.subtract)\
                                   .then_inc(sem("t_ready"), 1)
                                continue
                            if l < NL - 1:
                                dve.wait_ge(sem("tw"), (NL - 2) * 2 * i + 2 * (l - 1) + g + 1)
                                if l == 1:
                                    dve.wait_ge(sem("t_ready"), (NL - 1) * 2 * i + g + 1)
                                to = halves(flat(ti, g), n)
                                dve.tensor_tensor(to, to, pg[g][1][:, 0:256].rearrange("p (k i) -> p k i", i=n),
                                                  ALU.subtract).then_inc(sem("t_ready"), 1)
                            dve.wait_ge(sem("ttw"), (NL - 1) * 2 * i + 2 * (l - 1) + g + 1)
                            to = halves(flat(tt, g), n, second=True)
                            dve.tensor_tensor(to, to, pg[g][2][:, 0:256].rearrange("p (k i) -> p k i", i=n),
                                              ALU.subtract).then_inc(sem("tt_ready"), 1)
                    for g in GROUPS:
                        dve.wait_ge(sem("o_sum"), 2 * i + g + 1)
                        last = dve.tensor_tensor(of_group(o, g), of_group(oi, g),
                                                 pg[g][2][:, :].rearrange("p (j d) -> p j d", j=DJ), ALU.add)
                    last.then_inc(sem("o_ready"), 1)
                    dve.wait_ge(sem("update"), i + 1)
                    dve.tensor_tensor(state[:, :, :, :].rearrange("p b j d -> p (b j d)"),
                                      state[:, :, :, :].rearrange("p b j d -> p (b j d)"),
                                      pj[:, :, :].rearrange("p b c -> p (b c)"), ALU.add).then_inc(sem("state_ready"), 1)
                    dve.wait_ge(sem("o_squared"), i + 1)
                    link(dve.tensor_reduce(ms[:, :], heads(sq2), AX_X, ALU.add))
                    link(dve.tensor_tensor(f2[:, :], nr[:, 1, :], nr[:, 1, :], ALU.mult))
                    link(dve.tensor_tensor(ms[:, :], ms[:, :], f2[:, :], ALU.mult))
                    dve.tensor_scalar(ms[:, :], ms[:, :], 1.0 / (256 * DHD), RMS_EPS, ALU.mult, ALU.add)\
                       .then_inc(sem("ms_ready"), 1)
                    dve.wait_ge(sem("f_ready"), i + 1)
                    link(dve.scalar_tensor_tensor(out=f2[:, :], in0=nr[:, 1, :], scalar=1.0 / 16, in1=f[:, :],
                                                  op0=ALU.mult, op1=ALU.mult))
                    link(dve.tensor_tensor(heads(o), heads(o), f2[:, :].unsqueeze(2).to_broadcast([P, DH, DHD]), ALU.mult))
                    dve.wait_ge(sem("z_ready"), i + 1)
                    dve.tensor_tensor(o[:, :], o[:, :], z[:, :], ALU.mult).then_inc(sem("on_ready"), 1)
                    dve.wait_ge(sem("out_ready"), i + 1)
                    dve.wait_ge(sem("x_loaded"), 32 * i + 32)
                    dve.wait_ge(sem("stored"), 32 * i)
                    dve.tensor_tensor(xo[:, :], xt[:, :], pg[0][1][:, 0:D], ALU.add).then_inc(sem("x_used"), 1)
                    assert links[0] == DVE_LINKS, links


AH, AHD = 4, 32
AN = P // NSEQ
NE, FF = 8, 512
CAP = NSEQ * SEQ // NE


def attention_rows(x, u, c):
    return x.rearrange("(l n) d -> l n d", l=NSEQ)[:, bass.ds(u * (4 * AN) + c * AN, AN), :]


def attention_phase(nc, x_in, y_out, route, in_t, in_b, in_b_cols, out_t, out_b, ln_g, ln_b, wg):
    NC = 4
    DVE_LINKS = 18
    OFF = -1e30
    with ExitStack() as ctx:
        def sb(name, shape):
            return ctx.enter_context(nc.sbuf_tensor("e_" + name, shape, F32))
        sem = semaphores(nc, ctx, "e")
        ident = sb("ident", [P, P])
        same = sb("same", [P, NSEQ, AN])
        mhalf = sb("mhalf", [P, NC])
        order = sb("order", [P, NE])
        win = sb("win", [P, 3 * D])
        wout = sb("wout", [P, D])
        wgs = sb("wgs", [P, NE])
        bqk = sb("bqk", [P, 3])
        bv = sb("bv", [P, D])
        ob = sb("ob", [P, D])
        lg = sb("lg", [P, D])
        lb = sb("lb", [P, D])
        xt = sb("xt", [P, NC, D])
        h = sb("h", [P, NC, D])
        hT = sb("hT", [P, 512])
        qT = sb("qT", [P, 512])
        kT = sb("kT", [P, 512])
        v = sb("v", [P, NC, D])
        sc = sb("sc", [P, AH, NC, P])
        mx = sb("mx", [P, AH * NC])
        pr = sb("pr", [P, AH, NC, P])
        den = sb("den", [P, AH * NC])
        rden = sb("rden", [P, AH, NC])
        prT = sb("prT", [P, AH, NC, P])
        on = sb("on", [P, NC, D])
        oT = sb("oT", [P, 512])
        y = sb("y", [P, NC, D])
        yT = sb("yT", [P, 512])
        st = sb("st", [P, NC, 6])
        mv = sb("mv", [P, NC, 2])
        ve = sb("ve", [P, NC])
        rstd = sb("rstd", [P, NC])
        lm = sb("lm", [P, NC])
        ld = sb("ld", [P, NC, NE])
        le = sb("le", [P, NC, NE])
        ls = sb("ls", [P, NC])
        lr = sb("lr", [P, NC])
        hit = sb("hit", [P, NC, NE])
        first = sb("first", [P, NC])
        rt = sb("rt", [P, NC, 2, NE])
        ps = [ctx.enter_context(nc.psum_tensor(f"e_ps{n}", [P, 512], F32)) for n in range(8)]
        block = ctx.enter_context(nc.Block())
        tiles = lambda t: t[:, :].rearrange("p (c d) -> p c d", c=NC)

        @block.sync
        def _(sp):
            for to, of in ((win[:, :], in_t), (wout[:, :], out_t), (wgs[:, :], wg),
                           (bqk[:, :], in_b_cols),
                           (bv[:, :], in_b[2 * D:3 * D].partition_broadcast(P)), (ob[:, :], out_b.partition_broadcast(P)),
                           (lg[:, :], ln_g.partition_broadcast(P)), (lb[:, :], ln_b.partition_broadcast(P))):
                sp.dma_start(to, of).then_inc(sem("weights"), 16)
            with sp.Fori(0, NT // NC) as u:
                sp.wait_ge(sem("h_ready"), u)
                for c in range(NC):
                    sp.dma_start(xt[:, c, :], attention_rows(x_in, u, c)).then_inc(sem("x_loaded"), 16)
                sp.wait_ge(sem("y_ready"), u + 1)
                for c in range(NC):
                    sp.dma_start(attention_rows(y_out, u, c), y[:, c, :]).then_inc(sem("stored"), 16)
                sp.wait_ge(sem("route_ready"), u + 1)
                for c in range(NC):
                    sp.dma_start(attention_rows(route, u, c), rt[:, c, :, :].rearrange("p a e -> p (a e)"))\
                      .then_inc(sem("stored"), 16)
            sp.wait_ge(sem("stored"), 16 * 2 * NT)

        @block.gpsimd
        def _(pool):
            make_identity(pool, ident, sem("ident"))
            pool.memset(mhalf[:, :], -0.5).then_inc(sem("ones"), 1)
            for e in range(NE):
                last = pool.memset(order[:, e:e + 1], float(NE - e))
            last.then_inc(sem("ones"), 1)
            pool.memset(same[:, :, :], OFF).then_inc(sem("same"), 1)
            for shift in range(1 - NSEQ, NSEQ):
                pool.wait_ge(sem("same"), shift + NSEQ)
                pool.affine_select(out=same[:, :, :], in_=same[:, :, :], compare_op=ALU.not_equal, fill=0.0,
                                   base=-AN * shift, pattern=[[-AN, NSEQ], [-1, AN]], channel_multiplier=1)\
                    .then_inc(sem("same"), 1)
            with pool.Fori(0, NT // NC) as u:
                pool.wait_ge(sem("var_ready"), 2 * u + 1)
                pool.tensor_tensor(rstd[:, :], ve[:, :], mhalf[:, :], ALU.pow).then_inc(sem("rstd_ready"), 1)
                pool.wait_ge(sem("var_ready"), 2 * u + 2)
                pool.tensor_tensor(rstd[:, :], ve[:, :], mhalf[:, :], ALU.pow).then_inc(sem("rstd_ready"), 1)

        @block.scalar
        def _(act):
            act.wait_ge(sem("weights"), 16 * 8)
            with act.Fori(0, NT // NC) as u:
                act.wait_ge(sem("h_turned"), u + 1)
                act.activation(hT[:, :], ps[0][:, :], ACT.Copy).then_inc(sem("hT_ready"), 1)
                act.wait_ge(sem("qk_ready"), u + 1)
                act.activation(qT[:, :], ps[1][:, :], ACT.Identity, bias=bqk[:, 0:1])
                act.activation(kT[:, :], ps[2][:, :], ACT.Identity, bias=bqk[:, 1:2]).then_inc(sem("qkT_ready"), 1)
                act.wait_ge(sem("max_ready"), u + 1)
                for j in range(AH):
                    for c in range(NC):
                        n = j * NC + c
                        last = act.activation(pr[:, j, c, :], sc[:, j, c, :], ACT.Exp, bias=mx[:, n:n + 1],
                                              accum_out=den[:, n:n + 1])
                    last.then_inc(sem("probs"), 1)
                for j in range(AH):
                    act.wait_ge(sem("probs_turned"), AH * u + j + 1)
                    act.activation(prT[:, j, :, :].rearrange("p c t -> p (c t)"), ps[4 + j][:, :], ACT.Copy)\
                       .then_inc(sem("prT_ready"), 1)
                act.wait_ge(sem("o_turned"), u + 1)
                act.activation(oT[:, :], ps[0][:, :], ACT.Copy).then_inc(sem("oT_ready"), 1)
                act.wait_ge(sem("y_turned"), u + 1)
                act.activation(yT[:, :], ps[0][:, :], ACT.Copy).then_inc(sem("yT_ready"), 1)
                act.wait_ge(sem("ld_ready"), u + 1)
                act.activation(le[:, :, :], ld[:, :, :], ACT.Exp).then_inc(sem("le_ready"), 1)

        @block.tensor
        def _(pe):
            pe.wait_ge(sem("ident"), 2)
            pe.wait_ge(sem("weights"), 16 * 8)
            with pe.Fori(0, NT // NC) as u:
                def turn(of, done):
                    for c in range(NC):
                        last = pe.transpose(ps[0][:, c * P:(c + 1) * P], of[:, c, :], ident[:, :])
                    last.then_inc(done, 1)

                pe.wait_ge(sem("h_ready"), u + 1)
                turn(h, sem("h_turned"))
                pe.wait_ge(sem("hT_ready"), u + 1)
                for n in range(2):
                    last = pe.matmul(ps[1 + n][:, :], win[:, n * D:(n + 1) * D], hT[:, :], start=True, stop=True)
                last.then_inc(sem("qk_ready"), 1)
                for c in range(NC):
                    last = pe.matmul(ps[3][:, c * P:(c + 1) * P], hT[:, c * P:(c + 1) * P], win[:, 2 * D:3 * D],
                                     start=True, stop=True)
                last.then_inc(sem("v_ready"), 1)
                pe.wait_ge(sem("qkT_ready"), u + 1)
                for j in range(AH):
                    rows = slice(AHD * j, AHD * j + AHD)
                    for c in range(NC):
                        here = slice(c * P, (c + 1) * P)
                        last = pe.matmul(ps[4 + j][:, here], qT[rows, here], kT[rows, here], start=True, stop=True)
                    last.then_inc(sem("scores"), 1)
                for j in range(AH):
                    pe.wait_ge(sem("probs"), AH * u + j + 1)
                    for c in range(NC):
                        last = pe.transpose(ps[4 + j][:, c * P:(c + 1) * P], pr[:, j, c, :], ident[:, :])
                    last.then_inc(sem("probs_turned"), 1)
                pe.wait_ge(sem("v_used"), u + 1)
                for j in range(AH):
                    pe.wait_ge(sem("prT_ready"), AH * u + j + 1)
                    for c in range(NC):
                        cols = slice(c * P + AHD * j, c * P + AHD * j + AHD)
                        last = pe.matmul(ps[1][:, cols], prT[:, j, c, :], v[:, c, AHD * j:AHD * j + AHD],
                                         start=True, stop=True)
                last.then_inc(sem("o_ready"), 1)
                pe.wait_ge(sem("on_ready"), u + 1)
                turn(on, sem("o_turned"))
                pe.wait_ge(sem("oT_ready"), u + 1)
                for c in range(NC):
                    last = pe.matmul(ps[2][:, c * P:(c + 1) * P], oT[:, c * P:(c + 1) * P], wout[:, :],
                                     start=True, stop=True)
                last.then_inc(sem("mixed"), 1)
                pe.wait_ge(sem("y_ready"), u + 1)
                turn(y, sem("y_turned"))
                pe.wait_ge(sem("yT_ready"), u + 1)
                for c in range(NC):
                    last = pe.matmul(ps[3][:, c * NE:(c + 1) * NE], yT[:, c * P:(c + 1) * P], wgs[:, :],
                                     start=True, stop=True)
                last.then_inc(sem("logits"), 1)

        @block.vector
        def _(dve):
            dve.wait_ge(sem("weights"), 16 * 8)
            dve.wait_ge(sem("ones"), 2)
            dve.wait_ge(sem("same"), 2 * NSEQ)
            with dve.Fori(0, NT // NC) as u:
                link, links = chain(dve, sem("dve"), u * DVE_LINKS)

                def row(t):
                    return t[:, :].unsqueeze(1).to_broadcast([P, NC, D])

                def normed(to, of, turn, done):
                    for c in range(NC):
                        last = dve.bn_stats(st[:, c, :], of[:, c, :])
                    link(last)
                    dve.sem_inc(sem("passed"))
                    for c in range(NC):
                        last = dve.bn_aggr(mv[:, c, :], st[:, c, :])
                    link(last)
                    dve.tensor_scalar(ve[:, :], mv[:, :, 1], LN_EPS, None, ALU.add).then_inc(sem("var_ready"), 1)
                    dve.wait_ge(sem("rstd_ready"), 2 * u + turn)
                    for c in range(NC):
                        last = dve.tensor_scalar(to[:, c, :], of[:, c, :], mv[:, c, 0:1], rstd[:, c:c + 1],
                                                 ALU.subtract, ALU.mult)
                    done(last)

                dve.wait_ge(sem("x_loaded"), 64 * u + 64)
                normed(h, xt, 1, lambda last: last.then_inc(sem("h_ready"), 1))
                dve.wait_ge(sem("v_ready"), u + 1)
                dve.tensor_tensor(v[:, :, :], tiles(ps[3]), row(bv), ALU.add).then_inc(sem("v_used"), 1)
                for j in range(AH):
                    dve.wait_ge(sem("scores"), AH * u + j + 1)
                    last = dve.scalar_tensor_tensor(
                        out=sc[:, j, :, :], in0=tiles(ps[4 + j]), scalar=float(AHD) ** -0.5,
                        in1=same[:, :, :].rearrange("p l n -> p (l n)").unsqueeze(1).to_broadcast([P, NC, P]),
                        op0=ALU.mult, op1=ALU.add)
                link(last)
                link(dve.tensor_reduce(mx[:, :], sc[:, :, :, :].rearrange("p j c s -> p (j c) s"), AX_X, ALU.max))
                dve.tensor_scalar(mx[:, :], mx[:, :], -1.0, None, ALU.mult).then_inc(sem("max_ready"), 1)
                dve.wait_ge(sem("probs"), AH * u + AH)
                link(dve.reciprocal(rden[:, :, :].rearrange("p j c -> p (j c)"), den[:, :]))
                dve.wait_ge(sem("o_ready"), u + 1)
                for c in range(NC):
                    last = dve.tensor_tensor(on[:, c, :].rearrange("p (j d) -> p j d", j=AH),
                                             ps[1][:, c * P:(c + 1) * P].rearrange("p (j d) -> p j d", j=AH),
                                             rden[:, :, c].unsqueeze(2).to_broadcast([P, AH, AHD]), ALU.mult)
                last.then_inc(sem("on_ready"), 1)
                dve.wait_ge(sem("mixed"), u + 1)
                link(dve.tensor_tensor(h[:, :, :], h[:, :, :], tiles(ps[2]), ALU.add))
                link(dve.tensor_tensor(h[:, :, :], h[:, :, :], row(ob), ALU.add))
                dve.wait_ge(sem("stored"), 128 * u)
                normed(y, h, 2, link)
                link(dve.tensor_tensor(y[:, :, :], y[:, :, :], row(lg), ALU.mult))
                dve.tensor_tensor(y[:, :, :], y[:, :, :], row(lb), ALU.add).then_inc(sem("y_ready"), 1)
                dve.wait_ge(sem("logits"), u + 1)
                lo = ps[3][:, 0:NC * NE].rearrange("p (c e) -> p c e", e=NE)
                spread = lambda t: t[:, :].unsqueeze(2).to_broadcast([P, NC, NE])
                link(dve.tensor_reduce(lm[:, :], lo, AX_X, ALU.max))
                dve.tensor_tensor(ld[:, :, :], lo, spread(lm), ALU.subtract).then_inc(sem("ld_ready"), 1)
                link(dve.tensor_tensor(hit[:, :, :], lo, spread(lm), ALU.is_equal))
                link(dve.tensor_tensor(hit[:, :, :], hit[:, :, :], order[:, :].unsqueeze(1).to_broadcast([P, NC, NE]),
                                       ALU.mult))
                link(dve.tensor_reduce(first[:, :], hit[:, :, :], AX_X, ALU.max))
                link(dve.tensor_tensor(rt[:, :, 0, :], hit[:, :, :], spread(first), ALU.is_equal))
                dve.wait_ge(sem("le_ready"), u + 1)
                link(dve.tensor_reduce(ls[:, :], le[:, :, :], AX_X, ALU.add))
                link(dve.reciprocal(lr[:, :], ls[:, :]))
                dve.tensor_tensor(rt[:, :, 1, :], rt[:, :, 0, :], spread(lr), ALU.mult).then_inc(sem("route_ready"), 1)
                assert links[0] == DVE_LINKS, links


def linear_expert_phase(nc, x_in, y_in, route, x_out, w1_rows, b1_t, w2_rows, b2, ln_g, ln_b):
    NC = 4
    KC = FF // P
    DVE_LINKS = 8
    with ExitStack() as ctx:
        def sb(name, shape):
            return ctx.enter_context(nc.sbuf_tensor("f_" + name, shape, F32))
        sem = semaphores(nc, ctx, "f")
        ident = sb("ident", [P, P])
        before = sb("before", [P, P])
        ones = sb("ones", [P, P])
        mhalf = sb("mhalf", [P, NC])
        w1s = sb("w1s", [P, NE * KC, D])
        w2s = sb("w2s", [P, NE * KC, D])
        w12 = sb("w12", [P, NE, D])
        b1s = sb("b1s", [P, NE * KC])
        b1d = sb("b1d", [P, NE * KC, NE])
        b2s = sb("b2s", [NE, D])
        b12 = sb("b12", [NE, D])
        lg = sb("lg", [P, D])
        lb = sb("lb", [P, D])
        rts = sb("rts", [P, NT, 2 * NE])
        hot = sb("hot", [P, NE, NT])
        total = sb("total", [P, NE, NT])
        earlier = sb("earlier", [P, NE, NT + 1])
        loc = sb("loc", [P, NE, NT])
        cw = sb("cw", [P, NT, NE])
        cur = sb("cur", [P, NC, NE])
        curT = sb("curT", [NE, 512])
        xt = sb("xt", [P, NC, D])
        yt = sb("yt", [P, NC, D])
        yT = sb("yT", [P, 512])
        part = sb("part", [P, 2, NE, D])
        moe = sb("moe", [P, NC, D])
        xo = sb("xo", [P, NC, D])
        st = sb("st", [P, NC, 6])
        mv = sb("mv", [P, NC, 2])
        ve = sb("ve", [P, NC])
        rstd = sb("rstd", [P, NC])
        ps = [ctx.enter_context(nc.psum_tensor(f"f_ps{n}", [P, 512], F32)) for n in range(4)]
        pe_out = [ctx.enter_context(nc.psum_tensor(f"f_pe{n}", [P, 2, 512], F32)) for n in range(2)]
        block = ctx.enter_context(nc.Block())
        tiles = lambda t: t[:, :].rearrange("p (c d) -> p c d", c=NC)

        @block.sync
        def _(sp):
            for to, of in ((w1s[:, :, :].rearrange("p k d -> p (k d)"), w1_rows),
                           (w2s[:, :, :].rearrange("p k d -> p (k d)"), w2_rows),
                           (b1s[:, :], b1_t), (b2s[:, :], b2),
                           (lg[:, :], ln_g.partition_broadcast(P)), (lb[:, :], ln_b.partition_broadcast(P)),
                           (rts[:, :, :], route.rearrange("(i p) f -> p i f", p=P))):
                sp.dma_start(to, of).then_inc(sem("weights"), 16)
            with sp.Fori(0, NSEQ) as u:
                sp.wait_ge(sem("x_used"), u)
                sp.dma_start(yt[:, :, :], load_seq(y_in, u)).then_inc(sem("loaded"), 16)
                sp.dma_start(xt[:, :, :], load_seq(x_in, u)).then_inc(sem("loaded"), 16)
                sp.wait_ge(sem("x_used"), u + 1)
                sp.dma_start(load_seq(x_out, u), xo[:, :, :]).then_inc(sem("stored"), 16)
            sp.wait_ge(sem("stored"), 16 * NSEQ)

        @block.gpsimd
        def _(pool):
            make_identity(pool, ident, sem("ident"))
            link, _ = chain(pool, sem("setup"), 0)
            pool.memset(mhalf[:, :], -0.5)
            pool.memset(ones[:, :], 1.0)
            link(pool.memset(before[:, :], 1.0))
            pool.affine_select(out=before[:, :], in_=before[:, :], compare_op=ALU.is_gt, fill=0.0, base=0,
                               pattern=[[1, P]], channel_multiplier=-1).then_inc(sem("masks"), 1)
            with pool.Fori(0, NSEQ) as u:
                pool.wait_ge(sem("var_ready"), u + 1)
                pool.tensor_tensor(rstd[:, :], ve[:, :], mhalf[:, :], ALU.pow).then_inc(sem("rstd_ready"), 1)

        @block.scalar
        def _(act):
            for n in range(2):
                act.wait_ge(sem("w12_sum"), n + 1)
                act.activation(w12[:, 4 * n:4 * n + 4, :].rearrange("p e d -> p (e d)"), ps[n][:, :], ACT.Copy)\
                   .then_inc(sem("w12_ready"), 1)
            with act.Fori(0, NSEQ) as u:
                act.wait_ge(sem("y_turned"), u + 1)
                act.activation(yT[:, :], ps[0][:, :], ACT.Copy).then_inc(sem("yT_ready"), 1)
                act.wait_ge(sem("cur_turned"), u + 1)
                act.activation(curT[:, :], ps[1][0:NE, :], ACT.Copy).then_inc(sem("curT_ready"), 1)

        @block.tensor
        def _(pe):
            pe.wait_ge(sem("ident"), 2)
            pe.wait_ge(sem("masks"), 1)
            pe.wait_ge(sem("weights"), 16 * 7)
            for e in range(NE):
                for k in range(KC):
                    last = pe.matmul(ps[e // 4][:, (e % 4) * D:(e % 4 + 1) * D], w1s[:, e * KC + k, :],
                                     w2s[:, e * KC + k, :], start=(k == 0), stop=(k == KC - 1))
                if e % 4 == 3:
                    last.then_inc(sem("w12_sum"), 1)
            pe.wait_ge(sem("b1_placed"), 1)
            for m in range(NE * KC):
                last = pe.matmul(ps[2][0:NE, 0:D], b1d[:, m, :], w2s[:, m, :], start=(m == 0), stop=(m == NE * KC - 1))
            last.then_inc(sem("b12_sum"), 1)
            pe.wait_ge(sem("hot_ready"), 1)
            flat = hot[:, :, :].rearrange("p e i -> p (e i)")
            pe.matmul(pe_out[0][:, 0, :], before[:, :], flat, start=True, stop=True)
            pe.matmul(pe_out[0][:, 1, :], ones[:, :], flat, start=True, stop=True).then_inc(sem("counted"), 1)
            pe.wait_ge(sem("w12_ready"), 2)
            pe.wait_ge(sem("b12_ready"), 1)
            with pe.Fori(0, NSEQ) as u:
                pe.wait_ge(sem("loaded"), 32 * u + 32)
                for c in range(NC):
                    last = pe.transpose(ps[0][:, c * P:(c + 1) * P], yt[:, c, :], ident[:, :])
                last.then_inc(sem("y_turned"), 1)
                pe.wait_ge(sem("cur_ready"), u + 1)
                for c in range(NC):
                    last = pe.transpose(ps[1][0:NE, c * P:(c + 1) * P], cur[:, c, :], ident[:, :])
                last.then_inc(sem("cur_turned"), 1)
                pe.wait_ge(sem("yT_ready"), u + 1)
                for c in range(NC):
                    if c >= 2:
                        pe.wait_ge(sem("weighed"), NC * u + c - 1)
                    for n in range(2):
                        last = pe.matmul(pe_out[c % 2][:, n, :], yT[:, c * P:(c + 1) * P],
                                         w12[:, 4 * n:4 * n + 4, :].rearrange("p e d -> p (e d)"), start=True, stop=True)
                    last.then_inc(sem("experts"), 1)
                pe.wait_ge(sem("curT_ready"), u + 1)
                for c in range(NC):
                    last = pe.matmul(ps[2][:, c * P:(c + 1) * P], curT[:, c * P:(c + 1) * P], b12[:, :],
                                     start=True, stop=True)
                last.then_inc(sem("biases"), 1)

        @block.vector
        def _(dve):
            dve.wait_ge(sem("weights"), 16 * 7)
            link, _ = chain(dve, sem("setup_dve"), 0)
            link(dve.memset(b1d[:, :, :], 0.0))
            for e in range(NE):
                last = dve.tensor_copy(b1d[:, e * KC:(e + 1) * KC, e], b1s[:, e * KC:(e + 1) * KC])
            last.then_inc(sem("b1_placed"), 1)
            dve.tensor_copy(hot[:, :, :], rts[:, :, 0:NE].rearrange("p i e -> p e i")).then_inc(sem("hot_ready"), 1)
            dve.memset(total[:, :, :], 1.0)
            link(dve.memset(earlier[:, :, 0:1], 0.0))
            dve.wait_ge(sem("counted"), 1)
            counts = pe_out[0][:, 1, :].rearrange("p (e i) -> p e i", e=NE)
            for e in range(NE):
                last = dve.tensor_tensor_scan(earlier[:, e, 1:NT + 1], total[:, e, :], counts[:, e, :], 0.0,
                                              ALU.mult, ALU.add)
            link(last)
            link(dve.tensor_tensor(loc[:, :, :], earlier[:, :, 0:NT],
                                   pe_out[0][:, 0, :].rearrange("p (e i) -> p e i", e=NE), ALU.add))
            link(dve.tensor_scalar(loc[:, :, :], loc[:, :, :], float(CAP), None, ALU.is_lt))
            link(dve.tensor_tensor(cw[:, :, :], rts[:, :, NE:2 * NE], loc[:, :, :].rearrange("p e i -> p i e"), ALU.mult))
            dve.wait_ge(sem("b12_sum"), 1)
            dve.tensor_tensor(b12[:, :], b2s[:, :], ps[2][0:NE, 0:D], ALU.add).then_inc(sem("b12_ready"), 1)
            with dve.Fori(0, NSEQ) as u:
                link, links = chain(dve, sem("dve"), u * DVE_LINKS)

                def row(t):
                    return t[:, :].unsqueeze(1).to_broadcast([P, NC, D])

                dve.wait_ge(sem("curT_ready"), u)
                dve.tensor_copy(cur[:, :, :], cw[:, bass.ds(u * NC, NC), :]).then_inc(sem("cur_ready"), 1)
                dve.wait_ge(sem("cur_ready"), u + 1)
                for c in range(NC):
                    dve.wait_ge(sem("experts"), NC * u + c + 1)
                    dve.tensor_tensor(part[:, c % 2, :, :],
                                      pe_out[c % 2][:, :, :].rearrange("p a (e d) -> p (a e) d", d=D),
                                      cur[:, c, :].unsqueeze(2).to_broadcast([P, NE, D]), ALU.mult)\
                       .then_inc(sem("weighed"), 1)
                    dve.wait_ge(sem("weighed"), NC * u + c + 1)
                    last = dve.tensor_reduce(moe[:, c, :], part[:, c % 2, :, :].rearrange("p e d -> p d e"), AX_X, ALU.add)
                link(last)
                dve.wait_ge(sem("biases"), u + 1)
                link(dve.tensor_tensor(moe[:, :, :], moe[:, :, :], tiles(ps[2]), ALU.add))
                dve.wait_ge(sem("loaded"), 32 * u + 32)
                link(dve.tensor_tensor(moe[:, :, :], moe[:, :, :], yt[:, :, :], ALU.add))
                for c in range(NC):
                    last = dve.bn_stats(st[:, c, :], moe[:, c, :])
                link(last)
                dve.sem_inc(sem("passed"))
                for c in range(NC):
                    last = dve.bn_aggr(mv[:, c, :], st[:, c, :])
                link(last)
                dve.tensor_scalar(ve[:, :], mv[:, :, 1], LN_EPS, None, ALU.add).then_inc(sem("var_ready"), 1)
                dve.wait_ge(sem("rstd_ready"), u + 1)
                for c in range(NC):
                    last = dve.tensor_scalar(moe[:, c, :], moe[:, c, :], mv[:, c, 0:1], rstd[:, c:c + 1],
                                             ALU.subtract, ALU.mult)
                link(last)
                link(dve.tensor_tensor(moe[:, :, :], moe[:, :, :], row(lg), ALU.mult))
                link(dve.tensor_tensor(moe[:, :, :], moe[:, :, :], row(lb), ALU.add))
                dve.wait_ge(sem("stored"), 16 * u)
                dve.tensor_tensor(xo[:, :, :], moe[:, :, :], xt[:, :, :], ALU.add).then_inc(sem("x_used"), 1)
                assert links[0] == DVE_LINKS, links


def build(nc, a, out):
    def scratch(name, shape):
        return nc.dram_tensor(name, shape, F32).ap()
    tokens = NSEQ * SEQ
    x1, x2, x3, y1 = (scratch(n, (tokens, D)) for n in ("x1", "x2", "x3", "y1"))
    h_t = scratch("h_t", (D, NSEQ, SEQ + TAPS - 1))
    gates = scratch("gates", (NSTEP, P, GATES))
    route = scratch("route", (tokens, 2 * NE))
    linear_attention_phase(nc, a["x"], x1, a["l0_wq_t"], a["l0_wk_t"], a["l0_wv_t"], a["l0_wo_t"], a["l0_norm_w"])
    expert_phase(nc, x1, x2, a["gate_t"], a["gate_bias"], a["wg_t"], a["wu_t"], a["wd_t"], a["wsg_t"], a["wsu_t"],
                 a["wsd_t"])
    gate_phase(nc, x2, h_t, gates, a["w_ba"], a["dt_bias"], a["a_log"])
    delta_phase(nc, x2, x3, h_t, gates, a["w_in"], a["conv_t"], a["l1_norm_w"], a["w_o"])
    attention_phase(nc, x3, y1, route, a["in_t"], a["in_b"], a["in_b_cols"], a["out_t"], a["out_b"], a["ln1_g"],
                    a["ln1_b"], a["wg"])
    linear_expert_phase(nc, x3, y1, route, out, a["w1_rows"], a["b1_t"], a["w2_rows"], a["b2"], a["ln2_g"], a["ln2_b"])


def kernel(**inputs):
    import numpy as np
    import concourse.bacc as bacc
    from concourse.bass_utils import run_bass_kernel_spmd

    i = {k: np.asarray(v) for k, v in inputs.items()}
    arrays = {
        "x": i["L0_attn_hidden_states"].reshape(NSEQ * SEQ, D),
        "l0_wq_t": i["L0_attn_Wq"].T, "l0_wk_t": i["L0_attn_Wk"].T, "l0_wv_t": i["L0_attn_Wv"].T,
        "l0_wo_t": i["L0_attn_Wo"].T, "l0_norm_w": i["L0_attn_norm_w"],
        "gate_t": i["L0_ffn_gate_w"].T, "gate_bias": i["L0_ffn_gate_bias"],
        "wg_t": i["L0_ffn_Wg"].reshape(-1, D).T, "wu_t": i["L0_ffn_Wu"].reshape(-1, D).T,
        "wd_t": i["L0_ffn_Wd"].transpose(0, 2, 1).reshape(-1, D),
        "wsg_t": i["L0_ffn_Ws_g"].T, "wsu_t": i["L0_ffn_Ws_u"].T, "wsd_t": i["L0_ffn_Ws_d"].T,
        "w_in": i["L1_attn_W_in"], "w_ba": i["L1_attn_W_ba"], "conv_t": i["L1_attn_conv_w"].reshape(-1, TAPS).T,
        "dt_bias": i["L1_attn_dt_bias"], "a_log": i["L1_attn_A_log"], "l1_norm_w": i["L1_attn_norm_w"],
        "w_o": i["L1_attn_W_o"],
        "in_t": i["L1_ffn_in_proj_w"].T, "in_b": i["L1_ffn_in_proj_b"],
        "in_b_cols": i["L1_ffn_in_proj_b"].reshape(3, D).T, "out_t": i["L1_ffn_out_proj_w"].T,
        "out_b": i["L1_ffn_out_proj_b"], "ln1_g": i["L1_ffn_ln1_g"], "ln1_b": i["L1_ffn_ln1_b"],
        "ln2_g": i["L1_ffn_ln2_g"], "ln2_b": i["L1_ffn_ln2_b"], "wg": i["L1_ffn_wg"],
        "w1_rows": i["L1_ffn_w1"].reshape(NE, D, FF // P, P).transpose(3, 0, 2, 1).reshape(P, -1),
        "w2_rows": i["L1_ffn_w2"].reshape(NE, FF // P, P, D).transpose(2, 0, 1, 3).reshape(P, -1),
        "b1_t": i["L1_ffn_b1"].reshape(NE, FF // P, P).transpose(2, 0, 1).reshape(P, NE * FF // P),
        "b2": i["L1_ffn_b2"],
    }
    arrays = {f"in_{k}": np.ascontiguousarray(v) for k, v in arrays.items()}
    nc = bacc.Bacc("TRN2", target_bir_lowering=False, num_devices=1)
    aps = {k[3:]: nc.dram_tensor(k, v.shape, F32, kind="ExternalInput").ap() for k, v in arrays.items()}
    out = nc.dram_tensor("out", (NSEQ * SEQ, D), F32, kind="ExternalOutput").ap()
    build(nc, aps, out)
    r = run_bass_kernel_spmd(nc, [arrays], core_ids=[0])
    return r.results[0]["out"].reshape(NSEQ, SEQ, D)
```

```python
from contextlib import ExitStack

import concourse.bass as bass
from concourse import mybir

F32 = mybir.dt.float32
ALU = mybir.AluOpType
ACT = mybir.ActivationFunctionType
AX_X = mybir.AxisListType.X

P = 128
D = 128
NSEQ, SEQ = 16, 512
NT = NSEQ * SEQ // P
LN_EPS = 1e-5


def semaphores(nc, ctx, phase):
    made = {}

    def sem(name):
        if name not in made:
            made[name] = nc.alloc_semaphore(name=f"{phase}_{name}")
        return made[name]

    def clear():
        nc.clear_and_free_semaphores(list(made.values()))
        nc.all_engine_barrier()
    ctx.callback(clear)
    return sem


def chain(engine, sem, start):
    done = [0]

    def link(ins):
        done[0] += 1
        ins.then_inc(sem, 1)
        engine.wait_ge(sem, start + done[0])
    return link, done


def load_seq(x, s):
    return x[bass.ds(s * SEQ, SEQ), :].rearrange("(c p) d -> p c d", p=P)


def make_identity(pool, ident, sem):
    pool.memset(ident[:, :], 0.0).then_inc(sem, 1)
    pool.wait_ge(sem, 1)
    pool.affine_select(out=ident[:, :], in_=ident[:, :], compare_op=ALU.not_equal, fill=1.0, base=0,
                       pattern=[[-1, P]], channel_multiplier=1).then_inc(sem, 1)


def linear_attention_phase(nc, x_in, x_out, wq_t, wk_t, wv_t, wo_t, norm_w):
    H, HD, HP = 8, 16, 32
    G = 4
    NC = SEQ // P
    V1 = HD + 1
    DVE_LINKS = 13
    with ExitStack() as ctx:
        def sb(name, shape):
            return ctx.enter_context(nc.sbuf_tensor("a_" + name, shape, F32))
        sem = semaphores(nc, ctx, "a")
        ident = sb("ident", [P, P])
        causal = sb("causal", [P, P])
        own_head = sb("own_head", [P, G, V1])
        mhalf = sb("mhalf", [P, 32])
        wq = sb("wq", [P, 2 * P])
        wkv = sb("wkv", [P, 3 * P])
        wo = sb("wo", [P, P])
        nw = sb("nw", [P, HD])
        xt = sb("xt", [P, NC, D])
        h = sb("h", [P, NC, D])
        hT = sb("hT", [P, SEQ])
        qT = sb("qT", [P, 2, SEQ])
        kT = sb("kT", [P, 2, SEQ])
        kt = sb("kt", [P, NC, 2 * P])
        v1 = sb("v1", [P, NC, H, V1])
        pr = sb("pr", [P, 2, G, 2, P])
        state = sb("state", [P, 2, G, V1])
        upd = sb("upd", [P, 2, G, V1])
        o = sb("o", [P, NC * H, V1])
        on = sb("on", [P, NC * H, HD])
        sq = sb("sq", [P, NC * H, HD])
        oT = sb("oT", [P, SEQ])
        xr = sb("xr", [P, NC, D])
        xo = sb("xo", [P, NC, D])
        st = sb("st", [P, NC, 6])
        mv = sb("mv", [P, NC, 2])
        ve = sb("ve", [P, NC])
        rstd = sb("rstd", [P, NC])
        den = sb("den", [P, NC * H])
        rden = sb("rden", [P, NC * H])
        var = sb("var", [P, NC * H])
        rms = sb("rms", [P, NC * H])
        ps = [ctx.enter_context(nc.psum_tensor(f"a_ps{n}", [P, 512], F32)) for n in range(8)]
        block = ctx.enter_context(nc.Block())

        @block.sync
        def _(sp):
            sp.wait_ge(sem("padded"), 2)
            sp.dma_start(wq[:, :].rearrange("p (h e) -> p h e", e=HP)[:, :, 0:HD],
                         wq_t.rearrange("d (h e) -> d h e", e=HD)).then_inc(sem("weights"), 16)
            sp.dma_start(wkv[:, 0:2 * P].rearrange("p (h e) -> p h e", e=HP)[:, :, 0:HD],
                         wk_t.rearrange("d (h e) -> d h e", e=HD)).then_inc(sem("weights"), 16)
            sp.dma_start(wkv[:, 2 * P:3 * P], wv_t).then_inc(sem("weights"), 16)
            sp.dma_start(wo[:, :], wo_t).then_inc(sem("weights"), 16)
            sp.dma_start(nw[:, :], norm_w.partition_broadcast(P)).then_inc(sem("weights"), 16)

            def load(s):
                sp.dma_start(xt[:, :, :], load_seq(x_in, s)).then_inc(sem("x_loaded"), 16)

            def store(s):
                sp.wait_ge(sem("x_used"), s + 1)
                sp.dma_start(load_seq(x_out, s), xo[:, :, :]).then_inc(sem("stored"), 16)

            load(0)
            with sp.Fori(0, NSEQ - 1) as s:
                sp.wait_ge(sem("h_ready"), s + 1)
                sp.wait_ge(sem("x_kept"), s + 1)
                load(s + 1)
                store(s)
            store(NSEQ - 1)
            sp.wait_ge(sem("stored"), 16 * NSEQ)

        @block.gpsimd
        def _(pool):
            make_identity(pool, ident, sem("ident"))
            pool.memset(wq[:, :], 0.0).then_inc(sem("padded"), 1)
            pool.memset(wkv[:, :], 0.0).then_inc(sem("padded"), 1)
            pool.memset(mhalf[:, :], -0.5).then_inc(sem("ones"), 1)
            pool.memset(v1[:, :, :, :], 1.0).then_inc(sem("ones"), 1)
            pool.memset(causal[:, :], 1.0).then_inc(sem("ones"), 1)
            pool.memset(own_head[:, :, :], 1.0).then_inc(sem("ones"), 1)
            pool.wait_ge(sem("ones"), 4)
            pool.affine_select(out=causal[:, :], in_=causal[:, :], compare_op=ALU.is_ge, fill=0.0, base=0,
                               pattern=[[1, P]], channel_multiplier=-1).then_inc(sem("ones"), 1)
            pool.affine_select(out=own_head[:, :, :], in_=own_head[:, :, :], compare_op=ALU.is_ge, fill=0.0,
                               base=0, pattern=[[-HP, G], [0, V1]], channel_multiplier=1).then_inc(sem("ones"), 1)
            pool.wait_ge(sem("ones"), 6)
            pool.affine_select(out=own_head[:, :, :], in_=own_head[:, :, :], compare_op=ALU.is_ge, fill=0.0,
                               base=HP - 1, pattern=[[HP, G], [0, V1]], channel_multiplier=-1).then_inc(sem("ones"), 1)

            def norm(s):
                pool.wait_ge(sem("var_ready"), s + 1)
                pool.tensor_tensor(rstd[:, :], ve[:, :], mhalf[:, 0:NC], ALU.pow).then_inc(sem("rstd_ready"), 1)

            def head_norms(s):
                pool.wait_ge(sem("hvar_ready"), s + 1)
                pool.tensor_tensor(rms[:, :], var[:, :], mhalf[:, :], ALU.pow).then_inc(sem("rms_ready"), 1)

            norm(0)
            with pool.Fori(0, NSEQ - 1) as s:
                norm(s + 1)
                head_norms(s)
            head_norms(NSEQ - 1)

        @block.scalar
        def _(act):
            def prepare(s):
                act.wait_ge(sem("h_turned"), s + 1)
                act.activation(hT[:, :], ps[0][:, :], ACT.Copy).then_inc(sem("hT_ready"), 1)
                act.wait_ge(sem("qk_ready"), s + 1)
                for g in range(2):
                    act.activation(qT[:, g, :], ps[1 + g][:, :], ACT.Copy)
                    last = act.activation(kT[:, g, :], ps[3 + g][:, :], ACT.Copy)
                last.then_inc(sem("qkT_ready"), 1)

            def turn(s):
                act.wait_ge(sem("o_turned"), s + 1)
                act.activation(oT[:, :], ps[0][:, :], ACT.Copy).then_inc(sem("oT_ready"), 1)

            def keep(s):
                act.wait_ge(sem("x_loaded"), 16 * s + 16)
                act.wait_ge(sem("x_used"), s)
                act.activation(xr[:, :, :], xt[:, :, :], ACT.Copy).then_inc(sem("x_kept"), 1)

            keep(0)
            prepare(0)
            with act.Fori(0, NSEQ - 1) as s:
                prepare(s + 1)
                turn(s)
                keep(s + 1)
            turn(NSEQ - 1)

        @block.tensor
        def _(pe):
            pe.wait_ge(sem("ident"), 2)
            pe.wait_ge(sem("weights"), 16 * 5)
            def prepare(s, sequences_out):
                pe.wait_ge(sem("h_ready"), s + 1)
                for c in range(NC):
                    last = pe.transpose(ps[0][:, c * P:(c + 1) * P], h[:, c, :], ident[:, :])
                last.then_inc(sem("h_turned"), 1)
                pe.wait_ge(sem("hT_ready"), s + 1)
                for g in range(2):
                    pe.matmul(ps[1 + g][:, :], wq[:, g * P:(g + 1) * P], hT[:, :], start=True, stop=True)
                    last = pe.matmul(ps[3 + g][:, :], wkv[:, g * P:(g + 1) * P], hT[:, :], start=True, stop=True)
                last.then_inc(sem("qk_ready"), 1)
                pe.wait_ge(sem("state_ready"), (NC + 1) * s)
                pe.wait_ge(sem("x_used"), sequences_out)
                for c in range(NC):
                    if c == 3:
                        pe.wait_ge(sem("kv_used"), NC * s + 1)
                    pe.matmul(ps[5 + c % 3][:, 0:3 * P], hT[:, c * P:(c + 1) * P], wkv[:, :],
                              start=True, stop=True).then_inc(sem("kv_ready"), 1)

            def chunks(s):
                pe.wait_ge(sem("qkT_ready"), s + 1)
                for c in range(NC):
                    here = slice(c * P, (c + 1) * P)
                    half = (c % 2) * 2 * P
                    for j in range(G):
                        for g in range(2):
                            last = pe.matmul(ps[1 + j][:, half + g * P:half + (g + 1) * P],
                                             kT[HP * j:HP * j + HD, g, here], qT[HP * j:HP * j + HD, g, here],
                                             start=True, stop=True)
                    last.then_inc(sem("scores"), 1)
                    pe.wait_ge(sem("state_ready"), (NC + 1) * s + c + 1)
                    for g in range(2):
                        pe.matmul(ps[5][:, g * G * V1:(g + 1) * G * V1], qT[:, g, here],
                                  state[:, g, :, :].rearrange("p h e -> p (h e)"),
                                  start=(g == 0), stop=False, skip_group_check=True)
                    pe.wait_ge(sem("probs"), NC * s + c + 1)
                    for hd in range(H):
                        last = pe.matmul(ps[5][:, hd * V1:(hd + 1) * V1], pr[:, c % 2, hd % G, hd // G, :],
                                         v1[:, c, hd, :], start=False, stop=True, skip_group_check=True)
                    last.then_inc(sem("o_ready"), 1)
                    for g in range(2):
                        last = pe.matmul(ps[7][:, g * G * V1:(g + 1) * G * V1], kt[:, c, g * P:(g + 1) * P],
                                         v1[:, c, g * G:(g + 1) * G, :].rearrange("p h e -> p (h e)"),
                                         start=True, stop=True)
                    last.then_inc(sem("update"), 1)

            def project(s, kv_used):
                pe.wait_ge(sem("on_ready"), s + 1)
                for c in range(NC):
                    last = pe.transpose(ps[0][:, c * P:(c + 1) * P],
                                        on[:, c * H:(c + 1) * H, :].rearrange("p h e -> p (h e)"), ident[:, :])
                last.then_inc(sem("o_turned"), 1)
                pe.wait_ge(sem("oT_ready"), s + 1)
                pe.wait_ge(sem("kv_used"), kv_used)
                for c in range(NC):
                    last = pe.matmul(ps[6][:, c * P:(c + 1) * P], oT[:, c * P:(c + 1) * P], wo[:, :],
                                     start=True, stop=True)
                last.then_inc(sem("y_ready"), 1)

            prepare(0, 0)
            with pe.Fori(0, NSEQ - 1) as s:
                chunks(s)
                prepare(s + 1, s)
                project(s, NC * s + 2 * NC)
            chunks(NSEQ - 1)
            project(NSEQ - 1, NC * NSEQ)

        @block.vector
        def _(dve):
            dve.wait_ge(sem("ones"), 7)
            dve.wait_ge(sem("weights"), 16 * 5)

            def norm_sums(s, link):
                dve.wait_ge(sem("x_loaded"), 16 * s + 16)
                for c in range(NC):
                    last = dve.bn_stats(st[:, c, :], xt[:, c, :])
                link(last)
                dve.sem_inc(sem("passed"))
                for c in range(NC):
                    last = dve.bn_aggr(mv[:, c, :], st[:, c, :])
                link(last)
                dve.tensor_scalar(ve[:, :], mv[:, :, 1], LN_EPS, None, ALU.add).then_inc(sem("var_ready"), 1)

            def norm(s):
                dve.wait_ge(sem("rstd_ready"), s + 1)
                for c in range(NC):
                    last = dve.tensor_scalar(h[:, c, :], xt[:, c, :], mv[:, c, 0:1], rstd[:, c:c + 1],
                                             ALU.subtract, ALU.mult)
                last.then_inc(sem("h_ready"), 1)

            def take_kv(s):
                for c in range(NC):
                    dve.wait_ge(sem("kv_ready"), NC * s + c + 1)
                    dve.tensor_copy(kt[:, c, :], ps[5 + c % 3][:, 0:2 * P])
                    last = dve.tensor_copy(v1[:, c, :, 0:HD],
                                           ps[5 + c % 3][:, 2 * P:3 * P].rearrange("p (h e) -> p h e", e=HD))
                    last.then_inc(sem("kv_used"), 1)
                dve.wait_ge(sem("kv_used"), NC * s + NC)
                dve.memset(state[:, :, :, :], 0.0).then_inc(sem("state_ready"), 1)

            def chunks(s, link, ahead=None):
                for c in range(NC):
                    half = (c % 2) * 2 * P
                    if ahead is not None and c == 1:
                        norm_sums(ahead, link)
                    if ahead is not None and c == 2:
                        norm(ahead)
                    dve.wait_ge(sem("scores"), NC * s + c + 1)
                    for j in range(G):
                        last = dve.tensor_tensor(
                            pr[:, c % 2, j, :, :], ps[1 + j][:, half:half + 2 * P].rearrange("p (g t) -> p g t", g=2),
                            causal[:, :].unsqueeze(1).to_broadcast([P, 2, P]), ALU.mult)
                    last.then_inc(sem("probs"), 1)
                    dve.wait_ge(sem("o_ready"), NC * s + c + 1)
                    dve.tensor_copy(o[:, c * H:(c + 1) * H, :],
                                    ps[5][:, 0:H * V1].rearrange("p (h e) -> p h e", e=V1))
                    dve.wait_ge(sem("update"), NC * s + c + 1)
                    link(dve.tensor_tensor(upd[:, :, :, :].rearrange("p g h e -> p g (h e)"),
                                           ps[7][:, 0:H * V1].rearrange("p (g e) -> p g e", g=2),
                                           own_head[:, :, :].rearrange("p h e -> p (h e)").unsqueeze(1)
                                           .to_broadcast([P, 2, G * V1]), ALU.mult))
                    dve.tensor_tensor(state[:, :, :, :], state[:, :, :, :], upd[:, :, :, :], ALU.add)\
                       .then_inc(sem("state_ready"), 1)
                    dve.wait_ge(sem("state_ready"), (NC + 1) * s + c + 2)

            def head_sums(s, link):
                link(dve.scalar_tensor_tensor(out=den[:, :], in0=o[:, :, HD], scalar=-1.0, in1=o[:, :, HD],
                                              op0=ALU.mult, op1=ALU.max))
                link(dve.tensor_scalar(den[:, :], den[:, :], 1.0, None, ALU.max))
                link(dve.reciprocal(rden[:, :], den[:, :]))
                link(dve.tensor_tensor(on[:, :, :], o[:, :, 0:HD],
                                       rden[:, :].unsqueeze(2).to_broadcast([P, NC * H, HD]), ALU.mult))
                link(dve.tensor_tensor(sq[:, :, :], on[:, :, :], on[:, :, :], ALU.mult))
                link(dve.tensor_reduce(var[:, :], sq[:, :, :], AX_X, ALU.add))
                dve.tensor_scalar(var[:, :], var[:, :], 1.0 / HD, 1e-5, ALU.mult, ALU.add)\
                   .then_inc(sem("hvar_ready"), 1)

            def head_norms(s, link):
                dve.wait_ge(sem("rms_ready"), s + 1)
                link(dve.tensor_tensor(on[:, :, :], on[:, :, :],
                                       rms[:, :].unsqueeze(2).to_broadcast([P, NC * H, HD]), ALU.mult))
                dve.tensor_tensor(on[:, :, :], on[:, :, :],
                                  nw[:, :].unsqueeze(1).to_broadcast([P, NC * H, HD]), ALU.mult)\
                   .then_inc(sem("on_ready"), 1)

            def residual(s):
                dve.wait_ge(sem("y_ready"), s + 1)
                dve.wait_ge(sem("x_kept"), s + 1)
                dve.wait_ge(sem("stored"), 16 * s)
                dve.tensor_tensor(xo[:, :, :], xr[:, :, :], ps[6][:, :].rearrange("p (c d) -> p c d", c=NC), ALU.add)\
                   .then_inc(sem("x_used"), 1)

            first, _ = chain(dve, sem("first"), 0)
            norm_sums(0, first)
            norm(0)
            take_kv(0)
            with dve.Fori(0, NSEQ - 1) as s:
                link, links = chain(dve, sem("dve"), s * DVE_LINKS)
                chunks(s, link, s + 1)
                head_sums(s, link)
                take_kv(s + 1)
                head_norms(s, link)
                residual(s)
                assert links[0] == DVE_LINKS, links
            final, _ = chain(dve, sem("final"), 0)
            chunks(NSEQ - 1, final)
            head_sums(NSEQ - 1, final)
            head_norms(NSEQ - 1, final)
            residual(NSEQ - 1)


def expert_phase(nc, x_in, x_out, gate_t, gate_bias, wg_t, wu_t, wd_t, wsg_t, wsu_t, wsd_t):
    E, NG, K, TG, SCALE = 16, 4, 4, 2, 2.5
    EG = E // NG
    NC = SEQ // P
    NB = E * 64 // P
    DVE_LINKS = 35
    BIG = 1e30
    with ExitStack() as ctx:
        def sb(name, shape):
            return ctx.enter_context(nc.sbuf_tensor("b_" + name, shape, F32))
        sem = semaphores(nc, ctx, "b")
        ident = sb("ident", [P, P])
        spread = sb("spread", [E, E, 64])
        before_g = sb("before_g", [P, NG, NG])
        before_e = sb("before_e", [P, E, E])
        mhalf = sb("mhalf", [P, 32])
        gw = sb("gw", [P, E])
        bias = sb("bias", [P, E])
        wg = sb("wg", [P, NB + 1, P])
        wu = sb("wu", [P, NB + 1, P])
        wd = sb("wd", [P, NB + 1, D])
        xt = sb("xt", [P, NC, D])
        h = sb("h", [P, NC, D])
        hT = sb("hT", [P, SEQ])
        th = sb("th", [P, 2, SEQ])
        gated = sb("gated", [P, 2, SEQ])
        both = sb("both", [P, 2, SEQ])
        act_sb = sb("act", [P, NB + 1, SEQ])
        xh = sb("xh", [P, NC, D])
        xo = sb("xo", [P, NC, D])
        st = sb("st", [P, NC, 6])
        mv = sb("mv", [P, NC, 2])
        ve = sb("ve", [P, NC])
        rstd = sb("rstd", [P, NC])
        ex = sb("ex", [P, NC, E])
        ex1 = sb("ex1", [P, NC, E])
        score = sb("score", [P, NC, E])
        sf = sb("sf", [P, NC * NG, EG])
        hi = sb("hi", [P, NC * NG, 2])
        lo = sb("lo", [P, NC * NG, 2])
        top1 = sb("top1", [P, NC * NG])
        mid = sb("mid", [P, NC * NG])
        lows = sb("lows", [P, NC * NG])
        gs = sb("gs", [P, NC, NG])
        ggt = sb("ggt", [P, NC, NG * NG])
        geq = sb("geq", [P, NC, NG * NG])
        grank = sb("grank", [P, NC * NG])
        gin = sb("gin", [P, NC * NG])
        gout = sb("gout", [P, NC * NG])
        sfm = sb("sfm", [P, NC, E])
        egt = sb("egt", [P, NC, E * E])
        eeq = sb("eeq", [P, NC, E * E])
        erank = sb("erank", [P, NC * E])
        w = sb("w", [P, NC, E])
        wsum = sb("wsum", [P, NC])
        wrec = sb("wrec", [P, NC])
        cw = sb("cw", [P, NC, E])
        cwT = sb("cwT", [E, SEQ])
        ps = [ctx.enter_context(nc.psum_tensor(f"b_ps{n}", [P, 512], F32)) for n in range(8)]
        block = ctx.enter_context(nc.Block())
        WEIGHTS = 16 * 8

        @block.sync
        def _(sp):
            for to, of in ((gw[:, :], gate_t), (bias[:, :], gate_bias.partition_broadcast(P)),
                           (wg[:, 0:NB, :], wg_t.rearrange("d (b m) -> d b m", m=P)),
                           (wu[:, 0:NB, :], wu_t.rearrange("d (b m) -> d b m", m=P)),
                           (wd[:, 0:NB, :], wd_t.rearrange("(b m) d -> m b d", m=P)),
                           (wg[:, NB, :], wsg_t), (wu[:, NB, :], wsu_t), (wd[:, NB, :], wsd_t)):
                sp.dma_start(to, of).then_inc(sem("weights"), 16)

            def load(s):
                sp.dma_start(xt[:, :, :], load_seq(x_in, s)).then_inc(sem("x_loaded"), 16)

            def store(s):
                sp.wait_ge(sem("x_used"), s + 1)
                sp.dma_start(load_seq(x_out, s), xo[:, :, :]).then_inc(sem("stored"), 16)

            load(0)
            with sp.Fori(0, NSEQ - 1) as s:
                sp.wait_ge(sem("xh_ready"), s + 1)
                load(s + 1)
                store(s)
            store(NSEQ - 1)
            sp.wait_ge(sem("stored"), 16 * NSEQ)

        @block.gpsimd
        def _(pool):
            make_identity(pool, ident, sem("ident"))
            pool.memset(mhalf[:, :], -0.5).then_inc(sem("ones"), 1)
            pool.memset(spread[:, :, :], 1.0).then_inc(sem("ones"), 1)
            pool.memset(before_g[:, :, :], 1.0).then_inc(sem("ones"), 1)
            pool.memset(before_e[:, :, :], 1.0).then_inc(sem("ones"), 1)
            pool.wait_ge(sem("ones"), 4)
            pool.affine_select(out=spread[:, :, :], in_=spread[:, :, :], compare_op=ALU.is_equal, fill=0.0, base=0,
                               pattern=[[-1, E], [0, 64]], channel_multiplier=1).then_inc(sem("ones"), 1)
            pool.affine_select(out=before_g[:, :, :], in_=before_g[:, :, :], compare_op=ALU.is_gt, fill=0.0, base=0,
                               pattern=[[1, NG], [-1, NG]], channel_multiplier=0).then_inc(sem("ones"), 1)
            pool.affine_select(out=before_e[:, :, :], in_=before_e[:, :, :], compare_op=ALU.is_gt, fill=0.0, base=0,
                               pattern=[[1, E], [-1, E]], channel_multiplier=0).then_inc(sem("ones"), 1)
            with pool.Fori(0, NSEQ) as s:
                pool.wait_ge(sem("var_ready"), s + 1)
                pool.tensor_tensor(rstd[:, :], ve[:, :], mhalf[:, 0:NC], ALU.pow).then_inc(sem("rstd_ready"), 1)

        @block.scalar
        def _(act):
            def prepare(s):
                act.wait_ge(sem("h_turned"), s + 1)
                act.activation(hT[:, :], ps[0][:, :], ACT.Copy).then_inc(sem("hT_ready"), 1)
                act.wait_ge(sem("logits"), s + 1)
                act.activation(ex[:, :, :], ps[1][:, 0:NC * E].rearrange("p (c e) -> p c e", e=E), ACT.Exp, scale=-1.0)\
                   .then_inc(sem("ex_ready"), 1)

            def main(s):
                for b in range(NB + 1):
                    act.wait_ge(sem("gate_up"), (NB + 1) * s + b + 1)
                    if b >= 2:
                        act.wait_ge(sem("gate_used"), NB * s + b - 1)
                    act.activation(th[:, b % 2, :], ps[2 + b % 2][:, :], ACT.Tanh, scale=0.5)\
                       .then_inc(sem("tanh"), 1)
                    if b == 1:
                        act.wait_ge(sem("cw_turned"), s + 1)
                        act.activation(cwT[:, :], ps[1][0:E, :], ACT.Copy).then_inc(sem("cwT_ready"), 1)

            prepare(0)
            with act.Fori(0, NSEQ - 1) as s:
                main(s)
                prepare(s + 1)
            main(NSEQ - 1)

        @block.tensor
        def _(pe):
            pe.wait_ge(sem("ident"), 2)
            pe.wait_ge(sem("ones"), 7)
            pe.wait_ge(sem("weights"), WEIGHTS)

            def prepare(s):
                pe.wait_ge(sem("h_ready"), s + 1)
                for c in range(NC):
                    last = pe.transpose(ps[0][:, c * P:(c + 1) * P], h[:, c, :], ident[:, :])
                last.then_inc(sem("h_turned"), 1)
                pe.wait_ge(sem("hT_ready"), s + 1)
                for c in range(NC):
                    last = pe.matmul(ps[1][:, c * E:(c + 1) * E], hT[:, c * P:(c + 1) * P], gw[:, :],
                                     start=True, stop=True)
                last.then_inc(sem("logits"), 1)

            def up(s, b):
                if b >= 2:
                    pe.wait_ge(sem("gate_used"), NB * s + b - 1)
                pe.matmul(ps[2 + b % 2][:, :], wg[:, b, :], hT[:, :], start=True, stop=True)
                pe.matmul(ps[4 + b % 2][:, :], wu[:, b, :], hT[:, :], start=True, stop=True)\
                  .then_inc(sem("gate_up"), 1)

            def channels(s):
                up(s, 0)
                up(s, 1)
                pe.wait_ge(sem("cw_ready"), s + 1)
                for c in range(NC):
                    last = pe.transpose(ps[1][0:E, c * P:(c + 1) * P], cw[:, c, :], ident[:, :])
                last.then_inc(sem("cw_turned"), 1)
                pe.wait_ge(sem("cwT_ready"), s + 1)
                for b in range(NB):
                    if b >= 2:
                        up(s, b)
                        pe.wait_ge(sem("acted"), NB * s + b - 1)
                    pe.matmul(ps[6 + b % 2][:, :], spread[:, 2 * b:2 * b + 2, :].rearrange("e a i -> e (a i)"),
                              cwT[:, :], start=True, stop=True).then_inc(sem("cw_spread"), 1)
                up(s, NB)

            def down(s):
                pe.wait_ge(sem("all_acted"), s + 1)
                for c in range(NC):
                    for b in range(NB + 1):
                        last = pe.matmul(ps[0][:, c * P:(c + 1) * P], act_sb[:, b, c * P:(c + 1) * P], wd[:, b, :],
                                         start=(b == 0), stop=(b == NB))
                last.then_inc(sem("y_ready"), 1)

            prepare(0)
            with pe.Fori(0, NSEQ - 1) as s:
                channels(s)
                pe.wait_ge(sem("x_used"), s)
                prepare(s + 1)
                down(s)
            channels(NSEQ - 1)
            down(NSEQ - 1)

        @block.vector
        def _(dve):
            dve.wait_ge(sem("ones"), 7)
            dve.wait_ge(sem("weights"), WEIGHTS)

            def norm_sums(s, link):
                dve.wait_ge(sem("x_loaded"), 16 * s + 16)
                for c in range(NC):
                    last = dve.bn_stats(st[:, c, :], xt[:, c, :])
                link(last)
                dve.sem_inc(sem("passed"))
                for c in range(NC):
                    last = dve.bn_aggr(mv[:, c, :], st[:, c, :])
                link(last)
                dve.tensor_scalar(ve[:, :], mv[:, :, 1], LN_EPS, None, ALU.add).then_inc(sem("var_ready"), 1)

            def norm(s):
                dve.wait_ge(sem("rstd_ready"), s + 1)
                for c in range(NC):
                    last = dve.tensor_scalar(h[:, c, :], xt[:, c, :], mv[:, c, 0:1], rstd[:, c:c + 1],
                                             ALU.subtract, ALU.mult)
                last.then_inc(sem("h_ready"), 1)

            def route(s, link):
                dve.wait_ge(sem("ex_ready"), s + 1)
                link(dve.tensor_scalar(ex1[:, :, :], ex[:, :, :], 1.0, None, ALU.add))
                link(dve.reciprocal(score[:, :, :], ex1[:, :, :]))
                sf_e = sf[:, :, :].rearrange("p (c g) a -> p c (g a)", c=NC)
                link(dve.tensor_tensor(sf_e, score[:, :, :], bias[:, :].unsqueeze(1).to_broadcast([P, NC, E]), ALU.add))
                dve.tensor_tensor(hi[:, :, :], sf[:, :, 0:EG:2], sf[:, :, 1:EG:2], ALU.max)
                link(dve.tensor_tensor(lo[:, :, :], sf[:, :, 0:EG:2], sf[:, :, 1:EG:2], ALU.min))
                dve.tensor_tensor(top1[:, :], hi[:, :, 0], hi[:, :, 1], ALU.max)
                dve.tensor_tensor(mid[:, :], hi[:, :, 0], hi[:, :, 1], ALU.min)
                link(dve.tensor_tensor(lows[:, :], lo[:, :, 0], lo[:, :, 1], ALU.max))
                link(dve.tensor_tensor(mid[:, :], mid[:, :], lows[:, :], ALU.max))
                link(dve.tensor_tensor(gs[:, :, :].rearrange("p c g -> p (c g)"), top1[:, :], mid[:, :], ALU.add))

                def rank(gt, eq, values, before, n, out):
                    view = lambda t, c: t[:, c, :].rearrange("p (i j) -> p i j", i=n)
                    for c in range(NC):
                        other = values[:, c, :].unsqueeze(1).to_broadcast([P, n, n])
                        own = values[:, c, :].unsqueeze(2).to_broadcast([P, n, n])
                        dve.tensor_tensor(view(gt, c), other, own, ALU.is_gt)
                        last = dve.tensor_tensor(view(eq, c), other, own, ALU.is_equal)
                    link(last)
                    link(dve.tensor_tensor(eq[:, :, :], eq[:, :, :], before[:, :, :].rearrange("p i j -> p (i j)")
                                           .unsqueeze(1).to_broadcast([P, NC, n * n]), ALU.mult))
                    link(dve.tensor_tensor(gt[:, :, :], gt[:, :, :], eq[:, :, :], ALU.add))
                    link(dve.tensor_reduce(out, gt[:, :, :].rearrange("p c (i j) -> p (c i) j", i=n), AX_X, ALU.add))

                rank(ggt, geq, gs, before_g, NG, grank[:, :])
                link(dve.tensor_scalar(gin[:, :], grank[:, :], float(TG), None, ALU.is_lt))
                dve.tensor_scalar(gout[:, :], gin[:, :], BIG, -BIG, ALU.mult, ALU.add)
                sfm_g = sfm[:, :, :].rearrange("p c (g a) -> p (c g) a", a=EG)
                link(dve.tensor_tensor(sfm_g, sf[:, :, :], gin[:, :].unsqueeze(2).to_broadcast([P, NC * NG, EG]), ALU.mult))
                link(dve.tensor_tensor(sfm_g, sfm_g, gout[:, :].unsqueeze(2).to_broadcast([P, NC * NG, EG]), ALU.add))
                rank(egt, eeq, sfm, before_e, E, erank[:, :])
                link(dve.tensor_scalar(erank[:, :], erank[:, :], float(K), None, ALU.is_lt))
                link(dve.tensor_tensor(w[:, :, :], score[:, :, :], erank[:, :].rearrange("p (c e) -> p c e", e=E), ALU.mult))
                link(dve.tensor_reduce(wsum[:, :], w[:, :, :], AX_X, ALU.add))
                link(dve.tensor_scalar(wsum[:, :], wsum[:, :], 1e-20, None, ALU.add))
                link(dve.reciprocal(wrec[:, :], wsum[:, :]))
                link(dve.tensor_scalar(wrec[:, :], wrec[:, :], SCALE / 2, None, ALU.mult))
                dve.tensor_tensor(cw[:, :, :], w[:, :, :], wrec[:, :].unsqueeze(2).to_broadcast([P, NC, E]), ALU.mult)\
                   .then_inc(sem("cw_ready"), 1)

            def keep(s):
                dve.tensor_tensor(xh[:, :, :], xt[:, :, :], h[:, :, :], ALU.add).then_inc(sem("xh_ready"), 1)

            def channels(s, link, ahead=None):
                for b in range(NB + 1):
                    if ahead is not None and b == 2:
                        norm_sums(ahead, link)
                    if ahead is not None and b == 4:
                        norm(ahead)
                    dve.wait_ge(sem("tanh"), (NB + 1) * s + b + 1)
                    link(dve.scalar_tensor_tensor(out=gated[:, b % 2, :], in0=th[:, b % 2, :], scalar=1.0,
                                                  in1=ps[2 + b % 2][:, :], op0=ALU.add, op1=ALU.mult))
                    if b < NB:
                        dve.tensor_tensor(both[:, b % 2, :], gated[:, b % 2, :], ps[4 + b % 2][:, :], ALU.mult)\
                           .then_inc(sem("gate_used"), 1)
                        dve.wait_ge(sem("gate_used"), NB * s + b + 1)
                        dve.wait_ge(sem("cw_spread"), NB * s + b + 1)
                        dve.tensor_tensor(act_sb[:, b, :], both[:, b % 2, :], ps[6 + b % 2][:, :], ALU.mult)\
                           .then_inc(sem("acted"), 1)
                    else:
                        dve.scalar_tensor_tensor(out=act_sb[:, b, :], in0=gated[:, b % 2, :], scalar=0.5,
                                                 in1=ps[4 + b % 2][:, :], op0=ALU.mult, op1=ALU.mult)\
                           .then_inc(sem("all_acted"), 1)

            def residual(s):
                dve.wait_ge(sem("stored"), 16 * s)
                dve.wait_ge(sem("xh_ready"), s + 1)
                dve.wait_ge(sem("y_ready"), s + 1)
                dve.tensor_tensor(xo[:, :, :], xh[:, :, :], ps[0][:, :].rearrange("p (c d) -> p c d", c=NC), ALU.add)\
                   .then_inc(sem("x_used"), 1)

            first, _ = chain(dve, sem("first"), 0)
            norm_sums(0, first)
            norm(0)
            route(0, first)
            keep(0)
            with dve.Fori(0, NSEQ - 1) as s:
                link, links = chain(dve, sem("dve"), s * DVE_LINKS)
                channels(s, link, s + 1)
                route(s + 1, link)
                residual(s)
                dve.wait_ge(sem("x_used"), s + 1)
                keep(s + 1)
                assert links[0] == DVE_LINKS, links
            final, _ = chain(dve, sem("final"), 0)
            channels(NSEQ - 1, final)
            residual(NSEQ - 1)


CH = 64
NCH = SEQ // CH
NPAIR = NSEQ // 2
NSTEP = NPAIR * NCH
LEAD = 2
DH, DHD, DJ = 16, 64, 8
TAPS = 4
CHT = CH + TAPS - 1
GATES = 5 * DH


def pair_rows(x, p, b, q, n):
    return x[bass.ds(p * (2 * SEQ) + (b * SEQ + q * n * CH), n * CH), :].rearrange("(c t) d -> t c d", t=CH)


def gate_phase(nc, x_in, h_t, gates, w_ba, dt_bias, a_log):
    NC = 4
    DVE_LINKS = 7
    with ExitStack() as ctx:
        def sb(name, shape):
            return ctx.enter_context(nc.sbuf_tensor("g_" + name, shape, F32))
        sem = semaphores(nc, ctx, "g")
        ident = sb("ident", [P, P])
        upto = sb("upto", [P, 2, CH])
        after = sb("after", [P, 2, CH])
        of_seq = sb("of_seq", [P, 2, CH])
        mhalf = sb("mhalf", [P, NC])
        pad = sb("pad", [P, LEAD, 2, CHT])
        wba = sb("wba", [P, 2 * DH])
        dt = sb("dt", [P, DH])
        alog = sb("alog", [P, DH])
        neg_a = sb("neg_a", [P, DH])
        xt = sb("xt", [P, NC, D])
        h = sb("h", [P, NC, D])
        hT = sb("hT", [P, NC, 2, CH])
        st = sb("st", [P, NC, 6])
        mv = sb("mv", [P, NC, 2])
        ve = sb("ve", [P, NC])
        rstd = sb("rstd", [P, NC])
        eb = sb("eb", [P, NC, DH])
        ad = sb("ad", [P, NC, DH])
        aa = sb("aa", [P, NC, DH])
        ea = sb("ea", [P, NC, DH])
        la = sb("la", [P, NC, DH])
        gg = sb("gg", [P, NC, DH])
        out = sb("out", [P, NC, 5, DH])
        ps = [ctx.enter_context(nc.psum_tensor(f"g_ps{n}", [P, 512], F32)) for n in range(4)]
        block = ctx.enter_context(nc.Block())

        @block.sync
        def _(sp):
            sp.dma_start(wba[:, :], w_ba).then_inc(sem("weights"), 16)
            sp.dma_start(dt[:, :], dt_bias.partition_broadcast(P)).then_inc(sem("weights"), 16)
            sp.dma_start(alog[:, :], a_log.partition_broadcast(P)).then_inc(sem("weights"), 16)
            sp.wait_ge(sem("pad_ready"), 1)
            sp.dma_start(h_t[NSTEP:NSTEP + LEAD, :, :, :].rearrange("n d b t -> d n b t"), pad[:, :, :, :])\
              .then_inc(sem("padded"), 16)
            sp.dma_start(gates[NSTEP:NSTEP + LEAD, :, :].rearrange("n p f -> p n f"),
                         pad[:, :, :, :].rearrange("p n b t -> p n (b t)")[:, :, 0:GATES]).then_inc(sem("padded"), 16)
            for p in range(NPAIR):
                sp.dma_start(h_t[p * NCH, :, :, 0:TAPS - 1], pad[:, 0, :, 0:TAPS - 1]).then_inc(sem("padded"), 16)
            with sp.Fori(0, NPAIR) as p:
                for q in range(2):
                    u = 2 * p + q
                    sp.wait_ge(sem("h_ready"), u)
                    for b in range(2):
                        sp.dma_start(xt[64 * b:64 * b + 64, :, :], pair_rows(x_in, p, b, q, NC))\
                          .then_inc(sem("x_loaded"), 16)
                    sp.wait_ge(sem("hT_ready"), u + 1)
                    step = p * NCH + q * NC
                    ahead = NC - q
                    for b in range(2):
                        sp.dma_start(h_t[bass.ds(step, NC), :, b, TAPS - 1:CHT].rearrange("c d t -> d c t"),
                                     hT[:, :, b, :]).then_inc(sem("stored"), 16)
                        sp.dma_start(h_t[bass.ds(step + 1, ahead), :, b, 0:TAPS - 1].rearrange("c d t -> d c t"),
                                     hT[:, 0:ahead, b, CH - TAPS + 1:CH]).then_inc(sem("stored"), 16)
                    sp.wait_ge(sem("gates_ready"), u + 1)
                    sp.dma_start(gates[bass.ds(p * NCH + q * NC, NC), :, :].rearrange("c p f -> p c f"),
                                 out[:, :, :, :].rearrange("p c a h -> p c (a h)")).then_inc(sem("stored"), 16)
            sp.wait_ge(sem("stored"), 16 * 5 * 2 * NPAIR)
            sp.wait_ge(sem("padded"), 16 * (2 + NPAIR))

        @block.gpsimd
        def _(pool):
            make_identity(pool, ident, sem("ident"))
            link, _ = chain(pool, sem("setup"), 0)
            link(pool.memset(pad[:, :, :, :], 0.0))
            pool.sem_inc(sem("pad_ready"))
            link(pool.memset(mhalf[:, :], -0.5))
            for t in (upto, after, of_seq):
                link(pool.memset(t[:, :, :], 0.0))
                for b in range(2):
                    link(pool.memset(t[64 * b:64 * b + 64, b, :], 1.0))
            for b in range(2):
                own = slice(64 * b, 64 * b + 64)
                link(pool.affine_select(out=upto[own, b, :], in_=upto[own, b, :], compare_op=ALU.is_ge, fill=0.0,
                                        base=0, pattern=[[1, CH]], channel_multiplier=-1))
                link(pool.affine_select(out=after[own, b, :], in_=after[own, b, :], compare_op=ALU.is_gt, fill=0.0,
                                        base=0, pattern=[[-1, CH]], channel_multiplier=1))
            pool.sem_inc(sem("masks"))
            with pool.Fori(0, 2 * NPAIR) as u:
                pool.wait_ge(sem("var_ready"), u + 1)
                pool.tensor_tensor(rstd[:, :], ve[:, :], mhalf[:, :], ALU.pow).then_inc(sem("rstd_ready"), 1)

        @block.scalar
        def _(act):
            act.wait_ge(sem("alog_ready"), 1)
            act.activation(neg_a[:, :], alog[:, :], ACT.Exp).then_inc(sem("a_ready"), 1)
            with act.Fori(0, 2 * NPAIR) as u:
                act.wait_ge(sem("h_turned"), u + 1)
                act.wait_ge(sem("stored"), 80 * u)
                act.activation(hT[:, :, :, :].rearrange("p c b t -> p (c b t)"), ps[0][:, :], ACT.Copy)\
                   .then_inc(sem("hT_ready"), 1)
                act.wait_ge(sem("ba_ready"), u + 1)
                act.activation(eb[:, :, :], ps[1][:, 0:NC * 2 * DH].rearrange("p (c e) -> p c e", c=NC)[:, :, 0:DH],
                               ACT.Exp, scale=-1.0).then_inc(sem("eb_ready"), 1)
                act.wait_ge(sem("aa_ready"), u + 1)
                act.activation(ea[:, :, :], aa[:, :, :], ACT.Exp, scale=-1.0).then_inc(sem("act"), 1)
                act.wait_ge(sem("act"), 2 * u + 1)
                act.activation(la[:, :, :], ea[:, :, :], ACT.Ln, bias=1.0).then_inc(sem("act"), 1)
                act.wait_ge(sem("sums_ready"), u + 1)
                act.activation(out[:, :, 2, :], ps[2][:, 0:NC * DH].rearrange("p (c h) -> p c h", c=NC), ACT.Exp)
                act.activation(out[:, :, 3, :], ps[2][:, NC * DH:2 * NC * DH].rearrange("p (c h) -> p c h", c=NC),
                               ACT.Exp)
                for b in range(2):
                    last = act.activation(out[:, :, 4, b * DJ:(b + 1) * DJ],
                                          ps[3][:, b * NC * DJ:(b + 1) * NC * DJ].rearrange("p (c j) -> p c j", c=NC),
                                          ACT.Exp)
                last.then_inc(sem("gates_ready"), 1)

        @block.tensor
        def _(pe):
            pe.wait_ge(sem("ident"), 2)
            pe.wait_ge(sem("masks"), 1)
            pe.wait_ge(sem("weights"), 48)
            with pe.Fori(0, 2 * NPAIR) as u:
                pe.wait_ge(sem("h_ready"), u + 1)
                for c in range(NC):
                    last = pe.transpose(ps[0][:, c * P:(c + 1) * P], h[:, c, :], ident[:, :])
                last.then_inc(sem("h_turned"), 1)
                pe.wait_ge(sem("hT_ready"), u + 1)
                for c in range(NC):
                    last = pe.matmul(ps[1][:, c * 2 * DH:(c + 1) * 2 * DH], hT[:, c, :, :].rearrange("p b t -> p (b t)"),
                                     wba[:, :], start=True, stop=True)
                last.then_inc(sem("ba_ready"), 1)
                pe.wait_ge(sem("g_ready"), u + 1)
                flat = gg[:, :, :].rearrange("p c h -> p (c h)")
                pe.matmul(ps[2][:, 0:NC * DH], upto[:, :, :].rearrange("p b t -> p (b t)"), flat, start=True, stop=True)
                pe.matmul(ps[2][:, NC * DH:2 * NC * DH], after[:, :, :].rearrange("p b t -> p (b t)"), flat,
                          start=True, stop=True)
                for g in range(2):
                    for b in range(2):
                        last = pe.matmul(ps[3][64 * g:64 * g + 64, b * NC * DJ:(b + 1) * NC * DJ],
                                         of_seq[:, :, :].rearrange("p b t -> p t b")[:, :, b],
                                         gg[:, :, :].rearrange("p c (j g) -> p c j g", g=2)[:, :, :, g],
                                         start=True, stop=True)
                last.then_inc(sem("sums_ready"), 1)

        @block.vector
        def _(dve):
            dve.wait_ge(sem("weights"), 48)
            dve.tensor_scalar(alog[:, :], alog[:, :], -2.3, None, ALU.max).then_inc(sem("alog_ready"), 1)
            dve.wait_ge(sem("a_ready"), 1)
            dve.tensor_scalar(neg_a[:, :], neg_a[:, :], -1.0, None, ALU.mult).then_inc(sem("a_ready"), 1)
            dve.wait_ge(sem("a_ready"), 2)
            with dve.Fori(0, 2 * NPAIR) as u:
                link, links = chain(dve, sem("dve"), u * DVE_LINKS)
                dve.wait_ge(sem("x_loaded"), 32 * u + 32)
                for c in range(NC):
                    last = dve.bn_stats(st[:, c, :], xt[:, c, :])
                link(last)
                dve.sem_inc(sem("passed"))
                for c in range(NC):
                    last = dve.bn_aggr(mv[:, c, :], st[:, c, :])
                link(last)
                dve.tensor_scalar(ve[:, :], mv[:, :, 1], LN_EPS, None, ALU.add).then_inc(sem("var_ready"), 1)
                dve.wait_ge(sem("rstd_ready"), u + 1)
                for c in range(NC):
                    last = dve.tensor_scalar(h[:, c, :], xt[:, c, :], mv[:, c, 0:1], rstd[:, c:c + 1],
                                             ALU.subtract, ALU.mult)
                last.then_inc(sem("h_ready"), 1)
                dve.wait_ge(sem("ba_ready"), u + 1)
                dve.wait_ge(sem("eb_ready"), u + 1)
                link(dve.tensor_tensor(ad[:, :, :],
                                       ps[1][:, 0:NC * 2 * DH].rearrange("p (c e) -> p c e", c=NC)[:, :, DH:2 * DH],
                                       dt[:, :].unsqueeze(1).to_broadcast([P, NC, DH]), ALU.add))
                dve.scalar_tensor_tensor(out=aa[:, :, :], in0=ad[:, :, :], scalar=-1.0, in1=ad[:, :, :],
                                         op0=ALU.mult, op1=ALU.max).then_inc(sem("aa_ready"), 1)
                link(dve.tensor_scalar(eb[:, :, :], eb[:, :, :], 1.0, None, ALU.add))
                dve.wait_ge(sem("stored"), 80 * u)
                link(dve.reciprocal(out[:, :, 0, :], eb[:, :, :]))
                dve.wait_ge(sem("act"), 2 * u + 2)
                link(dve.scalar_tensor_tensor(out=gg[:, :, :], in0=ad[:, :, :], scalar=0.0, in1=la[:, :, :],
                                              op0=ALU.max, op1=ALU.add))
                link(dve.tensor_tensor(gg[:, :, :], gg[:, :, :], neg_a[:, :].unsqueeze(1).to_broadcast([P, NC, DH]),
                                       ALU.mult))
                dve.tensor_copy(out[:, :, 1, :], gg[:, :, :]).then_inc(sem("g_ready"), 1)
                assert links[0] == DVE_LINKS, links


SB = 16
NBLK = P // SB


def delta_phase(nc, x_in, x_out, h_t, gates, a_blocks, t_blocks, w_in, conv_t, norm_w, w_o):
    KV = DH * DHD
    HH = DH // 2
    HB = CH // 2
    DVE_LINKS = 12
    POOL_LINKS = 2 * SB - 1
    L2_EPS, RMS_EPS = 1e-6, 1e-6
    HALVES = range(2)
    SEQS = range(2)
    BLOCKS = [(b, u) for b in SEQS for u in range(2)]

    with ExitStack() as ctx:
        def sb(name, shape):
            return ctx.enter_context(nc.sbuf_tensor("d_" + name, shape, F32))
        sem = semaphores(nc, ctx, "d")
        ident = sb("ident", [P, P])
        later = sb("later", [P, 2, CH])
        upto = sb("upto", [P, CH])
        hk = sb("hk", [P, 2])
        hi = sb("hi", [P, 1])
        lo = sb("lo", [P, 1])
        powers = sb("powers", [P, 2, DH])
        mhalf = sb("mhalf", [P, DH])
        taps = sb("taps", [P, TAPS, 3 * KV])
        cwb = sb("cwb", [P, 3 * KV])
        wz = sb("wz", [P, KV])
        wo = sb("wo", [P, DJ, D])
        nw = sb("nw", [P, DHD])
        hx = sb("hx", [P, 2, CHT])
        hs = sb("hs", [P, TAPS, P])
        gin = sb("gin", [P, GATES])
        gt = sb("gt", [P, 5, DH])
        xt = sb("xt", [P, D])
        xo = sb("xo", [P, D])
        th = sb("th", [P, 2, 512])
        kqT = sb("kqT", [P, DJ, 4 * CH])
        kT = sb("kT", [P, DJ, P])
        ktok = sb("ktok", [P, KV])
        v = sb("v", [P, KV])
        z = sb("z", [P, KV])
        sq = sb("sq", [P, KV])
        n4 = sb("n4", [P, 2, DH])
        nr = sb("nr", [P, 2, DH])
        nq = sb("nq", [P, DH])
        wr_now = sb("wr_now", [P, DH])
        ktok_now = sb("ktok_now", [P, KV])
        qk_now = sb("qk_now", [P, DH, CH])
        cc = sb("cc", [P, DH])
        wr = sb("wr", [P, DH])
        gU = sb("gU", [P, DH, CH])
        dd = sb("dd", [P, DH, CH])
        ddm = sb("ddm", [P, DH, CH])
        at = sb("at", [P, DH, CH])
        qk = sb("qk", [P, DH, CH])
        ablk = sb("ablk", [P, SB, SB])
        tblk = sb("tblk", [P, 2, SB, SB])
        one = sb("one", [P, SB, SB])
        prod = sb("prod", [P, SB, SB])
        ti = sb("ti", [P, DH, HB])
        tt = sb("tt", [P, DH, CH])
        w4 = sb("w4", [P, DH, HB])
        w5 = sb("w5", [P, DH, HB])
        state = sb("state", [P, 2, DJ, 2, DHD])
        faded = sb("faded", [P, 2, DJ, DHD])
        r = sb("r", [P, KV])
        y = sb("y", [P, KV])
        yw = sb("yw", [P, KV])
        oi = sb("oi", [P, KV])
        o = sb("o", [P, KV])
        yT = sb("yT", [P, DJ, P])
        ms = sb("ms", [P, DH])
        f = sb("f", [P, DH])
        f2 = sb("f2", [P, DH])
        pa = ctx.enter_context(nc.psum_tensor("d_pa", [P, 2, 512], F32))
        pb = ctx.enter_context(nc.psum_tensor("d_pb", [P, 2, 512], F32))
        pc = ctx.enter_context(nc.psum_tensor("d_pc", [P, 4, 512], F32))
        sq2 = r

        def rows_of(b, u=None):
            return slice(64 * b, 64 * b + 64) if u is None else slice(64 * b + HB * u, 64 * b + HB * u + HB)

        def heads(t):
            return t[:, :].rearrange("p (h d) -> p h d", d=DHD)

        def half(m):
            return slice(HH * m, HH * m + HH)

        def spread(t, n=DHD):
            return t.unsqueeze(2).to_broadcast([t.shape[0], t.shape[1], n])

        block = ctx.enter_context(nc.Block())
        WEIGHTS = 16 * 4

        @block.sync
        def _(sp):
            sp.dma_start(taps[:, TAPS - 1, :], w_in[:, 0:3 * KV]).then_inc(sem("weights"), 16)
            sp.dma_start(wz[:, :], w_in[:, 3 * KV:4 * KV]).then_inc(sem("weights"), 16)
            sp.dma_start(wo[:, :, :], w_o.rearrange("(j m) d -> m j d", m=P)).then_inc(sem("weights"), 16)
            sp.dma_start(nw[:, :], norm_w.partition_broadcast(P)).then_inc(sem("weights"), 16)
            for j in range(TAPS):
                if j:
                    sp.wait_ge(sem("tap_scaled"), j)
                sp.dma_start(cwb[:, :], conv_t[j, :].partition_broadcast(P)).then_inc(sem("filter"), 16)

            def load(k):
                sp.dma_start(hx[:, :, :], h_t[bass.ds(k, 1), :, :, :].rearrange("o d b t -> d (o b) t"))\
                  .then_inc(sem("h_loaded"), 16)
                sp.dma_start(gin[:, :], gates[bass.ds(k, 1), :, :].rearrange("o p f -> p (o f)"))\
                  .then_inc(sem("gates_loaded"), 16)

            def exchange(k):
                sp.wait_ge(sem("at_ready"), 2 * k + 2)
                for n in range(NBLK):
                    c0 = SB * (n % (CH // SB))
                    sp.dma_start(a_blocks[n, :, :, :].rearrange("h s t -> s h t"),
                                 at[SB * n:SB * n + SB, :, c0:c0 + SB]).then_inc(sem("a_stored"), 16)
                sp.wait_ge(sem("a_stored"), 16 * NBLK * (k + 1))
                sp.dma_start(ablk[:, :, :], a_blocks.rearrange("n h s t -> (n h) s t")).then_inc(sem("a_loaded"), 16)
                sp.wait_ge(sem("turned_back"), k + 1)
                sp.dma_start(t_blocks.rearrange("n h a r c -> (n h) a r c"), tblk[:, :, :, :]).then_inc(sem("t_stored"), 16)
                sp.wait_ge(sem("t_stored"), 16 * (k + 1))
                sp.wait_ge(sem("solved"), 2 * k)
                for n in range(NBLK):
                    rows, c0, c1 = slice(SB * n, SB * n + SB), SB * (n % (CH // SB)), SB * (n % (HB // SB))
                    sp.dma_start(ti[rows, :, c1:c1 + SB], t_blocks[n, :, 1, :, :].rearrange("h r c -> r h c"))\
                      .then_inc(sem("t_loaded"), 16)
                    sp.dma_start(tt[rows, :, c0:c0 + SB], t_blocks[n, :, 0, :, :].rearrange("h r c -> r h c"))\
                      .then_inc(sem("t_loaded"), 16)

            load(0)
            sp.wait_ge(sem("shifted"), 1)
            sp.wait_ge(sem("gates_taken"), 1)
            load(1)
            sp.wait_ge(sem("constants"), 1)
            exchange(0)
            with sp.Fori(0, NPAIR) as p:
                with sp.Fori(0, NCH) as c:
                    i = p * NCH + c
                    sp.wait_ge(sem("x_used"), i)
                    for b in SEQS:
                        sp.dma_start(xt[rows_of(b), :], x_in[bass.ds(p * (2 * SEQ) + c * CH + b * SEQ, CH), :])\
                          .then_inc(sem("x_loaded"), 16)
                    sp.wait_ge(sem("shifted"), i + 2)
                    sp.wait_ge(sem("gates_taken"), i + 2)
                    load(i + 2)
                    exchange(i + 1)
                    sp.wait_ge(sem("x_used"), i + 1)
                    for b in SEQS:
                        sp.dma_start(x_out[bass.ds(p * (2 * SEQ) + c * CH + b * SEQ, CH), :], xo[rows_of(b), :])\
                          .then_inc(sem("stored"), 16)
            sp.wait_ge(sem("stored"), 32 * NSTEP)
            sp.wait_ge(sem("t_loaded"), 32 * NBLK * (NSTEP + 1))

        @block.gpsimd
        def _(pool):
            make_identity(pool, ident, sem("ident"))
            link, _ = chain(pool, sem("setup"), 0)
            link(pool.memset(mhalf[:, :], -0.5))
            link(pool.memset(powers[:, 0, :], 0.5))
            link(pool.memset(powers[:, 1, :], -0.5))
            link(pool.memset(later[:, :, :], 0.0))
            link(pool.memset(upto[:, :], 1.0))
            link(pool.memset(hk[:, :], 1.0))
            for t in (tt, ti, w4, w5):
                link(pool.memset(t[:, :, :], 0.0))
            for b in SEQS:
                own = rows_of(b)
                link(pool.memset(later[own, b, :], 1.0))
                link(pool.affine_select(out=later[own, b, :], in_=later[own, b, :], compare_op=ALU.is_gt, fill=0.0,
                                        base=0, pattern=[[-1, CH]], channel_multiplier=1))
                link(pool.affine_select(out=upto[own, :], in_=upto[own, :], compare_op=ALU.is_ge, fill=0.0,
                                        base=0, pattern=[[1, CH]], channel_multiplier=-1))
                link(pool.affine_select(out=hk[own, :], in_=hk[own, :], compare_op=ALU.is_ge, fill=0.0, base=-SB,
                                        pattern=[[-HB, 2]], channel_multiplier=1))
                link(pool.affine_select(out=hk[own, :], in_=hk[own, :], compare_op=ALU.is_ge, fill=0.0, base=HB - 1,
                                        pattern=[[HB, 2]], channel_multiplier=-1))
            link(pool.memset(one[:, :, :], 0.0))
            link(pool.affine_select(out=one[:, :, :], in_=one[:, :, :], compare_op=ALU.not_equal, fill=1.0,
                                    base=0, pattern=[[-1, SB], [1, SB]], channel_multiplier=0))
            link(pool.tensor_tensor(hi[:, :], hk[:, 0:1], hk[:, 1:2], ALU.add))
            link(pool.memset(lo[:, :], 1.0))
            link(pool.tensor_tensor(lo[:, :], lo[:, :], hi[:, :], ALU.subtract))
            pool.sem_inc(sem("constants"))

            def exponent_terms(k):
                pool.wait_ge(sem("gates_taken"), k + 1)
                pool.tensor_tensor(gU[:, :, :], spread(gt[:, 1, :], CH), upto[:, :].unsqueeze(1).to_broadcast([P, DH, CH]),
                                   ALU.mult).then_inc(sem("gU_ready"), 1)

            def masked_decays(k):
                for m in HALVES:
                    pool.wait_ge(sem("dd_ready"), 2 * k + m + 1)
                    pool.tensor_tensor(ddm[:, half(m), :], dd[:, half(m), :],
                                       upto[:, :].unsqueeze(1).to_broadcast([P, HH, CH]), ALU.mult)\
                        .then_inc(sem("ddm_ready"), 1)

            def norms(k):
                pool.wait_ge(sem("n4_ready"), k + 1)
                pool.tensor_tensor(nr[:, :, :], n4[:, :, :], powers[:, :, :], ALU.pow).then_inc(sem("nr_ready"), 1)

            def substitute(k, link):
                pool.wait_ge(sem("t_stored"), 16 * k)
                pool.sem_inc(sem("passed_pool"))
                link(pool.tensor_copy(tblk[:, 0, :, :], one[:, :, :]))
                pool.wait_ge(sem("a_loaded"), 16 * k + 16)
                for s in range(SB - 1):
                    n = SB - 1 - s
                    link(pool.tensor_tensor(prod[:, 0:s + 1, 0:n],
                                            tblk[:, 0, 0:s + 1, s].unsqueeze(2).to_broadcast([P, s + 1, n]),
                                            ablk[:, s, s + 1:SB].unsqueeze(1).to_broadcast([P, s + 1, n]), ALU.mult))
                    link(pool.tensor_tensor(tblk[:, 0, 0:s + 1, s + 1:SB], tblk[:, 0, 0:s + 1, s + 1:SB],
                                            prod[:, 0:s + 1, 0:n], ALU.subtract))
                pool.sem_inc(sem("passed_pool"))
                pool.tensor_copy(tblk[:, 1, :, :], tblk[:, 0, :, :].rearrange("p c s -> p s c"))\
                    .then_inc(sem("turned_back"), 1)

            def finish(k):
                pool.wait_ge(sem("proj_used"), 8 * k + 8)
                pool.tensor_tensor(heads(z), heads(z), nw[:, :].unsqueeze(1).to_broadcast([P, DH, DHD]), ALU.mult)\
                    .then_inc(sem("z_ready"), 1)

            pool.wait_ge(sem("nw_halved"), 1)
            exponent_terms(0)
            masked_decays(0)
            norms(0)
            first, _ = chain(pool, sem("first_pool"), 0)
            substitute(0, first)
            finish(0)
            with pool.Fori(0, NPAIR) as p:
                with pool.Fori(0, NCH) as c:
                    i = p * NCH + c
                    k = i + 1
                    pool.wait_ge(sem("qs_taken"), i + 1)
                    pool.tensor_tensor(heads(oi), heads(oi), spread(gt[:, 2, :]), ALU.mult).then_inc(sem("oi_ready"), 1)
                    pool.wait_ge(sem("t_loaded"), 32 * NBLK * (i + 1))
                    pool.tensor_tensor(ti[:, :, 0:SB], ti[:, :, 0:SB],
                                       lo[:, :].unsqueeze(2).to_broadcast([P, DH, SB]), ALU.mult)\
                        .then_inc(sem("ti_clean"), 1)
                    exponent_terms(k)
                    masked_decays(k)
                    for m in HALVES:
                        pool.wait_ge(sem("y_ready"), 2 * i + m + 1)
                        pool.tensor_tensor(heads(yw)[:, half(m), :], heads(y)[:, half(m), :],
                                           spread(wr_now[:, half(m)]), ALU.mult).then_inc(sem("yw_ready"), 1)
                    norms(k)
                    pool.wait_ge(sem("ms_ready"), i + 1)
                    pool.tensor_tensor(f[:, :], ms[:, :], mhalf[:, :], ALU.pow).then_inc(sem("f_ready"), 1)
                    link, links = chain(pool, sem("pool"), i * POOL_LINKS)
                    substitute(k, link)
                    assert links[0] == POOL_LINKS, links
                    finish(k)

        @block.scalar
        def _(act):
            turned = pa[:, :, :].rearrange("p a c -> p (a c)")

            def shift(k):
                act.wait_ge(sem("h_loaded"), 16 * k + 16)
                act.wait_ge(sem("projected"), 8 * k)
                for t in range(TAPS):
                    last = act.activation(hs[:, t, :].rearrange("p (b t) -> p b t", b=2), hx[:, :, t:t + CH], ACT.Copy)
                last.then_inc(sem("shifted"), 1)

            def tanh(k, n):
                act.wait_ge(sem("projected"), 8 * k + n + 1)
                if n >= 2:
                    act.wait_ge(sem("proj_used"), 8 * k + n - 1)
                else:
                    act.wait_ge(sem("proj_used"), 8 * k)
                act.activation(th[:, n % 2, :], pa[:, n % 2, :], ACT.Tanh, scale=0.5).then_inc(sem("tanh"), 1)

            def decays(k):
                act.wait_ge(sem("exponents"), k + 1)
                for m in HALVES:
                    act.activation(dd[:, half(m), :], pa[:, m, :].rearrange("p (h t) -> p h t", t=CH), ACT.Exp)\
                       .then_inc(sem("decays"), 1)

            def place_k(k):
                act.wait_ge(sem("proj_used"), 8 * k + 4)
                act.activation(kqT[:, :, :].rearrange("p j (a t) -> p j a t", t=CH)[:, :, 0:4:3, :],
                               kT[:, :, :].rearrange("p j (b t) -> p j b t", b=2), ACT.Copy).then_inc(sem("k_placed"), 1)

            def square_q(k):
                act.wait_ge(sem("kq_turned"), 2 * k + 1)
                act.activation(sq[:, :], turned, ACT.Square).then_inc(sem("squared"), 1)

            def take_k(k):
                act.wait_ge(sem("kq_turned"), 2 * k + 2)
                act.wait_ge(sem("kept"), k)
                act.activation(ktok[:, :], turned, ACT.Copy)
                act.wait_ge(sem("q_summed"), k + 1)
                act.activation(sq[:, :], turned, ACT.Square).then_inc(sem("squared"), 1)

            shift(0)
            for n in range(4):
                tanh(0, n)
            decays(0)
            place_k(0)
            square_q(0)
            take_k(0)
            for n in range(4, 8):
                tanh(0, n)
            with act.Fori(0, NPAIR) as p:
                with act.Fori(0, NCH) as c:
                    i = p * NCH + c
                    k = i + 1
                    shift(k)
                    act.activation(ktok_now[:, :], ktok[:, :], ACT.Copy)
                    act.wait_ge(sem("qk_read"), 2 * k)
                    act.activation(qk_now[:, :, :], qk[:, :, :], ACT.Copy).then_inc(sem("kept"), 1)
                    for b in SEQS:
                        act.wait_ge(sem("ks"), 2 * i + b + 1)
                        last = act.activation(oi[rows_of(b), :], pc[rows_of(1 - b), 2 * b:2 * b + 2, :]
                                              .rearrange("p a c -> p (a c)"), ACT.Copy)
                    last.then_inc(sem("qs_taken"), 1)
                    for n in range(4):
                        tanh(k, n)
                    decays(k)
                    place_k(k)
                    act.wait_ge(sem("w5_sum"), i + 1)
                    for b in SEQS:
                        last = act.activation(w5[rows_of(b, 1), :, :],
                                              pb[rows_of(b, 1), 0, :].rearrange("p (h c) -> p h c", c=HB), ACT.Copy)
                    last.then_inc(sem("w5_ready"), 1)
                    act.wait_ge(sem("t5_sum"), i + 1)
                    for b in SEQS:
                        last = act.activation(tt[rows_of(b, 0), :, HB:CH],
                                              pb[rows_of(b, 0), 1, :].rearrange("p (h c) -> p h c", c=HB), ACT.Copy,
                                              scale=-1.0)
                    last.then_inc(sem("tt_ready"), 1)
                    square_q(k)
                    for m in HALVES:
                        act.wait_ge(sem("solved"), 2 * i + m + 1)
                        act.activation(y[:, m * 512:(m + 1) * 512], pc[:, m, :], ACT.Copy).then_inc(sem("y_ready"), 1)
                    take_k(k)
                    act.wait_ge(sem("o_ready"), i + 1)
                    act.activation(sq2[:, :], o[:, :], ACT.Square).then_inc(sem("o_squared"), 1)
                    tanh(k, 4)
                    tanh(k, 5)
                    for n in range(2):
                        act.wait_ge(sem("o_turned"), 2 * i + n + 1)
                        act.activation(yT[:, 4 * n:4 * n + 4, :],
                                       pc[:, 2 + n, :].rearrange("p (j t) -> p j t", j=4), ACT.Copy)\
                           .then_inc(sem("yT_ready"), 1)
                    tanh(k, 6)
                    tanh(k, 7)

        @block.tensor
        def _(pe):
            def hold(s, value):
                pe.wait_ge(s, value)
                pe.sem_inc(sem("passed"))

            def project(k, n):
                if n == 0:
                    pe.wait_ge(sem("shifted"), k + 1)
                    pe.wait_ge(sem("proj_used"), 8 * k)
                elif n in (2, 3, 6, 7):
                    pe.wait_ge(sem("proj_used"), 8 * k + n - 1)
                elif n == 4:
                    pe.wait_ge(sem("squared"), 2 * k + 2)
                if n < 4:
                    for jj in range(4):
                        for t in range(TAPS):
                            ch = n * 512 + jj * P
                            last = pe.matmul(pa[:, n % 2, jj * P:(jj + 1) * P], taps[:, t, ch:ch + P],
                                             hs[:, t, :], start=(t == 0), stop=(t == TAPS - 1))
                elif n < 6:
                    for t in range(TAPS):
                        ch = n * 512
                        last = pe.matmul(pa[:, n % 2, :], hs[:, t, :], taps[:, t, ch:ch + 512],
                                         start=(t == 0), stop=(t == TAPS - 1))
                else:
                    last = pe.matmul(pa[:, n % 2, :], hs[:, TAPS - 1, :],
                                     wz[:, (n - 6) * 512:(n - 5) * 512], start=True, stop=True)
                last.then_inc(sem("projected"), 1)

            def exponents(k):
                pe.wait_ge(sem("gU_ready"), k + 1)
                pe.wait_ge(sem("proj_used"), 8 * k + 4)
                for m in HALVES:
                    last = pe.matmul(pa[:, m, :], later[:, :, :].rearrange("p b s -> p (b s)"),
                                     gU[:, half(m), :].rearrange("p h t -> p (h t)"), start=True, stop=True)
                last.then_inc(sem("exponents"), 1)

            def turn_q(k):
                pe.wait_ge(sem("decays"), 2 * k + 2)
                for j in range(DJ):
                    last = pe.transpose(pa[:, j // 4, (j % 4) * P:(j % 4 + 1) * P], kqT[:, j, CH:3 * CH], ident[:, :])
                last.then_inc(sem("kq_turned"), 1)

            def turn_k(k):
                pe.wait_ge(sem("squared"), 2 * k + 1)
                for j in range(DJ):
                    last = pe.transpose(pa[:, j // 4, (j % 4) * P:(j % 4 + 1) * P], kT[:, j, :], ident[:, :])
                last.then_inc(sem("kq_turned"), 1)

            def kkq(k, m):
                if m == 0:
                    hold(sem("k_placed"), k + 1)
                    hold(sem("tt_ready"), k)
                else:
                    hold(sem("qk_read"), 2 * k + 1)
                for h in range(HH * m, HH * m + HH):
                    j, g = h // 2, h % 2
                    rows = slice(64 * g, 64 * g + 64)
                    for b in SEQS:
                        last = pe.matmul(pb[rows_of(b), g, (j % 4) * P:(j % 4 + 1) * P],
                                         kqT[rows, j, 3 * CH * b:3 * CH * b + CH], kqT[rows, j, P * b:P * b + P],
                                         start=True, stop=True)
                last.then_inc(sem("kkq"), 1)

            pe.wait_ge(sem("ident"), 2)
            pe.wait_ge(sem("constants"), 1)
            pe.wait_ge(sem("weights_ready"), 1)
            for n in range(4):
                project(0, n)
            exponents(0)
            turn_q(0)
            kkq(0, 0)
            turn_k(0)
            project(0, 4)
            project(0, 5)
            kkq(0, 1)
            project(0, 6)
            project(0, 7)
            with pe.Fori(0, NPAIR) as p:
                with pe.Fori(0, NCH) as c:
                    i = p * NCH + c
                    k = i + 1
                    pe.wait_ge(sem("state_ready"), 9 * p + c + 1)
                    pe.wait_ge(sem("x_used"), i)
                    for b in SEQS:
                        for j in range(DJ):
                            last = pe.matmul(pc[:, 2 * b + j // 4, (j % 4) * P:(j % 4 + 1) * P],
                                             kqT[:, j, P * b:P * b + P],
                                             state[:, b, j, :, :].rearrange("p g d -> p (g d)"), start=True, stop=True)
                        last.then_inc(sem("ks"), 1)
                    project(k, 0)
                    project(k, 1)
                    project(k, 2)
                    hold(sem("qk_read"), 2 * i + 2)
                    hold(sem("ti_clean"), i + 1)
                    for h in range(DH):
                        for b, u in BLOCKS:
                            rows = rows_of(b, u)
                            last = pe.matmul(pb[rows, 0, h * SB:(h + 1) * SB], at[rows, h, HB * u:HB * u + HB],
                                             ti[rows, h, 0:SB], start=True, stop=True)
                    last.then_inc(sem("w4_sum"), 1)
                    project(k, 3)
                    hold(sem("w4_ready"), i + 1)
                    for h in range(DH):
                        for b in SEQS:
                            rows = rows_of(b, 0)
                            last = pe.matmul(pb[rows, 1, h * SB:(h + 1) * SB], tt[rows, h, 0:HB], w4[rows, h, 0:SB],
                                             start=True, stop=True)
                        for b, u in BLOCKS:
                            rows = rows_of(b, u)
                            last = pe.matmul(pb[rows, 1, (DH + h) * SB:(DH + h + 1) * SB], w4[rows, h, :],
                                             tt[rows, h, HB * u + SB:HB * u + HB], start=True, stop=True)
                    last.then_inc(sem("t4_sum"), 1)
                    exponents(k)
                    hold(sem("t4_ready"), i + 1)
                    for h in range(DH):
                        for b in SEQS:
                            last = pe.matmul(pb[rows_of(b, 1), 0, h * HB:(h + 1) * HB], at[rows_of(b, 0), h, HB:CH],
                                             ti[rows_of(b, 0), h, :], start=True, stop=True)
                    last.then_inc(sem("w5_sum"), 1)
                    turn_q(k)
                    hold(sem("w5_ready"), i + 1)
                    for h in range(DH):
                        for b in SEQS:
                            last = pe.matmul(pb[rows_of(b, 0), 1, h * HB:(h + 1) * HB], w5[rows_of(b, 1), h, :],
                                             tt[rows_of(b, 1), h, HB:CH], start=True, stop=True)
                    last.then_inc(sem("t5_sum"), 1)
                    hold(sem("r_ready"), i + 1)
                    hold(sem("qs_taken"), i + 1)
                    hold(sem("tt_ready"), i + 1)
                    for m in HALVES:
                        for h in range(HH * m, HH * m + HH):
                            for b in SEQS:
                                last = pe.matmul(pc[rows_of(b), m, (h % HH) * DHD:(h % HH + 1) * DHD],
                                                 tt[rows_of(b), h, :], r[rows_of(b), h * DHD:(h + 1) * DHD],
                                                 start=True, stop=True)
                        last.then_inc(sem("solved"), 1)
                    turn_k(k)
                    kkq(k, 0)
                    hold(sem("kept"), i + 1)
                    for m in HALVES:
                        hold(sem("y_ready"), 2 * i + m + 1)
                        for h in range(HH * m, HH * m + HH):
                            for b in SEQS:
                                last = pe.matmul(pc[rows_of(b), 2 + m, (h % HH) * DHD:(h % HH + 1) * DHD],
                                                 qk_now[rows_of(b), h, :], y[rows_of(b), h * DHD:(h + 1) * DHD],
                                                 start=True, stop=True)
                        last.then_inc(sem("o_sum"), 1)
                    kkq(k, 1)
                    hold(sem("o_ready"), i + 1)
                    for m in HALVES:
                        hold(sem("yw_ready"), 2 * i + m + 1)
                        for j in range(4 * m, 4 * m + 4):
                            for b in SEQS:
                                last = pe.matmul(pc[:, 2 * b + m, (j % 4) * P:(j % 4 + 1) * P],
                                                 ktok_now[rows_of(b), j * P:(j + 1) * P], yw[rows_of(b), j * P:(j + 1) * P],
                                                 start=True, stop=True)
                    last.then_inc(sem("update"), 1)
                    project(k, 4)
                    project(k, 5)
                    pe.wait_ge(sem("on_ready"), i + 1)
                    for n in range(2):
                        for jj in range(4):
                            j = 4 * n + jj
                            last = pe.transpose(pc[:, 2 + n, jj * P:(jj + 1) * P], o[:, j * P:(j + 1) * P], ident[:, :])
                        last.then_inc(sem("o_turned"), 1)
                    project(k, 6)
                    pe.wait_ge(sem("yT_ready"), 2 * i + 2)
                    pe.wait_ge(sem("state_ready"), 9 * p + c + 2)
                    for j in range(DJ):
                        last = pe.matmul(pc[:, 0, 0:D], yT[:, j, :], wo[:, j, :], start=(j == 0), stop=(j == DJ - 1))
                    last.then_inc(sem("out_ready"), 1)
                    project(k, 7)

        @block.vector
        def _(dve):
            dve.wait_ge(sem("weights"), WEIGHTS)
            for j in range(TAPS):
                dve.wait_ge(sem("filter"), 16 * j + 16)
                dve.tensor_tensor(taps[:, j, :], taps[:, TAPS - 1, :], cwb[:, :], ALU.mult).then_inc(sem("tap_scaled"), 1)
            dve.tensor_scalar(nw[:, :], nw[:, :], 0.5, None, ALU.mult).then_inc(sem("nw_halved"), 1)
            dve.wait_ge(sem("tap_scaled"), TAPS)
            dve.wait_ge(sem("constants"), 1)
            dve.sem_inc(sem("weights_ready"))

            def take_gates(k):
                dve.wait_ge(sem("gates_loaded"), 16 * k + 16)
                dve.tensor_copy(gt[:, :, :].rearrange("p a h -> p (a h)"), gin[:, :]).then_inc(sem("gates_taken"), 1)

            def use_projection(k, n):
                dve.wait_ge(sem("tanh"), 8 * k + n + 1)
                if n < 2:
                    to = kqT[:, 4 * n:4 * n + 4, CH:3 * CH]
                    own = lambda t: t.rearrange("p (j t) -> p j t", j=4)
                elif n < 4:
                    to = kT[:, 4 * (n - 2):4 * (n - 2) + 4, :]
                    own = lambda t: t.rearrange("p (j t) -> p j t", j=4)
                else:
                    to = (v if n < 6 else z)[:, (n % 2) * 512:(n % 2 + 1) * 512]
                    own = lambda t: t
                dve.scalar_tensor_tensor(out=to, in0=own(th[:, n % 2, :]), scalar=1.0, in1=own(pa[:, n % 2, :]),
                                         op0=ALU.add, op1=ALU.mult).then_inc(sem("proj_used"), 1)

            def sum_q(k):
                dve.wait_ge(sem("squared"), 2 * k + 1)
                dve.tensor_reduce(n4[:, 1, :], heads(sq), AX_X, ALU.add).then_inc(sem("q_summed"), 1)

            def key_terms(k, link):
                dve.wait_ge(sem("squared"), 2 * k + 2)
                link(dve.tensor_reduce(n4[:, 0, :], heads(sq), AX_X, ALU.add))
                dve.tensor_scalar(n4[:, :, :], n4[:, :, :], 0.25, L2_EPS, ALU.mult, ALU.add)\
                   .then_inc(sem("n4_ready"), 1)
                dve.wait_ge(sem("n4_ready"), k + 1)
                link(dve.reciprocal(cc[:, :], n4[:, 0, :]))
                link(dve.scalar_tensor_tensor(out=cc[:, :], in0=cc[:, :], scalar=0.25, in1=gt[:, 0, :],
                                              op0=ALU.mult, op1=ALU.mult))
                dve.tensor_tensor(wr[:, :], cc[:, :], gt[:, 3, :], ALU.mult)
                for m in HALVES:
                    dve.wait_ge(sem("decays"), 2 * k + m + 1)
                    dve.tensor_tensor(dd[:, half(m), :], dd[:, half(m), :], spread(cc[:, half(m)], CH), ALU.mult)\
                       .then_inc(sem("dd_ready"), 1)

            def weigh(k, m):
                dve.wait_ge(sem("kkq"), 2 * k + m + 1)
                dve.wait_ge(sem("dd_ready"), 2 * k + m + 1)
                dve.wait_ge(sem("ddm_ready"), 2 * k + m + 1)
                dve.wait_ge(sem("kept"), k)
                for b in SEQS:
                    own = rows_of(b)
                    by_g = lambda t: t[own, half(m), :].rearrange("p (j g) t -> p g j t", g=2)
                    sums = pb[own, :, :].rearrange("p g (j a t) -> p g j a t", a=2, t=CH)
                    last_a = dve.tensor_tensor(by_g(at), by_g(dd), sums[:, :, :, b, :], ALU.mult)
                    last_q = dve.tensor_tensor(by_g(qk), by_g(ddm), sums[:, :, :, 1 - b, :], ALU.mult)
                last_a.then_inc(sem("at_ready"), 1)
                last_q.then_inc(sem("qk_read"), 1)

            def scale_v(k, link):
                dve.wait_ge(sem("nr_ready"), k + 1)
                link(dve.tensor_tensor(heads(v), heads(v), spread(nr[:, 0, :]), ALU.mult))

            take_gates(0)
            first, _ = chain(dve, sem("first"), 0)
            for n in range(4):
                use_projection(0, n)
            sum_q(0)
            key_terms(0, first)
            weigh(0, 0)
            use_projection(0, 4)
            use_projection(0, 5)
            weigh(0, 1)
            use_projection(0, 6)
            use_projection(0, 7)
            scale_v(0, first)
            with dve.Fori(0, NPAIR) as p:
                dve.memset(state[:, :, :, :, :].rearrange("p b j g d -> p (b j g d)"), 0.0).then_inc(sem("state_ready"), 1)
                with dve.Fori(0, NCH) as c:
                    i = p * NCH + c
                    k = i + 1
                    link, links = chain(dve, sem("dve"), i * DVE_LINKS)
                    dve.tensor_copy(nq[:, :], nr[:, 1, :])
                    dve.wait_ge(sem("yw_ready"), 2 * i)
                    link(dve.tensor_copy(wr_now[:, :], wr[:, :]))
                    for b in SEQS:
                        own = rows_of(b)
                        dve.wait_ge(sem("ks"), 2 * i + b + 1)
                        last = dve.tensor_tensor(heads(r)[own, :, :],
                                                 pc[own, 2 * b:2 * b + 2, :].rearrange("p a (h d) -> p (a h) d", d=DHD),
                                                 spread(gt[own, 2, :]), ALU.mult)
                    link(last)
                    dve.tensor_tensor(r[:, :], v[:, :], r[:, :], ALU.subtract).then_inc(sem("r_ready"), 1)
                    use_projection(k, 0)
                    for g in range(2):
                        rows = slice(64 * g, 64 * g + 64)
                        last = dve.tensor_tensor(faded[rows, :, :, :].rearrange("p b j d -> p (b j) d"),
                                                 state[rows, :, :, g, :].rearrange("p b j d -> p (b j) d"),
                                                 spread(gt[rows, 4, :]), ALU.mult)
                    link(last)
                    use_projection(k, 1)
                    dve.wait_ge(sem("oi_ready"), i + 1)
                    take_gates(k)
                    use_projection(k, 2)
                    dve.wait_ge(sem("w4_sum"), i + 1)
                    dve.tensor_scalar(w4[:, :, 0:SB], pb[:, 0, 0:DH * SB].rearrange("p (h c) -> p h c", c=SB), hi[:, 0:1],
                                      None, ALU.mult).then_inc(sem("w4_ready"), 1)
                    use_projection(k, 3)
                    dve.wait_ge(sem("t4_sum"), i + 1)
                    for b in SEQS:
                        own = rows_of(b, 0)
                        dve.tensor_tensor(ti[own, :, 0:SB], ti[own, :, 0:SB],
                                          pb[own, 1, 0:DH * SB].rearrange("p (h c) -> p h c", c=SB), ALU.subtract)
                    for b, u in BLOCKS:
                        own, cols = rows_of(b, u), slice(HB * u + SB, HB * u + HB)
                        last = dve.scalar_tensor_tensor(
                            out=tt[own, :, cols], in0=tt[own, :, cols], scalar=hi[own, 0:1],
                            in1=pb[own, 1, DH * SB:2 * DH * SB].rearrange("p (h c) -> p h c", c=SB),
                            op0=ALU.mult, op1=ALU.subtract)
                    last.then_inc(sem("t4_ready"), 1)
                    sum_q(k)
                    key_terms(k, link)
                    weigh(k, 0)
                    for m in HALVES:
                        dve.wait_ge(sem("o_sum"), 2 * i + m + 1)
                        last = dve.tensor_tensor(o[:, m * 512:(m + 1) * 512], oi[:, m * 512:(m + 1) * 512],
                                                 pc[:, 2 + m, :], ALU.add)
                    last.then_inc(sem("o_ready"), 1)
                    dve.wait_ge(sem("o_squared"), i + 1)
                    link(dve.tensor_reduce(ms[:, :], heads(sq2), AX_X, ALU.add))
                    link(dve.tensor_tensor(f2[:, :], nq[:, :], nq[:, :], ALU.mult))
                    link(dve.tensor_tensor(ms[:, :], ms[:, :], f2[:, :], ALU.mult))
                    dve.tensor_scalar(ms[:, :], ms[:, :], 1.0 / (256 * DHD), RMS_EPS, ALU.mult, ALU.add)\
                       .then_inc(sem("ms_ready"), 1)
                    weigh(k, 1)
                    dve.wait_ge(sem("update"), i + 1)
                    for g in range(2):
                        rows = slice(64 * g, 64 * g + 64)
                        last = dve.tensor_tensor(state[rows, :, :, g, :].rearrange("p b j d -> p (b j) d"),
                                                 faded[rows, :, :, :].rearrange("p b j d -> p (b j) d"),
                                                 pc[rows, :, :].rearrange("p a (j g d) -> p (a j) g d", g=2, d=DHD)[:, :, g, :],
                                                 ALU.add)
                    last.then_inc(sem("state_ready"), 1)
                    dve.wait_ge(sem("f_ready"), i + 1)
                    link(dve.scalar_tensor_tensor(out=f2[:, :], in0=nq[:, :], scalar=1.0 / 16, in1=f[:, :],
                                                  op0=ALU.mult, op1=ALU.mult))
                    link(dve.tensor_tensor(heads(o), heads(o), spread(f2[:, :]), ALU.mult))
                    dve.wait_ge(sem("z_ready"), i + 1)
                    dve.tensor_tensor(o[:, :], o[:, :], z[:, :], ALU.mult).then_inc(sem("on_ready"), 1)
                    dve.wait_ge(sem("on_ready"), i + 1)
                    use_projection(k, 4)
                    use_projection(k, 5)
                    use_projection(k, 6)
                    dve.wait_ge(sem("out_ready"), i + 1)
                    dve.wait_ge(sem("x_loaded"), 32 * i + 32)
                    dve.wait_ge(sem("stored"), 32 * i)
                    dve.tensor_tensor(xo[:, :], xt[:, :], pc[:, 0, 0:D], ALU.add).then_inc(sem("x_used"), 1)
                    use_projection(k, 7)
                    scale_v(k, link)
                    assert links[0] == DVE_LINKS, links


AH, AHD = 4, 32
AN = P // NSEQ
NE, FF = 8, 512
CAP = NSEQ * SEQ // NE


def attention_rows(x, u, c):
    return x.rearrange("(l n) d -> l n d", l=NSEQ)[:, bass.ds(u * (4 * AN) + c * AN, AN), :]


def attention_phase(nc, x_in, y_out, route, in_t, in_b, in_b_cols, out_t, out_b, ln_g, ln_b, wg):
    NC = 4
    NU = NT // NC
    DVE_LINKS = 17
    OFF = -1e30
    with ExitStack() as ctx:
        def sb(name, shape):
            return ctx.enter_context(nc.sbuf_tensor("e_" + name, shape, F32))
        sem = semaphores(nc, ctx, "e")
        ident = sb("ident", [P, P])
        same = sb("same", [P, NSEQ, AN])
        mhalf = sb("mhalf", [P, NC])
        order = sb("order", [P, NE])
        win = sb("win", [P, 3 * D])
        wout = sb("wout", [P, D])
        wgs = sb("wgs", [P, NE])
        bqk = sb("bqk", [P, 3])
        bv = sb("bv", [P, D])
        ob = sb("ob", [P, D])
        lg = sb("lg", [P, D])
        lb = sb("lb", [P, D])
        xt = sb("xt", [P, NC, D])
        h = sb("h", [P, NC, D])
        hb = sb("hb", [P, NC, D])
        hT = sb("hT", [P, 512])
        qT = sb("qT", [P, 512])
        kT = sb("kT", [P, 512])
        v = sb("v", [P, NC, D])
        sc = sb("sc", [P, AH, NC, P])
        mx = sb("mx", [P, AH * NC])
        pr = sb("pr", [P, AH, NC, P])
        den = sb("den", [P, AH * NC])
        rden = sb("rden", [P, AH, NC])
        prT = sb("prT", [P, AH, NC, P])
        on = sb("on", [P, NC, D])
        oT = sb("oT", [P, 512])
        y = sb("y", [P, NC, D])
        yT = sb("yT", [P, 512])
        st = sb("st", [P, NC, 6])
        mv = sb("mv", [P, NC, 2])
        ve = sb("ve", [P, NC])
        rstd = sb("rstd", [P, NC])
        lm = sb("lm", [P, NC])
        ld = sb("ld", [P, NC, NE])
        le = sb("le", [P, NC, NE])
        ls = sb("ls", [P, NC])
        lr = sb("lr", [P, NC])
        hit = sb("hit", [P, NC, NE])
        first = sb("first", [P, NC])
        rt = sb("rt", [P, NC, 2, NE])
        ps = [ctx.enter_context(nc.psum_tensor(f"e_ps{n}", [P, 512], F32)) for n in range(8)]
        block = ctx.enter_context(nc.Block())
        tiles = lambda t: t[:, :].rearrange("p (c d) -> p c d", c=NC)

        @block.sync
        def _(sp):
            for to, of in ((win[:, :], in_t), (wout[:, :], out_t), (wgs[:, :], wg),
                           (bqk[:, :], in_b_cols),
                           (bv[:, :], in_b[2 * D:3 * D].partition_broadcast(P)), (ob[:, :], out_b.partition_broadcast(P)),
                           (lg[:, :], ln_g.partition_broadcast(P)), (lb[:, :], ln_b.partition_broadcast(P))):
                sp.dma_start(to, of).then_inc(sem("weights"), 16)

            def load(u):
                for c in range(NC):
                    sp.dma_start(xt[:, c, :], attention_rows(x_in, u, c)).then_inc(sem("x_loaded"), 16)

            def store(u):
                sp.wait_ge(sem("y_ready"), u + 1)
                for c in range(NC):
                    sp.dma_start(attention_rows(y_out, u, c), y[:, c, :]).then_inc(sem("stored"), 16)
                sp.wait_ge(sem("route_ready"), u + 1)
                for c in range(NC):
                    sp.dma_start(attention_rows(route, u, c), rt[:, c, :, :].rearrange("p a e -> p (a e)"))\
                      .then_inc(sem("stored"), 16)

            load(0)
            sp.wait_ge(sem("h_ready"), 1)
            load(1)
            with sp.Fori(1, NU - 1) as u:
                sp.wait_ge(sem("h_ready"), u + 1)
                load(u + 1)
                store(u - 1)
            store(NU - 2)
            store(NU - 1)
            sp.wait_ge(sem("stored"), 16 * 2 * NT)

        @block.gpsimd
        def _(pool):
            make_identity(pool, ident, sem("ident"))
            pool.memset(mhalf[:, :], -0.5).then_inc(sem("ones"), 1)
            for e in range(NE):
                last = pool.memset(order[:, e:e + 1], float(NE - e))
            last.then_inc(sem("ones"), 1)
            pool.memset(same[:, :, :], OFF).then_inc(sem("same"), 1)
            for shift in range(1 - NSEQ, NSEQ):
                pool.wait_ge(sem("same"), shift + NSEQ)
                pool.affine_select(out=same[:, :, :], in_=same[:, :, :], compare_op=ALU.not_equal, fill=0.0,
                                   base=-AN * shift, pattern=[[-AN, NSEQ], [-1, AN]], channel_multiplier=1)\
                    .then_inc(sem("same"), 1)

            def norm(var_ready, rstd_ready, u):
                pool.wait_ge(var_ready, u + 1)
                pool.tensor_tensor(rstd[:, :], ve[:, :], mhalf[:, :], ALU.pow).then_inc(rstd_ready, 1)

            h_norm = lambda u: norm(sem("h_var"), sem("h_rstd"), u)
            y_norm = lambda u: norm(sem("y_var"), sem("y_rstd"), u)
            h_norm(0)
            h_norm(1)
            with pool.Fori(1, NU - 1) as u:
                y_norm(u - 1)
                h_norm(u + 1)
            y_norm(NU - 2)
            y_norm(NU - 1)

        @block.scalar
        def _(act):
            act.wait_ge(sem("weights"), 16 * 8)

            def prepare(u):
                act.wait_ge(sem("h_turned"), u + 1)
                act.activation(hT[:, :], ps[0][:, :], ACT.Copy).then_inc(sem("hT_ready"), 1)
                act.wait_ge(sem("qk_ready"), u + 1)
                act.activation(qT[:, :], ps[1][:, :], ACT.Identity, bias=bqk[:, 0:1])
                act.activation(kT[:, :], ps[2][:, :], ACT.Identity, bias=bqk[:, 1:2]).then_inc(sem("qkT_ready"), 1)

            def attend(u):
                act.wait_ge(sem("max_ready"), u + 1)
                for j in range(AH):
                    for c in range(NC):
                        n = j * NC + c
                        last = act.activation(pr[:, j, c, :], sc[:, j, c, :], ACT.Exp, bias=mx[:, n:n + 1],
                                              accum_out=den[:, n:n + 1])
                    last.then_inc(sem("probs"), 1)
                for j in range(AH):
                    act.wait_ge(sem("probs_turned"), AH * u + j + 1)
                    act.activation(prT[:, j, :, :].rearrange("p c t -> p (c t)"), ps[4 + j][:, :], ACT.Copy)\
                       .then_inc(sem("prT_ready"), 1)

            def mix(u):
                act.wait_ge(sem("o_turned"), u + 1)
                act.activation(oT[:, :], ps[0][:, :], ACT.Copy).then_inc(sem("oT_ready"), 1)

            def gate(u):
                act.wait_ge(sem("y_turned"), u + 1)
                act.activation(yT[:, :], ps[0][:, :], ACT.Copy).then_inc(sem("yT_ready"), 1)
                act.wait_ge(sem("ld_ready"), u + 1)
                act.activation(le[:, :, :], ld[:, :, :], ACT.Exp).then_inc(sem("le_ready"), 1)

            prepare(0)
            attend(0)
            prepare(1)
            with act.Fori(1, NU - 1) as u:
                mix(u - 1)
                attend(u)
                prepare(u + 1)
                gate(u - 1)
            mix(NU - 2)
            attend(NU - 1)
            gate(NU - 2)
            mix(NU - 1)
            gate(NU - 1)

        @block.tensor
        def _(pe):
            pe.wait_ge(sem("ident"), 2)
            pe.wait_ge(sem("weights"), 16 * 8)
            def turn(of, done):
                for c in range(NC):
                    last = pe.transpose(ps[0][:, c * P:(c + 1) * P], of[:, c, :], ident[:, :])
                last.then_inc(done, 1)

            def prepare(u, residuals):
                pe.wait_ge(sem("h_ready"), u + 1)
                turn(h, sem("h_turned"))
                pe.wait_ge(sem("hT_ready"), u + 1)
                pe.wait_ge(sem("on_ready"), u)
                pe.wait_ge(sem("residual"), residuals)
                for n in range(2):
                    last = pe.matmul(ps[1 + n][:, :], win[:, n * D:(n + 1) * D], hT[:, :], start=True, stop=True)
                last.then_inc(sem("qk_ready"), 1)
                for c in range(NC):
                    last = pe.matmul(ps[3][:, c * P:(c + 1) * P], hT[:, c * P:(c + 1) * P], win[:, 2 * D:3 * D],
                                     start=True, stop=True)
                last.then_inc(sem("v_ready"), 1)

            def scores(u):
                pe.wait_ge(sem("qkT_ready"), u + 1)
                for j in range(AH):
                    rows = slice(AHD * j, AHD * j + AHD)
                    for c in range(NC):
                        here = slice(c * P, (c + 1) * P)
                        last = pe.matmul(ps[4 + j][:, here], qT[rows, here], kT[rows, here], start=True, stop=True)
                    last.then_inc(sem("scores"), 1)

            def attend(u):
                for j in range(AH):
                    pe.wait_ge(sem("probs"), AH * u + j + 1)
                    for c in range(NC):
                        last = pe.transpose(ps[4 + j][:, c * P:(c + 1) * P], pr[:, j, c, :], ident[:, :])
                    last.then_inc(sem("probs_turned"), 1)
                pe.wait_ge(sem("v_used"), u + 1)
                for j in range(AH):
                    pe.wait_ge(sem("prT_ready"), AH * u + j + 1)
                    for c in range(NC):
                        cols = slice(c * P + AHD * j, c * P + AHD * j + AHD)
                        last = pe.matmul(ps[1][:, cols], prT[:, j, c, :], v[:, c, AHD * j:AHD * j + AHD],
                                         start=True, stop=True)
                last.then_inc(sem("o_ready"), 1)

            def mix(u):
                pe.wait_ge(sem("on_ready"), u + 1)
                pe.wait_ge(sem("route_ready"), u)
                turn(on, sem("o_turned"))
                pe.wait_ge(sem("oT_ready"), u + 1)
                for c in range(NC):
                    last = pe.matmul(ps[2][:, c * P:(c + 1) * P], oT[:, c * P:(c + 1) * P], wout[:, :],
                                     start=True, stop=True)
                last.then_inc(sem("mixed"), 1)

            def gate(u):
                pe.wait_ge(sem("y_ready"), u + 1)
                turn(y, sem("y_turned"))
                pe.wait_ge(sem("yT_ready"), u + 1)
                for c in range(NC):
                    last = pe.matmul(ps[0][:, c * NE:(c + 1) * NE], yT[:, c * P:(c + 1) * P], wgs[:, :],
                                     start=True, stop=True)
                last.then_inc(sem("logits"), 1)

            prepare(0, 0)
            scores(0)
            attend(0)
            prepare(1, 0)
            with pe.Fori(1, NU - 1) as u:
                scores(u)
                mix(u - 1)
                attend(u)
                prepare(u + 1, u)
                gate(u - 1)
            scores(NU - 1)
            mix(NU - 2)
            attend(NU - 1)
            gate(NU - 2)
            mix(NU - 1)
            gate(NU - 1)

        @block.vector
        def _(dve):
            dve.wait_ge(sem("weights"), 16 * 8)
            dve.wait_ge(sem("ones"), 2)
            dve.wait_ge(sem("same"), 2 * NSEQ)
            def row(t):
                return t[:, :].unsqueeze(1).to_broadcast([P, NC, D])

            def normed(to, of, link, var_ready, rstd_ready, u, done):
                for c in range(NC):
                    last = dve.bn_stats(st[:, c, :], of[:, c, :])
                link(last)
                dve.sem_inc(sem("passed"))
                for c in range(NC):
                    last = dve.bn_aggr(mv[:, c, :], st[:, c, :])
                link(last)
                dve.tensor_scalar(ve[:, :], mv[:, :, 1], LN_EPS, None, ALU.add).then_inc(var_ready, 1)
                dve.wait_ge(rstd_ready, u + 1)
                for c in range(NC):
                    last = dve.tensor_scalar(to[:, c, :], of[:, c, :], mv[:, c, 0:1], rstd[:, c:c + 1],
                                             ALU.subtract, ALU.mult)
                done(last)

            def prepare(u, link):
                dve.wait_ge(sem("x_loaded"), 64 * u + 64)
                normed(h, xt, link, sem("h_var"), sem("h_rstd"), u, lambda last: last.then_inc(sem("h_ready"), 1))

            def keep(u, link):
                dve.wait_ge(sem("h_ready"), u + 1)
                link(dve.tensor_tensor(hb[:, :, :], h[:, :, :], row(ob), ALU.add))

            def take_v(u):
                dve.wait_ge(sem("v_ready"), u + 1)
                dve.tensor_tensor(v[:, :, :], tiles(ps[3]), row(bv), ALU.add).then_inc(sem("v_used"), 1)

            def soften(u, link):
                for j in range(AH):
                    dve.wait_ge(sem("scores"), AH * u + j + 1)
                    last = dve.scalar_tensor_tensor(
                        out=sc[:, j, :, :], in0=tiles(ps[4 + j]), scalar=float(AHD) ** -0.5,
                        in1=same[:, :, :].rearrange("p l n -> p (l n)").unsqueeze(1).to_broadcast([P, NC, P]),
                        op0=ALU.mult, op1=ALU.add)
                link(last)
                link(dve.tensor_reduce(mx[:, :], sc[:, :, :, :].rearrange("p j c s -> p (j c) s"), AX_X, ALU.max))
                dve.tensor_scalar(mx[:, :], mx[:, :], -1.0, None, ALU.mult).then_inc(sem("max_ready"), 1)

            def take_o(u, link):
                dve.wait_ge(sem("probs"), AH * u + AH)
                link(dve.reciprocal(rden[:, :, :].rearrange("p j c -> p (j c)"), den[:, :]))
                dve.wait_ge(sem("o_ready"), u + 1)
                for c in range(NC):
                    last = dve.tensor_tensor(on[:, c, :].rearrange("p (j d) -> p j d", j=AH),
                                             ps[1][:, c * P:(c + 1) * P].rearrange("p (j d) -> p j d", j=AH),
                                             rden[:, :, c].unsqueeze(2).to_broadcast([P, AH, AHD]), ALU.mult)
                last.then_inc(sem("on_ready"), 1)

            def finish(u, link):
                dve.wait_ge(sem("mixed"), u + 1)
                dve.tensor_tensor(hb[:, :, :], hb[:, :, :], tiles(ps[2]), ALU.add).then_inc(sem("residual"), 1)
                dve.wait_ge(sem("residual"), u + 1)
                dve.wait_ge(sem("stored"), 128 * u)
                normed(y, hb, link, sem("y_var"), sem("y_rstd"), u, link)
                link(dve.tensor_tensor(y[:, :, :], y[:, :, :], row(lg), ALU.mult))
                dve.tensor_tensor(y[:, :, :], y[:, :, :], row(lb), ALU.add).then_inc(sem("y_ready"), 1)

            def choose(u, link):
                dve.wait_ge(sem("logits"), u + 1)
                lo = ps[0][:, 0:NC * NE].rearrange("p (c e) -> p c e", e=NE)
                spread = lambda t: t[:, :].unsqueeze(2).to_broadcast([P, NC, NE])
                link(dve.tensor_reduce(lm[:, :], lo, AX_X, ALU.max))
                dve.tensor_tensor(ld[:, :, :], lo, spread(lm), ALU.subtract).then_inc(sem("ld_ready"), 1)
                link(dve.tensor_tensor(hit[:, :, :], lo, spread(lm), ALU.is_equal))
                link(dve.tensor_tensor(hit[:, :, :], hit[:, :, :], order[:, :].unsqueeze(1).to_broadcast([P, NC, NE]),
                                       ALU.mult))
                link(dve.tensor_reduce(first[:, :], hit[:, :, :], AX_X, ALU.max))
                link(dve.tensor_tensor(rt[:, :, 0, :], hit[:, :, :], spread(first), ALU.is_equal))
                dve.wait_ge(sem("le_ready"), u + 1)
                link(dve.tensor_reduce(ls[:, :], le[:, :, :], AX_X, ALU.add))
                link(dve.reciprocal(lr[:, :], ls[:, :]))
                dve.tensor_tensor(rt[:, :, 1, :], rt[:, :, 0, :], spread(lr), ALU.mult).then_inc(sem("route_ready"), 1)

            start, _ = chain(dve, sem("start"), 0)
            prepare(0, start)
            take_v(0)
            soften(0, start)
            keep(0, start)
            prepare(1, start)
            take_o(0, start)
            take_v(1)
            with dve.Fori(1, NU - 1) as u:
                link, links = chain(dve, sem("dve"), (u - 1) * DVE_LINKS)
                soften(u, link)
                finish(u - 1, link)
                keep(u, link)
                prepare(u + 1, link)
                take_o(u, link)
                take_v(u + 1)
                choose(u - 1, link)
                assert links[0] == DVE_LINKS, links
            final, _ = chain(dve, sem("final"), 0)
            soften(NU - 1, final)
            finish(NU - 2, final)
            keep(NU - 1, final)
            take_o(NU - 1, final)
            choose(NU - 2, final)
            finish(NU - 1, final)
            choose(NU - 1, final)


def linear_expert_phase(nc, x_in, y_in, route, x_out, w1_rows, b1_t, w2_rows, b2, ln_g, ln_b):
    NC = 4
    KC = FF // P
    DVE_LINKS = 8
    with ExitStack() as ctx:
        def sb(name, shape):
            return ctx.enter_context(nc.sbuf_tensor("f_" + name, shape, F32))
        sem = semaphores(nc, ctx, "f")
        ident = sb("ident", [P, P])
        before = sb("before", [P, P])
        ones = sb("ones", [P, P])
        mhalf = sb("mhalf", [P, NC])
        w1s = sb("w1s", [P, NE * KC, D])
        w2s = sb("w2s", [P, NE * KC, D])
        w12 = sb("w12", [P, NE, D])
        b1s = sb("b1s", [P, NE * KC])
        b1d = sb("b1d", [P, NE * KC, NE])
        b2s = sb("b2s", [NE, D])
        b12 = sb("b12", [NE, D])
        lg = sb("lg", [P, D])
        lb = sb("lb", [P, D])
        rts = sb("rts", [P, NT, 2 * NE])
        hot = sb("hot", [P, NE, NT])
        total = sb("total", [P, NE, NT])
        earlier = sb("earlier", [P, NE, NT + 1])
        loc = sb("loc", [P, NE, NT])
        cw = sb("cw", [P, NT, NE])
        cur = sb("cur", [P, NC, NE])
        curT = sb("curT", [NE, 512])
        xt = sb("xt", [P, 2, NC, D])
        yt = sb("yt", [P, 2, NC, D])
        yT = sb("yT", [P, 512])
        part = sb("part", [P, 2, NE, D])
        moe = sb("moe", [P, NC, D])
        xo = sb("xo", [P, NC, D])
        st = sb("st", [P, NC, 6])
        mv = sb("mv", [P, NC, 2])
        ve = sb("ve", [P, NC])
        rstd = sb("rstd", [P, NC])
        ps = [ctx.enter_context(nc.psum_tensor(f"f_ps{n}", [P, 512], F32)) for n in range(4)]
        pe_out = [ctx.enter_context(nc.psum_tensor(f"f_pe{n}", [P, 2, 512], F32)) for n in range(2)]
        block = ctx.enter_context(nc.Block())
        tiles = lambda t: t[:, :].rearrange("p (c d) -> p c d", c=NC)

        @block.sync
        def _(sp):
            for to, of in ((w1s[:, :, :].rearrange("p k d -> p (k d)"), w1_rows),
                           (w2s[:, :, :].rearrange("p k d -> p (k d)"), w2_rows),
                           (b1s[:, :], b1_t), (b2s[:, :], b2),
                           (lg[:, :], ln_g.partition_broadcast(P)), (lb[:, :], ln_b.partition_broadcast(P)),
                           (rts[:, :, :], route.rearrange("(i p) f -> p i f", p=P))):
                sp.dma_start(to, of).then_inc(sem("weights"), 16)
            with sp.Fori(0, NSEQ // 2) as v:
                for n in range(2):
                    sp.wait_ge(sem(f"x_used{n}"), v)
                    sp.dma_start(yt[:, n, :, :], load_seq(y_in, 2 * v + n)).then_inc(sem(f"loaded{n}"), 16)
                    sp.dma_start(xt[:, n, :, :], load_seq(x_in, 2 * v + n)).then_inc(sem(f"loaded{n}"), 16)
            sp.wait_ge(sem("stored"), 16 * NSEQ)

        @block.gpsimd
        def _(pool):
            make_identity(pool, ident, sem("ident"))
            link, _ = chain(pool, sem("setup"), 0)
            pool.memset(mhalf[:, :], -0.5)
            pool.memset(ones[:, :], 1.0)
            link(pool.memset(before[:, :], 1.0))
            pool.affine_select(out=before[:, :], in_=before[:, :], compare_op=ALU.is_gt, fill=0.0, base=0,
                               pattern=[[1, P]], channel_multiplier=-1).then_inc(sem("masks"), 1)
            with pool.Fori(0, NSEQ) as u:
                pool.wait_ge(sem("var_ready"), u + 1)
                pool.tensor_tensor(rstd[:, :], ve[:, :], mhalf[:, :], ALU.pow).then_inc(sem("rstd_ready"), 1)

        @block.scalar
        def _(act):
            for n in range(2):
                act.wait_ge(sem("w12_sum"), n + 1)
                act.activation(w12[:, 4 * n:4 * n + 4, :].rearrange("p e d -> p (e d)"), ps[n][:, :], ACT.Copy)\
                   .then_inc(sem("w12_ready"), 1)
            with act.Fori(0, NSEQ // 2) as v:
                for n in range(2):
                    u = 2 * v + n
                    act.wait_ge(sem("y_turned"), u + 1)
                    act.activation(yT[:, :], ps[0][:, :], ACT.Copy).then_inc(sem("yT_ready"), 1)
                    act.wait_ge(sem("cur_turned"), u + 1)
                    act.activation(curT[:, :], ps[1][0:NE, :], ACT.Copy).then_inc(sem("curT_ready"), 1)
                    act.wait_ge(sem(f"x_used{n}"), v + 1)
                    act.dma_start(load_seq(x_out, u), xo[:, :, :]).then_inc(sem("stored"), 16)

        @block.tensor
        def _(pe):
            pe.wait_ge(sem("ident"), 2)
            pe.wait_ge(sem("masks"), 1)
            pe.wait_ge(sem("weights"), 16 * 7)
            for e in range(NE):
                for k in range(KC):
                    last = pe.matmul(ps[e // 4][:, (e % 4) * D:(e % 4 + 1) * D], w1s[:, e * KC + k, :],
                                     w2s[:, e * KC + k, :], start=(k == 0), stop=(k == KC - 1))
                if e % 4 == 3:
                    last.then_inc(sem("w12_sum"), 1)
            pe.wait_ge(sem("b1_placed"), 1)
            for m in range(NE * KC):
                last = pe.matmul(ps[2][0:NE, 0:D], b1d[:, m, :], w2s[:, m, :], start=(m == 0), stop=(m == NE * KC - 1))
            last.then_inc(sem("b12_sum"), 1)
            pe.wait_ge(sem("hot_ready"), 1)
            flat = hot[:, :, :].rearrange("p e i -> p (e i)")
            pe.matmul(pe_out[0][:, 0, :], before[:, :], flat, start=True, stop=True)
            pe.matmul(pe_out[0][:, 1, :], ones[:, :], flat, start=True, stop=True).then_inc(sem("counted"), 1)
            pe.wait_ge(sem("w12_ready"), 2)
            pe.wait_ge(sem("b12_ready"), 1)
            with pe.Fori(0, NSEQ // 2) as v:
                for odd in range(2):
                    u = 2 * v + odd
                    pe.wait_ge(sem(f"loaded{odd}"), 32 * v + 32)
                    for c in range(NC):
                        last = pe.transpose(ps[0][:, c * P:(c + 1) * P], yt[:, odd, c, :], ident[:, :])
                    last.then_inc(sem("y_turned"), 1)
                    pe.wait_ge(sem("cur_ready"), u + 1)
                    for c in range(NC):
                        last = pe.transpose(ps[1][0:NE, c * P:(c + 1) * P], cur[:, c, :], ident[:, :])
                    last.then_inc(sem("cur_turned"), 1)
                    pe.wait_ge(sem("yT_ready"), u + 1)
                    for c in range(NC):
                        if c >= 2:
                            pe.wait_ge(sem("weighed"), NC * u + c - 1)
                        for n in range(2):
                            last = pe.matmul(pe_out[c % 2][:, n, :], yT[:, c * P:(c + 1) * P],
                                             w12[:, 4 * n:4 * n + 4, :].rearrange("p e d -> p (e d)"), start=True, stop=True)
                        last.then_inc(sem("experts"), 1)
                    pe.wait_ge(sem("curT_ready"), u + 1)
                    for c in range(NC):
                        last = pe.matmul(ps[2][:, c * P:(c + 1) * P], curT[:, c * P:(c + 1) * P], b12[:, :],
                                         start=True, stop=True)
                    last.then_inc(sem("biases"), 1)

        @block.vector
        def _(dve):
            dve.wait_ge(sem("weights"), 16 * 7)
            link, _ = chain(dve, sem("setup_dve"), 0)
            link(dve.memset(b1d[:, :, :], 0.0))
            for e in range(NE):
                last = dve.tensor_copy(b1d[:, e * KC:(e + 1) * KC, e], b1s[:, e * KC:(e + 1) * KC])
            last.then_inc(sem("b1_placed"), 1)
            dve.tensor_copy(hot[:, :, :], rts[:, :, 0:NE].rearrange("p i e -> p e i")).then_inc(sem("hot_ready"), 1)
            dve.memset(total[:, :, :], 1.0)
            link(dve.memset(earlier[:, :, 0:1], 0.0))
            dve.wait_ge(sem("counted"), 1)
            counts = pe_out[0][:, 1, :].rearrange("p (e i) -> p e i", e=NE)
            for e in range(NE):
                last = dve.tensor_tensor_scan(earlier[:, e, 1:NT + 1], total[:, e, :], counts[:, e, :], 0.0,
                                              ALU.mult, ALU.add)
            link(last)
            link(dve.tensor_tensor(loc[:, :, :], earlier[:, :, 0:NT],
                                   pe_out[0][:, 0, :].rearrange("p (e i) -> p e i", e=NE), ALU.add))
            link(dve.tensor_scalar(loc[:, :, :], loc[:, :, :], float(CAP), None, ALU.is_lt))
            link(dve.tensor_tensor(cw[:, :, :], rts[:, :, NE:2 * NE], loc[:, :, :].rearrange("p e i -> p i e"), ALU.mult))
            dve.wait_ge(sem("b12_sum"), 1)
            dve.tensor_tensor(b12[:, :], b2s[:, :], ps[2][0:NE, 0:D], ALU.add).then_inc(sem("b12_ready"), 1)
            with dve.Fori(0, NSEQ // 2) as v:
                for odd in range(2):
                    u = 2 * v + odd
                    link, links = chain(dve, sem("dve"), u * DVE_LINKS)

                    def row(t):
                        return t[:, :].unsqueeze(1).to_broadcast([P, NC, D])

                    dve.wait_ge(sem("curT_ready"), u)
                    dve.tensor_copy(cur[:, :, :], cw[:, bass.ds(u * NC, NC), :]).then_inc(sem("cur_ready"), 1)
                    dve.wait_ge(sem("cur_ready"), u + 1)
                    for c in range(NC):
                        dve.wait_ge(sem("experts"), NC * u + c + 1)
                        dve.tensor_tensor(part[:, c % 2, :, :],
                                          pe_out[c % 2][:, :, :].rearrange("p a (e d) -> p (a e) d", d=D),
                                          cur[:, c, :].unsqueeze(2).to_broadcast([P, NE, D]), ALU.mult)\
                           .then_inc(sem("weighed"), 1)
                        dve.wait_ge(sem("weighed"), NC * u + c + 1)
                        last = dve.tensor_reduce(moe[:, c, :], part[:, c % 2, :, :].rearrange("p e d -> p d e"), AX_X, ALU.add)
                    link(last)
                    dve.wait_ge(sem("biases"), u + 1)
                    link(dve.tensor_tensor(moe[:, :, :], moe[:, :, :], tiles(ps[2]), ALU.add))
                    dve.wait_ge(sem(f"loaded{odd}"), 32 * v + 32)
                    link(dve.tensor_tensor(moe[:, :, :], moe[:, :, :], yt[:, odd, :, :], ALU.add))
                    for c in range(NC):
                        last = dve.bn_stats(st[:, c, :], moe[:, c, :])
                    link(last)
                    dve.sem_inc(sem("passed"))
                    for c in range(NC):
                        last = dve.bn_aggr(mv[:, c, :], st[:, c, :])
                    link(last)
                    dve.tensor_scalar(ve[:, :], mv[:, :, 1], LN_EPS, None, ALU.add).then_inc(sem("var_ready"), 1)
                    dve.wait_ge(sem("rstd_ready"), u + 1)
                    for c in range(NC):
                        last = dve.tensor_scalar(moe[:, c, :], moe[:, c, :], mv[:, c, 0:1], rstd[:, c:c + 1],
                                                 ALU.subtract, ALU.mult)
                    link(last)
                    link(dve.tensor_tensor(moe[:, :, :], moe[:, :, :], row(lg), ALU.mult))
                    link(dve.tensor_tensor(moe[:, :, :], moe[:, :, :], row(lb), ALU.add))
                    dve.wait_ge(sem("stored"), 16 * u)
                    dve.tensor_tensor(xo[:, :, :], moe[:, :, :], xt[:, odd, :, :], ALU.add).then_inc(sem(f"x_used{odd}"), 1)
                    assert links[0] == DVE_LINKS, links


def build(nc, a, out):
    def scratch(name, shape):
        return nc.dram_tensor(name, shape, F32).ap()
    tokens = NSEQ * SEQ
    x1, x2, x3, y1 = (scratch(n, (tokens, D)) for n in ("x1", "x2", "x3", "y1"))
    h_t = scratch("h_t", (NSTEP + LEAD, D, 2, CHT))
    gates = scratch("gates", (NSTEP + LEAD, P, GATES))
    a_blocks = scratch("a_blocks", (NBLK, DH, SB, SB))
    t_blocks = scratch("t_blocks", (NBLK, DH, 2, SB, SB))
    route = scratch("route", (tokens, 2 * NE))
    linear_attention_phase(nc, a["x"], x1, a["l0_wq_t"], a["l0_wk_t"], a["l0_wv_t"], a["l0_wo_t"], a["l0_norm_w"])
    expert_phase(nc, x1, x2, a["gate_t"], a["gate_bias"], a["wg_t"], a["wu_t"], a["wd_t"], a["wsg_t"], a["wsu_t"],
                 a["wsd_t"])
    gate_phase(nc, x2, h_t, gates, a["w_ba"], a["dt_bias"], a["a_log"])
    delta_phase(nc, x2, x3, h_t, gates, a_blocks, t_blocks, a["w_in"], a["conv_t"], a["l1_norm_w"], a["w_o"])
    attention_phase(nc, x3, y1, route, a["in_t"], a["in_b"], a["in_b_cols"], a["out_t"], a["out_b"], a["ln1_g"],
                    a["ln1_b"], a["wg"])
    linear_expert_phase(nc, x3, y1, route, out, a["w1_rows"], a["b1_t"], a["w2_rows"], a["b2"], a["ln2_g"], a["ln2_b"])


def kernel(**inputs):
    import numpy as np
    import concourse.bacc as bacc
    from concourse.bass_utils import run_bass_kernel_spmd

    i = {k: np.asarray(v) for k, v in inputs.items()}
    arrays = {
        "x": i["L0_attn_hidden_states"].reshape(NSEQ * SEQ, D),
        "l0_wq_t": i["L0_attn_Wq"].T, "l0_wk_t": i["L0_attn_Wk"].T, "l0_wv_t": i["L0_attn_Wv"].T,
        "l0_wo_t": i["L0_attn_Wo"].T, "l0_norm_w": i["L0_attn_norm_w"],
        "gate_t": i["L0_ffn_gate_w"].T, "gate_bias": i["L0_ffn_gate_bias"],
        "wg_t": i["L0_ffn_Wg"].reshape(-1, D).T, "wu_t": i["L0_ffn_Wu"].reshape(-1, D).T,
        "wd_t": i["L0_ffn_Wd"].transpose(0, 2, 1).reshape(-1, D),
        "wsg_t": i["L0_ffn_Ws_g"].T, "wsu_t": i["L0_ffn_Ws_u"].T, "wsd_t": i["L0_ffn_Ws_d"].T,
        "w_in": i["L1_attn_W_in"], "w_ba": i["L1_attn_W_ba"], "conv_t": i["L1_attn_conv_w"].reshape(-1, TAPS).T,
        "dt_bias": i["L1_attn_dt_bias"], "a_log": i["L1_attn_A_log"], "l1_norm_w": i["L1_attn_norm_w"],
        "w_o": i["L1_attn_W_o"],
        "in_t": i["L1_ffn_in_proj_w"].T, "in_b": i["L1_ffn_in_proj_b"],
        "in_b_cols": i["L1_ffn_in_proj_b"].reshape(3, D).T, "out_t": i["L1_ffn_out_proj_w"].T,
        "out_b": i["L1_ffn_out_proj_b"], "ln1_g": i["L1_ffn_ln1_g"], "ln1_b": i["L1_ffn_ln1_b"],
        "ln2_g": i["L1_ffn_ln2_g"], "ln2_b": i["L1_ffn_ln2_b"], "wg": i["L1_ffn_wg"],
        "w1_rows": i["L1_ffn_w1"].reshape(NE, D, FF // P, P).transpose(3, 0, 2, 1).reshape(P, -1),
        "w2_rows": i["L1_ffn_w2"].reshape(NE, FF // P, P, D).transpose(2, 0, 1, 3).reshape(P, -1),
        "b1_t": i["L1_ffn_b1"].reshape(NE, FF // P, P).transpose(2, 0, 1).reshape(P, NE * FF // P),
        "b2": i["L1_ffn_b2"],
    }
    arrays = {f"in_{k}": np.ascontiguousarray(v) for k, v in arrays.items()}
    nc = bacc.Bacc("TRN2", target_bir_lowering=False, num_devices=1)
    aps = {k[3:]: nc.dram_tensor(k, v.shape, F32, kind="ExternalInput").ap() for k, v in arrays.items()}
    out = nc.dram_tensor("out", (NSEQ * SEQ, D), F32, kind="ExternalOutput").ap()
    build(nc, aps, out)
    r = run_bass_kernel_spmd(nc, [arrays], core_ids=[0])
    return r.results[0]["out"].reshape(NSEQ, SEQ, D)
```
